# Optimizing a Trainium2 kernel written in Bass

```python
import numpy as np
import jax
import jax.numpy as jnp

def _softmax(x, axis=-1):
    return jax.nn.softmax(x, axis=axis)

def _gelu(x):
    return jax.nn.gelu(x, approximate=True)

def _silu(x):
    return jax.nn.silu(x)

def _sigmoid(x):
    return jax.nn.sigmoid(x)

def _layernorm(x, axis=-1, eps=1e-05):
    m = jnp.mean(x, axis=axis, keepdims=True)
    v = jnp.var(x, axis=axis, keepdims=True)
    return (x - m) / jnp.sqrt(v + eps)

def _scatter_add(tgt, idx, src, axis=0):
    return tgt.at[idx].add(src)

def _segment_sum(src, seg, n):
    return jax.ops.segment_sum(src, seg, n)
kernel_name = 'mk_sandwich_d1_jaxref_r8_59b23c'

def setup_inputs(seed: int=0):
    np.random.seed(seed)
    _w = jnp.asarray

    def _L0_attn_setup():
        import jax, jax.numpy as jnp
        import numpy as np
        HID = 128
        NH = 16
        HD = HID // NH
        RANK = 16
        B, L = (2, 256)
        key = jax.random.key(seed)
        ks = jax.random.split(key, 9)
        s = 0.02
        return {'x': jax.random.normal(ks[0], (B, L, HID), dtype=jnp.float32), 'Wq': jax.random.normal(ks[1], (HID, HID), dtype=jnp.float32) * s, 'Wk': jax.random.normal(ks[2], (HID, HID), dtype=jnp.float32) * s, 'Wv': jax.random.normal(ks[3], (HID, HID), dtype=jnp.float32) * s, 'Wg': jax.random.normal(ks[4], (HID, HID), dtype=jnp.float32) * s, 'Wgk1': jax.random.normal(ks[5], (HID, RANK), dtype=jnp.float32) * s, 'Wgk2': jax.random.normal(ks[6], (RANK, HID), dtype=jnp.float32) * s, 'bgk2': jnp.zeros((HID,), dtype=jnp.float32), 'gamma': jnp.ones((HID,), dtype=jnp.float32), 'beta': jnp.zeros((HID,), dtype=jnp.float32), 'Wout': jax.random.normal(ks[7], (HID, HID), dtype=jnp.float32) * s}
    _L0_attn_in = _L0_attn_setup()

    def _L0_ffn_setup():
        import jax, jax.numpy as jnp
        import numpy as np
        DIM = 128
        DEPTH = 6
        HEADS = 16
        DIM_HEAD = 64
        WINDOW = 32
        INNER = HEADS * DIM_HEAD
        DIM_INNER = int(DIM * 4 * 2 / 3)
        QK_SCALE = 8.0

        def shift_tokens(t):
            a, s = jnp.split(t, 2, -1)
            s = jnp.pad(s, ((0, 0), (1, 0), (0, 0)))[:, :-1]
            return jnp.concatenate([a, s], -1)

        def l2norm(t):
            return t / jnp.maximum(jnp.linalg.norm(t, axis=-1, keepdims=True), 1e-12)

        def rotate_half(x):
            x1, x2 = jnp.split(x, 2, -1)
            return jnp.concatenate([-x2, x1], -1)

        def rotary_tables(n):
            half = jnp.arange(0, DIM_HEAD, 2, dtype=jnp.float32)
            inv_freq = 1.0 / 10000.0 ** (half / DIM_HEAD)
            t = jnp.arange(n, dtype=jnp.float32)
            freqs = t[:, None] * inv_freq[None, :]
            freqs = jnp.concatenate([freqs, freqs], -1)
            base_scale = (half + 0.4 * DIM_HEAD) / (1.4 * DIM_HEAD)
            power = (t - n // 2) / (WINDOW // 2)
            scale = base_scale[None, :] ** power[:, None]
            scale = jnp.concatenate([scale, scale], -1)
            return (freqs, scale)

        def local_attention(q, k, v):
            b, h, n, d = q.shape
            w = WINDOW
            nw = n // w
            bq = q.reshape(b, h, nw, w, d)
            bk = k.reshape(b, h, nw, w, d)
            bv = v.reshape(b, h, nw, w, d)

            def look(t):
                p = jnp.pad(t, ((0, 0), (0, 0), (1, 0), (0, 0), (0, 0)))
                return jnp.concatenate([p[:, :, :nw], p[:, :, 1:]], axis=3)
            bk2, bv2 = (look(bk), look(bv))
            seq = jnp.arange(n).reshape(nw, w)
            seq_p = jnp.pad(seq, ((1, 0), (0, 0)), constant_values=-1)
            jt = jnp.concatenate([seq_p[:nw], seq_p[1:]], axis=1)
            it = seq[:, :, None]
            jb = jt[:, None, :]
            mask = (it < jb) | (it > jb + w) | (jb == -1)
            sim = jnp.einsum('bhwie,bhwje->bhwij', bq, bk2) * QK_SCALE
            sim = jnp.where(mask, -jnp.finfo(sim.dtype).max, sim)
            attn = jax.nn.softmax(sim, -1)
            out = jnp.einsum('bhwij,bhwje->bhwie', attn, bv2)
            return out.reshape(b, h, n, d)

        def attn_layer(x, Wqkv, qs, ksc, Wo):
            b, n, _ = x.shape
            qkv = x @ Wqkv
            q, k, v = jnp.split(qkv, 3, -1)
            sh = lambda t: t.reshape(b, n, HEADS, DIM_HEAD).transpose(0, 2, 1, 3)
            q, k, v = (sh(q), sh(k), sh(v))
            q = l2norm(q) * qs
            k = l2norm(k) * ksc
            freqs, scale = rotary_tables(n)
            cos, sin = (jnp.cos(freqs), jnp.sin(freqs))
            q = q * cos * scale + rotate_half(q) * sin * scale
            inv = 1.0 / scale
            k = k * cos * inv + rotate_half(k) * sin * inv
            out = local_attention(q, k, v)
            out = out.transpose(0, 2, 1, 3).reshape(b, n, INNER)
            return out @ Wo

        def ffn_layer(x, g, bln, W1, b1, W2, b2):
            mu = x.mean(-1, keepdims=True)
            var = ((x - mu) ** 2).mean(-1, keepdims=True)
            xn = (x - mu) / jnp.sqrt(var + 1e-05) * g + bln
            hg = xn @ W1 + b1
            a, gate = jnp.split(hg, 2, -1)
            return a * jax.nn.gelu(gate, approximate=False) @ W2 + b2
        key = jax.random.key(seed)
        ks = jax.random.split(key, 8)
        B, N = (2, 256)
        init = lambda k, shape: jax.random.normal(k, shape, jnp.float32) * 0.02
        return {'x': jax.random.normal(ks[0], (B, N, DIM), jnp.float32), 'Wqkv': init(ks[1], (DEPTH, DIM, 3 * INNER)), 'q_scale': jnp.ones((DEPTH, DIM_HEAD), jnp.float32), 'k_scale': jnp.ones((DEPTH, DIM_HEAD), jnp.float32), 'Wo': init(ks[2], (DEPTH, INNER, DIM)), 'ln_g': jnp.ones((DEPTH, DIM), jnp.float32), 'ln_b': jnp.zeros((DEPTH, DIM), jnp.float32), 'W1': init(ks[3], (DEPTH, DIM, 2 * DIM_INNER)), 'b1': jnp.zeros((DEPTH, 2 * DIM_INNER), jnp.float32), 'W2': init(ks[4], (DEPTH, DIM_INNER, DIM)), 'b2': jnp.zeros((DEPTH, DIM), jnp.float32)}
    _L0_ffn_in = _L0_ffn_setup()
    _d = {'L0_attn_x': _L0_attn_in['x'], 'L0_attn_Wq': _L0_attn_in['Wq'], 'L0_attn_Wk': _L0_attn_in['Wk'], 'L0_attn_Wv': _L0_attn_in['Wv'], 'L0_attn_Wg': _L0_attn_in['Wg'], 'L0_attn_Wgk1': _L0_attn_in['Wgk1'], 'L0_attn_Wgk2': _L0_attn_in['Wgk2'], 'L0_attn_bgk2': _L0_attn_in['bgk2'], 'L0_attn_gamma': _L0_attn_in['gamma'], 'L0_attn_beta': _L0_attn_in['beta'], 'L0_attn_Wout': _L0_attn_in['Wout'], 'L0_ffn_Wqkv': _L0_ffn_in['Wqkv'], 'L0_ffn_q_scale': _L0_ffn_in['q_scale'], 'L0_ffn_k_scale': _L0_ffn_in['k_scale'], 'L0_ffn_Wo': _L0_ffn_in['Wo'], 'L0_ffn_ln_g': _L0_ffn_in['ln_g'], 'L0_ffn_ln_b': _L0_ffn_in['ln_b'], 'L0_ffn_W1': _L0_ffn_in['W1'], 'L0_ffn_b1': _L0_ffn_in['b1'], 'L0_ffn_W2': _L0_ffn_in['W2'], 'L0_ffn_b2': _L0_ffn_in['b2']}
    _x0 = _d['L0_attn_x']
    _d['L0_attn_x'] = jax.random.normal(jax.random.fold_in(jax.random.key(seed), 1), (2, 1024, 128), dtype=_x0.dtype)
    del _x0
    return _d

def reference(L0_attn_x, L0_attn_Wq, L0_attn_Wk, L0_attn_Wv, L0_attn_Wg, L0_attn_Wgk1, L0_attn_Wgk2, L0_attn_bgk2, L0_attn_gamma, L0_attn_beta, L0_attn_Wout, L0_ffn_Wqkv, L0_ffn_q_scale, L0_ffn_k_scale, L0_ffn_Wo, L0_ffn_ln_g, L0_ffn_ln_b, L0_ffn_W1, L0_ffn_b1, L0_ffn_W2, L0_ffn_b2):

    def _L0_attn_ref(x, Wq, Wk, Wv, Wg, Wgk1, Wgk2, bgk2, gamma, beta, Wout):
        import jax, jax.numpy as jnp
        import numpy as np
        HID = 128
        NH = 16
        HD = HID // NH
        RANK = 16
        B, L = (2, 256)
        Bb, Ll, Hid = x.shape
        H, Dh = (NH, HD)
        q = (x @ Wq).reshape(Bb, Ll, H, Dh)
        k = (x @ Wk).reshape(Bb, Ll, H, Dh)
        v = (x @ Wv).reshape(Bb, Ll, H, Dh)
        gk = (jax.nn.log_sigmoid(x @ Wgk1 @ Wgk2 + bgk2) / 16.0).reshape(Bb, Ll, H, Dh)
        qT = jnp.transpose(q, (1, 0, 2, 3))
        kT = jnp.transpose(k, (1, 0, 2, 3))
        vT = jnp.transpose(v, (1, 0, 2, 3))
        gT = jnp.transpose(gk, (1, 0, 2, 3))

        def step(state, inp):
            qt, kt, vt, gt = inp
            gate = jnp.exp(gt)
            state = state * gate[..., None] + vt[..., None] * kt[..., None, :]
            out_t = jnp.einsum('bhvk,bhk->bhv', state, qt)
            return (state, out_t)
        state0 = jnp.zeros((Bb, H, Dh, Dh), dtype=x.dtype)
        _, outs = jax.lax.scan(step, state0, (qT, kT, vT, gT))
        out = jnp.transpose(outs, (1, 0, 2, 3)).reshape(Bb, Ll, Hid)
        mu = out.mean(-1, keepdims=True)
        var = out.var(-1, keepdims=True)
        out = (out - mu) / jnp.sqrt(var + 1e-05) * gamma + beta
        out = out * jax.nn.silu(x @ Wg)
        return out @ Wout

    def _L0_ffn_ref(x, Wqkv, q_scale, k_scale, Wo, ln_g, ln_b, W1, b1, W2, b2):
        import jax, jax.numpy as jnp
        import numpy as np
        DIM = 128
        DEPTH = 6
        HEADS = 16
        DIM_HEAD = 64
        WINDOW = 32
        INNER = HEADS * DIM_HEAD
        DIM_INNER = int(DIM * 4 * 2 / 3)
        QK_SCALE = 8.0

        def shift_tokens(t):
            a, s = jnp.split(t, 2, -1)
            s = jnp.pad(s, ((0, 0), (1, 0), (0, 0)))[:, :-1]
            return jnp.concatenate([a, s], -1)

        def l2norm(t):
            return t / jnp.maximum(jnp.linalg.norm(t, axis=-1, keepdims=True), 1e-12)

        def rotate_half(x):
            x1, x2 = jnp.split(x, 2, -1)
            return jnp.concatenate([-x2, x1], -1)

        def rotary_tables(n):
            half = jnp.arange(0, DIM_HEAD, 2, dtype=jnp.float32)
            inv_freq = 1.0 / 10000.0 ** (half / DIM_HEAD)
            t = jnp.arange(n, dtype=jnp.float32)
            freqs = t[:, None] * inv_freq[None, :]
            freqs = jnp.concatenate([freqs, freqs], -1)
            base_scale = (half + 0.4 * DIM_HEAD) / (1.4 * DIM_HEAD)
            power = (t - n // 2) / (WINDOW // 2)
            scale = base_scale[None, :] ** power[:, None]
            scale = jnp.concatenate([scale, scale], -1)
            return (freqs, scale)

        def local_attention(q, k, v):
            b, h, n, d = q.shape
            w = WINDOW
            nw = n // w
            bq = q.reshape(b, h, nw, w, d)
            bk = k.reshape(b, h, nw, w, d)
            bv = v.reshape(b, h, nw, w, d)

            def look(t):
                p = jnp.pad(t, ((0, 0), (0, 0), (1, 0), (0, 0), (0, 0)))
                return jnp.concatenate([p[:, :, :nw], p[:, :, 1:]], axis=3)
            bk2, bv2 = (look(bk), look(bv))
            seq = jnp.arange(n).reshape(nw, w)
            seq_p = jnp.pad(seq, ((1, 0), (0, 0)), constant_values=-1)
            jt = jnp.concatenate([seq_p[:nw], seq_p[1:]], axis=1)
            it = seq[:, :, None]
            jb = jt[:, None, :]
            mask = (it < jb) | (it > jb + w) | (jb == -1)
            sim = jnp.einsum('bhwie,bhwje->bhwij', bq, bk2) * QK_SCALE
            sim = jnp.where(mask, -jnp.finfo(sim.dtype).max, sim)
            attn = jax.nn.softmax(sim, -1)
            out = jnp.einsum('bhwij,bhwje->bhwie', attn, bv2)
            return out.reshape(b, h, n, d)

        def attn_layer(x, Wqkv, qs, ksc, Wo):
            b, n, _ = x.shape
            qkv = x @ Wqkv
            q, k, v = jnp.split(qkv, 3, -1)
            sh = lambda t: t.reshape(b, n, HEADS, DIM_HEAD).transpose(0, 2, 1, 3)
            q, k, v = (sh(q), sh(k), sh(v))
            q = l2norm(q) * qs
            k = l2norm(k) * ksc
            freqs, scale = rotary_tables(n)
            cos, sin = (jnp.cos(freqs), jnp.sin(freqs))
            q = q * cos * scale + rotate_half(q) * sin * scale
            inv = 1.0 / scale
            k = k * cos * inv + rotate_half(k) * sin * inv
            out = local_attention(q, k, v)
            out = out.transpose(0, 2, 1, 3).reshape(b, n, INNER)
            return out @ Wo

        def ffn_layer(x, g, bln, W1, b1, W2, b2):
            mu = x.mean(-1, keepdims=True)
            var = ((x - mu) ** 2).mean(-1, keepdims=True)
            xn = (x - mu) / jnp.sqrt(var + 1e-05) * g + bln
            hg = xn @ W1 + b1
            a, gate = jnp.split(hg, 2, -1)
            return a * jax.nn.gelu(gate, approximate=False) @ W2 + b2
        for i in range(DEPTH):
            x = attn_layer(shift_tokens(x), Wqkv[i], q_scale[i], k_scale[i], Wo[i]) + x
            x = ffn_layer(shift_tokens(x), ln_g[i], ln_b[i], W1[i], b1[i], W2[i], b2[i]) + x
        return x
    x = L0_attn_x
    x = x + _layernorm(_L0_attn_ref(_layernorm(x, axis=-1), L0_attn_Wq, L0_attn_Wk, L0_attn_Wv, L0_attn_Wg, L0_attn_Wgk1, L0_attn_Wgk2, L0_attn_bgk2, L0_attn_gamma, L0_attn_beta, L0_attn_Wout), axis=-1)
    x = x + _layernorm(_L0_ffn_ref(_layernorm(x, axis=-1), L0_ffn_Wqkv, L0_ffn_q_scale, L0_ffn_k_scale, L0_ffn_Wo, L0_ffn_ln_g, L0_ffn_ln_b, L0_ffn_W1, L0_ffn_b1, L0_ffn_W2, L0_ffn_b2), axis=-1)
    return x

_drawn_inputs = setup_inputs


def setup_inputs(seed=0):
    import zlib

    import numpy as np

    out = dict(_drawn_inputs(seed))
    spreads = {'L0_attn_bgk2': (0.0, 0.1),
     'L0_attn_gamma': (1.0, 0.2),
     'L0_attn_beta': (0.0, 0.1),
     'L0_ffn_q_scale': (1.0, 0.6),
     'L0_ffn_k_scale': (1.0, 0.6),
     'L0_ffn_ln_g': (1.0, 0.6),
     'L0_ffn_ln_b': (0.0, 0.8),
     'L0_ffn_b1': (0.0, 0.8),
     'L0_ffn_b2': (0.0, 0.326)}
    factors = {'L0_attn_Wgk1': 8.0, 'L0_attn_Wgk2': 8.0, 'L0_ffn_W1': 4.489, 'L0_ffn_W2': 4.419}
    for name, (base, spread) in spreads.items():
        noise = np.random.default_rng([zlib.crc32(name.encode()), seed]).standard_normal(out[name].shape)
        drawn = base * np.exp(spread * noise) if base else spread * noise
        out[name] = jnp.asarray(drawn.astype(out[name].dtype))
    for name, factor in factors.items():
        out[name] = (out[name] * factor).astype(out[name].dtype)
    return out
```

```python
from contextlib import ExitStack

import concourse.bass as bass
from concourse import mybir

F32 = mybir.dt.float32
BF16 = mybir.dt.bfloat16
I32 = mybir.dt.int32
ALU = mybir.AluOpType
ACT = mybir.ActivationFunctionType
AX_X = mybir.AxisListType.X

P = 128
DIM = 128
BATCH = 2
LENGTH = 1024
POS = LENGTH // P
ROWS = BATCH * POS
GLA_HEADS = 16
GLA_DH = 8
RANK = 16
DEPTH = 6
HEADS = 16
DH = 64
PAIRS = HEADS // 2
INNER = HEADS * DH
HALF = DH // 2
WIN = 32
KEYS = 2 * WIN
HIDDEN = int(DIM * 4 * 2 / 3)
CHUNKS = [(c * P, min(P, HIDDEN - c * P)) for c in range((HIDDEN + P - 1) // P)]
NCH = len(CHUNKS)
QK_SCALE = 8.0
EPS = 1e-5
MASKED = -1e30
TILES = ROWS * DEPTH
BANK = 512
FRAME = 3 * WIN
RSQRT_SEED = 0x5F3759DF


def wait(eng, sem, value):
    if not (isinstance(value, int) and value <= 0):
        eng.wait_ge(sem, value)


class Tile:

    def __init__(self, pair, seq):
        self.pair, self.seq = pair, seq

    def lag(self, n):
        d = self.seq - n
        return Tile(self.pair + d // 2, d % 2)

    @property
    def index(self):
        return self.pair * 2 + self.seq

    @property
    def pos(self):
        return self.pair % POS

    @property
    def layer(self):
        return self.pair // POS

    @property
    def live(self):
        return not isinstance(self.pair, int) or 0 <= self.index < TILES


def at(ap, index, size=1):
    return bass.ds(index * size, size)


def build(nc, x, Wq_rep, Wk_rep, Wv, Wg, Wgk1, Wgk2, bgk2, gamma, beta, Wout,
          Wqkv, q_scale, k_scale, Wo, ln_g, ln_b, W1, b1, W2, b2, rope, mask, first, out):
    ctx = ExitStack()
    with ctx:
        def sem(name, stack=ctx):
            return stack.enter_context(nc.semaphore(name))

        def sb(name, shape, dt=F32, stack=ctx):
            return stack.enter_context(nc.sbuf_tensor(name, shape, dt))

        X = sb("X", [P, BATCH, POS, DIM])
        X1 = sb("X1", [P, BATCH, POS, DIM])
        ident = sb("ident", [P, P])
        minus_half = sb("minus_half", [P, ROWS])
        eps = sb("eps", [P, ROWS])
        PS = ctx.enter_context(nc.psum_tensor("PS", [P, 8 * BANK], F32))

        def bank(j, n=1):
            return PS[:, j * BANK:(j + n) * BANK]

        x_ready = sem("x_ready")
        const_ready = sem("const_ready")
        with ExitStack() as one:
            phase_one(nc, one, sem, sb, bank, locals())
        with ExitStack() as two:
            phase_two(nc, two, sem, sb, bank, locals())
        with ExitStack() as three:
            phase_three(nc, three, sem, sb, locals())


def phase_one(nc, stack, new_sem, new_sb, bank, env):
    X, X1, ident, minus_half, eps = (env[k] for k in ("X", "X1", "ident", "minus_half", "eps"))
    x_ready, const_ready = env["x_ready"], env["const_ready"]

    def sem(name):
        return new_sem(name, stack)

    def sb(name, shape, dt=F32):
        return new_sb(name, shape, dt, stack)

    T = BATCH * LENGTH
    NB = T // BANK
    wk = sb("wk", [P, GLA_DH, P])
    wq = sb("wq", [P, GLA_DH, P])
    wv = sb("wv", [P, P])
    wg = sb("wg", [P, P])
    wgk1 = sb("wgk1", [P, RANK])
    wgk2 = sb("wgk2", [RANK, P])
    wout = sb("wout", [P, P])
    bgk = sb("bgk", [P, 1])
    gam = sb("gam", [P, DIM])
    bet = sb("bet", [P, DIM])
    xn = sb("xn", [P, ROWS, DIM])
    xnT = sb("xnT", [P, T])
    vT = sb("vT", [P, T])
    low = sb("low", [RANK, T])
    gate = sb("gate", [P, T])
    za = sb("za", [P, T])
    zb = sb("zb", [P, T])
    kv = sb("kv", [P, 2, LENGTH])
    st = sb("st", [P, 2, LENGTH])
    sq = sb("sqg", [P, 2, LENGTH])
    oT = sb("oT", [P, T])
    stats = sb("stats1", [P, ROWS, 6])
    mv = sb("mv1", [P, ROWS, 2])
    rstd = sb("rstd1", [P, ROWS])

    loaded = sem("p1_loaded")
    pool_self = sem("p1_pool_self")
    moments = sem("p1_moments")
    rstd_ready = sem("p1_rstd")
    dve_self = sem("p1_dve_self")
    normed = sem("p1_normed")
    turned = sem("p1_turned")
    turned_out = sem("p1_turned_out")
    proj = sem("p1_proj")
    proj_out = sem("p1_proj_out")
    z_ready = sem("p1_z")
    act_self = sem("p1_act_self")
    soft = sem("p1_soft")
    arg_ready = sem("p1_arg")
    gate_ready = sem("p1_gate")
    krep_done = sem("p1_krep")
    krep_used = sem("p1_krep_used")
    qrep_done = sem("p1_qrep")
    read_done = sem("p1_read")
    summed = sem("p1_summed")
    gmul_done = sem("p1_gmul")
    silu_done = sem("p1_silu")
    o_used = sem("p1_o_used")
    mixed = sem("p1_mixed")
    y_done = sem("p1_y")
    y_used = sem("p1_y_used")
    x1_ready = sem("p1_x1")

    LOOPS = [(b, kk) for kk in range(GLA_DH) for b in range(BATCH)]
    x1f = X1[:, :, :, :].rearrange("p b n d -> p (b n) d")
    xf = X[:, :, :, :].rearrange("p b n d -> p (b n) d")
    with nc.Block() as block:

        @block.sync
        def _(sp):
            sp.dma_start(X1[:, :, :, :], env["x"].rearrange("b (n t) d -> t b n d", t=P)).then_inc(loaded, 16)
            for dst, src in ((wv[:, :], env["Wv"]), (wk[:, :, :], env["Wk_rep"]), (wq[:, :, :], env["Wq_rep"]),
                             (wgk1[:, :], env["Wgk1"]), (wgk2[:, :], env["Wgk2"]),
                             (bgk[:, :], env["bgk2"].rearrange("(p o) -> p o", o=1)),
                             (wg[:, :], env["Wg"]), (wout[:, :], env["Wout"]),
                             (gam[:, :], env["gamma"].rearrange("(o d) -> o d", o=1).to_broadcast([P, DIM])),
                             (bet[:, :], env["beta"].rearrange("(o d) -> o d", o=1).to_broadcast([P, DIM]))):
                sp.dma_start(dst, src).then_inc(loaded, 16)

        ALL_LOADED = 16 * 11

        @block.gpsimd
        def _(pool):
            nc.gpsimd.memset(ident[:, :], 0.0).then_inc(pool_self, 1)
            nc.gpsimd.memset(minus_half[:, :], -0.5).then_inc(const_ready, 1)
            nc.gpsimd.memset(eps[:, :], EPS).then_inc(const_ready, 1)
            pool.wait_ge(pool_self, 1)
            nc.gpsimd.affine_select(out=ident[:, :], in_=ident[:, :], compare_op=ALU.not_equal, fill=1.0,
                                    base=0, pattern=[[-1, P]], channel_multiplier=1).then_inc(const_ready, 1)
            pool.wait_ge(const_ready, 3)
            steps = [1]

            def inverse_deviation(k):
                pool.wait_ge(moments, k + 1)
                nc.gpsimd.tensor_tensor(rstd[:, :], mv[:, :, 1], eps[:, :], ALU.add).then_inc(pool_self, 1)
                steps[0] += 1
                pool.wait_ge(pool_self, steps[0])
                nc.gpsimd.tensor_tensor(rstd[:, :], rstd[:, :], minus_half[:, :], ALU.pow).then_inc(rstd_ready, 1)

            inverse_deviation(0)
            for i, (b, kk) in enumerate(LOOPS):
                pool.wait_ge(read_done, i + 1)
                dst = oT[:, b * LENGTH:(b + 1) * LENGTH]
                if kk == 0:
                    nc.gpsimd.tensor_copy(dst, sq[:, i % 2, :]).then_inc(summed, 1)
                else:
                    pool.wait_ge(summed, i - 1)
                    nc.gpsimd.tensor_tensor(dst, dst, sq[:, i % 2, :], ALU.add).then_inc(summed, 1)
            for k in (1, 2, 3):
                inverse_deviation(k)

        @block.tensor
        def _(pe):
            def turn(src, tiles_ready, use, base):
                for j in range(NB):
                    for i in range(4):
                        pe.wait_ge(tiles_ready, base + 4 * j + i + 1)
                        last = nc.tensor.transpose(bank(j)[:, i * P:(i + 1) * P], src(4 * j + i), ident[:, :])
                    last.then_inc(turned, 1)

            pe.wait_ge(const_ready, 3)
            turn(lambda i: xn[:, i, :], normed, None, 0)
            pe.wait_ge(loaded, ALL_LOADED)
            for j in range(NB):
                pe.wait_ge(turned_out, j + 1)
                nc.tensor.matmul(bank(4 + j), wv[:, :], xnT[:, j * BANK:(j + 1) * BANK],
                                 start=True, stop=True).then_inc(proj, 1)
            for j in range(NB):
                nc.tensor.matmul(bank(j)[0:RANK, :], wgk1[:, :], xnT[:, j * BANK:(j + 1) * BANK],
                                 start=True, stop=True).then_inc(proj, 1)
            for j in range(NB):
                pe.wait_ge(proj_out, 5 + j)
                nc.tensor.matmul(bank(4 + j), wgk2[:, :], low[:, j * BANK:(j + 1) * BANK],
                                 start=True, stop=True).then_inc(proj, 1)
            for i, (b, kk) in enumerate(LOOPS):
                base = 4 * (i % 2)
                if i == 1:
                    pe.wait_ge(z_ready, NB)
                if i >= 2:
                    pe.wait_ge(krep_used, i - 1)
                for j in range(2):
                    last = nc.tensor.matmul(bank(base + j), wk[:, kk, :],
                                            xnT[:, b * LENGTH + j * BANK:b * LENGTH + (j + 1) * BANK],
                                            start=True, stop=True)
                last.then_inc(krep_done, 1)
                if i >= 2:
                    pe.wait_ge(read_done, i - 1)
                for j in range(2):
                    last = nc.tensor.matmul(bank(base + 2 + j), wq[:, kk, :],
                                            xnT[:, b * LENGTH + j * BANK:b * LENGTH + (j + 1) * BANK],
                                            start=True, stop=True)
                last.then_inc(qrep_done, 1)
            pe.wait_ge(read_done, len(LOOPS))
            for j in range(NB):
                for i in range(4):
                    t = 4 * j + i
                    last = nc.tensor.matmul(bank(4 + j)[:, i * P:(i + 1) * P], xnT[:, t * P:(t + 1) * P],
                                            wg[:, :], start=True, stop=True)
                last.then_inc(gmul_done, 1)
            pe.wait_ge(summed, len(LOOPS))
            for j in range(NB):
                for i in range(4):
                    t = 4 * j + i
                    last = nc.tensor.transpose(bank(j)[:, i * P:(i + 1) * P], oT[:, t * P:(t + 1) * P], ident[:, :])
                last.then_inc(turned, 1)
            pe.wait_ge(o_used, ROWS)
            for j in range(NB):
                for i in range(4):
                    t = 4 * j + i
                    pe.wait_ge(mixed, t + 1)
                    last = nc.tensor.transpose(bank(j)[:, i * P:(i + 1) * P], xn[:, t, :], ident[:, :])
                last.then_inc(turned, 1)
            pe.wait_ge(silu_done, NB)
            for j in range(NB):
                pe.wait_ge(turned_out, NB + j + 1)
                for i in range(4):
                    t = 4 * j + i
                    last = nc.tensor.matmul(bank(4 + j)[:, i * P:(i + 1) * P], xnT[:, t * P:(t + 1) * P],
                                            wout[:, :], start=True, stop=True)
                last.then_inc(y_done, 1)

        @block.scalar
        def _(act):
            for j in range(NB):
                act.wait_ge(turned, j + 1)
                nc.scalar.activation(xnT[:, j * BANK:(j + 1) * BANK], bank(j), ACT.Copy).then_inc(turned_out, 1)
            for j in range(NB):
                act.wait_ge(proj, j + 1)
                nc.scalar.activation(vT[:, j * BANK:(j + 1) * BANK], bank(4 + j), ACT.Copy).then_inc(proj_out, 1)
            for j in range(NB):
                act.wait_ge(proj, NB + j + 1)
                nc.scalar.activation(low[:, j * BANK:(j + 1) * BANK], bank(j)[0:RANK, :],
                                     ACT.Copy).then_inc(proj_out, 1)
            for j in range(NB):
                s = slice(j * BANK, (j + 1) * BANK)
                act.wait_ge(z_ready, j + 1)
                nc.scalar.activation(zb[:, s], za[:, s], ACT.Abs).then_inc(act_self, 1)
            for j in range(NB):
                s = slice(j * BANK, (j + 1) * BANK)
                act.wait_ge(act_self, j + 1)
                nc.scalar.activation(zb[:, s], zb[:, s], ACT.Exp, scale=-1.0).then_inc(act_self, 1)
            for j in range(NB):
                s = slice(j * BANK, (j + 1) * BANK)
                act.wait_ge(act_self, NB + j + 1)
                nc.scalar.activation(zb[:, s], zb[:, s], ACT.Ln, bias=1.0).then_inc(soft, 1)
            for j in range(NB):
                s = slice(j * BANK, (j + 1) * BANK)
                act.wait_ge(arg_ready, j + 1)
                nc.scalar.activation(gate[:, s], zb[:, s], ACT.Exp, scale=1.0 / 16.0).then_inc(gate_ready, 1)
            for j in range(NB):
                act.wait_ge(gmul_done, j + 1)
                nc.scalar.activation(za[:, j * BANK:(j + 1) * BANK], bank(4 + j), ACT.Silu).then_inc(silu_done, 1)
            for j in range(NB):
                act.wait_ge(turned, 2 * NB + j + 1)
                nc.scalar.activation(xnT[:, j * BANK:(j + 1) * BANK], bank(j), ACT.Copy).then_inc(turned_out, 1)

        @block.vector
        def _(dve):
            links = [0]

            def link(ins):
                links[0] += 1
                ins.then_inc(dve_self, 1)
                dve.wait_ge(dve_self, links[0])

            def take_moments(k, src, ready=None):
                for t in range(ROWS):
                    if ready is not None and t % 4 == 0:
                        dve.wait_ge(*ready(t))
                    last = nc.vector.bn_stats(stats[:, t, :], src(t))
                link(last)
                for t in range(ROWS):
                    last = nc.vector.bn_aggr(mv[:, t, :], stats[:, t, :])
                last.then_inc(moments, 1)
                dve.wait_ge(rstd_ready, k + 1)

            def normalise(dst, src, t):
                return nc.vector.tensor_scalar(dst, src, mv[:, t, 0:1], rstd[:, t:t + 1], ALU.subtract, ALU.mult)

            dve.wait_ge(loaded, ALL_LOADED)
            take_moments(0, lambda t: x1f[:, t, :])
            for t in range(ROWS):
                normalise(xn[:, t, :], x1f[:, t, :], t).then_inc(normed, 1)
            for j in range(NB):
                s = slice(j * BANK, (j + 1) * BANK)
                dve.wait_ge(proj, 2 * NB + j + 1)
                nc.vector.tensor_scalar(za[:, s], bank(4 + j), bgk[:, 0:1], None, ALU.add).then_inc(z_ready, 1)
            dve.wait_ge(z_ready, NB)
            for j in range(NB):
                s = slice(j * BANK, (j + 1) * BANK)
                dve.wait_ge(soft, j + 1)
                nc.vector.scalar_tensor_tensor(zb[:, s], za[:, s], 0.0, zb[:, s], ALU.min,
                                               ALU.subtract).then_inc(arg_ready, 1)
            dve.wait_ge(gate_ready, NB)
            for i, (b, kk) in enumerate(LOOPS):
                s = slice(b * LENGTH, (b + 1) * LENGTH)
                base = 4 * (i % 2)
                dve.wait_ge(krep_done, i + 1)
                ins = nc.vector.tensor_tensor(kv[:, i % 2, :], bank(base, 2), vT[:, s], ALU.mult)
                ins.then_inc(krep_used, 1)
                dve.wait_ge(krep_used, i + 1)
                link(nc.vector.tensor_tensor_scan(st[:, i % 2, :], gate[:, s], kv[:, i % 2, :], 0.0,
                                                  ALU.mult, ALU.add))
                dve.wait_ge(qrep_done, i + 1)
                if i >= 2:
                    dve.wait_ge(summed, i - 1)
                nc.vector.tensor_tensor(sq[:, i % 2, :], bank(base + 2, 2), st[:, i % 2, :],
                                        ALU.mult).then_inc(read_done, 1)
            take_moments(1, lambda t: bank(t // 4)[:, (t % 4) * P:(t % 4 + 1) * P],
                         lambda t: (turned, NB + t // 4 + 1))
            for t in range(ROWS):
                normalise(xn[:, t, :], bank(t // 4)[:, (t % 4) * P:(t % 4 + 1) * P], t).then_inc(o_used, 1)
            dve.wait_ge(o_used, ROWS)
            wide = [P, ROWS, DIM]
            link(nc.vector.tensor_tensor(xn[:, :, :], xn[:, :, :], gam[:, :].unsqueeze(1).to_broadcast(wide), ALU.mult))
            link(nc.vector.tensor_tensor(xn[:, :, :], xn[:, :, :], bet[:, :].unsqueeze(1).to_broadcast(wide), ALU.add))
            zv = za[:, :].rearrange("p (t d) -> p t d", d=DIM)
            for t in range(ROWS):
                if t % 4 == 0:
                    dve.wait_ge(silu_done, t // 4 + 1)
                nc.vector.tensor_tensor(xn[:, t, :], xn[:, t, :], zv[:, t, :], ALU.mult).then_inc(mixed, 1)

            def y(t):
                return bank(4 + t // 4)[:, (t % 4) * P:(t % 4 + 1) * P]

            take_moments(2, y, lambda t: (y_done, t // 4 + 1))
            for t in range(ROWS):
                last = normalise(vT[:, t * DIM:(t + 1) * DIM], y(t), t)
            link(last)
            link(nc.vector.tensor_tensor(x1f, x1f, vT[:, :].rearrange("p (t d) -> p t d", d=DIM), ALU.add))
            take_moments(3, lambda t: x1f[:, t, :])
            for t in range(ROWS):
                normalise(xf[:, t, :], x1f[:, t, :], t).then_inc(x_ready, 1)


def phase_two(nc, stack, new_sem, new_sb, bank, env):
    X, ident, minus_half, eps = (env[k] for k in ("X", "ident", "minus_half", "eps"))
    x_ready = env["x_ready"]

    def sem(name):
        return new_sem(name, stack)

    def sb(name, shape, dt=F32):
        return new_sb(name, shape, dt, stack)

    wkq = sb("wkq", [P, 2 * INNER])
    wv = sb("w_v", [P, INNER])
    wo = sb("w_o", [P, PAIRS, DIM])
    w1 = sb("w_1", [P, 2 * HIDDEN])
    w2 = sb("w_2", [P, NCH, DIM])
    scales = sb("scales", [P, DEPTH, 4, DH])
    g_all = sb("g_all", [P, DEPTH])
    b_all = sb("b_all", [P, DEPTH])
    b1_all = sb("b1_all", [P, 2, NCH, DEPTH])
    b2_all = sb("b2_all", [P, DEPTH, DIM])
    ropes = sb("ropes", [P, POS, 4 * DH])
    mask_in = sb("mask_in", [P, POS + 1, KEYS])
    masks = sb("masks", [P, POS + 1, KEYS], BF16)
    first = sb("first", [P, POS])
    ident16 = sb("ident16", [P, P], BF16)
    xcur = sb("xcur", [P, DIM])
    xs = [sb(f"xs{b}", [P, WIN + P + 1]) for b in range(2)]
    turn_tab = [sb(f"turn_tab{b}", [P, 4, DH]) for b in range(2)]
    sqr = sb("sqr", [P, 2 * HEADS, DH])
    kq = sb("kq", [P, 2, HEADS, DH])
    kq_sin = sb("kq_sin", [P, 2, HEADS, DH])
    ss = sb("ss", [P, 2 * HEADS])
    seed = sb("seed", [P, 2 * HEADS], I32)
    inv = sb("inv", [P, 2 * HEADS])
    tmp = sb("tmp", [P, 2 * HEADS])
    kT = [sb(f"kT{b}", [P, PAIRS, WIN + P]) for b in range(2)]
    qbd = sb("qbd", [P, PAIRS, 4, 2, WIN])
    vf = [sb(f"vf{b}", [FRAME, 2, INNER]) for b in range(2)]
    mx = sb("mx", [P, HEADS])
    ex = sb("ex", [P, HEADS, KEYS])
    es = sb("es", [P, HEADS])
    er = sb("er", [P, HEADS])
    pd = sb("pd", [P, HEADS, FRAME])
    pT = sb("pT", [FRAME, HEADS, P])
    oT = sb("o_T", [P, PAIRS, P])
    xmid = [sb(f"xmid{b}", [P, DIM]) for b in range(2)]
    xf = [sb(f"xf{b}", [P, P + 1]) for b in range(2)]
    stats = sb("stats2", [P, 6])
    mv = sb("mv2", [P, 2])
    rstd = sb("rstd2", [P, 1])
    vareps = sb("vareps", [P, 1])
    xn = sb("xn2", [P, DIM])
    xnT = sb("xnT2", [P, P])
    ge = sb("ge", [P, NCH, P])
    u = sb("u", [P, NCH, P])
    xm2 = sb("xm2", [P, DIM])

    small = sem("small_loaded")
    init = sem("init")
    wkq_in, wv_in, wo_in, w1_in, w2_in = (sem(n) for n in ("wkq_in", "wv_in", "wo_in", "w1_in", "w2_in"))
    xcur_ready = sem("xcur_ready")
    rope_ready = sem("rope_ready")
    xp_done = sem("xp_done")
    xs_halo = sem("xs_halo")
    xs_ready = sem("xs_ready")
    k_done, q_done, v_done = sem("k_done"), sem("q_done"), sem("v_done")
    k_sq, q_sq, v_out = sem("k_sq"), sem("q_sq"), sem("v_out")
    k_prod, q_prod = sem("k_prod"), sem("q_prod")
    norm_chain = sem("norm_chain")
    norm_ready = sem("norm_ready")
    k_sum, q_sum = sem("k_sum"), sem("q_sum")
    k_hat, q_hat = sem("k_hat"), sem("q_hat")
    k_halo = sem("k_halo")
    tk_done, tq_done, tk_out, tq_out = sem("tk_done"), sem("tq_done"), sem("tk_out"), sem("tq_out")
    s_done = sem("s_done")
    max_ready = sem("max_ready")
    d_ready = sem("d_ready")
    exp_done = sem("exp_done")
    sum_chain = sem("sum_chain")
    p_ready = sem("p_ready")
    pt_done, pt_out = sem("pt_done"), sem("pt_out")
    pv_done, o_out = sem("pv_done"), sem("o_out")
    wo_done = sem("wo_done")
    xmid_ready = sem("xmid_ready")
    f1_done, xf_halo, xf_ready, f2_done = sem("f1_done"), sem("xf_halo"), sem("xf_ready"), sem("f2_done")
    ln_chain = sem("ln_chain")
    ln_moments = sem("ln_moments")
    eps_added = sem("eps_added")
    rstd_ready = sem("rstd_ready")
    xn_ready = sem("xn_ready")
    f3_done = sem("f3_done")
    xnT_ready = sem("xnT_ready")
    gate_done, up_done = sem("gate_done"), sem("up_done")
    gelu_done = sem("gelu_done")
    u_ready = sem("u_ready")
    y2_done = sem("y2_done")
    bias_added = sem("bias_added")

    SMALL = []

    TAIL = 3
    HEAD_STEPS = range(-1, 4)
    LOOP_PAIRS = (2, (TILES - 2) // 2)
    TAIL_STEPS = range(2 * LOOP_PAIRS[1], TILES + TAIL)

    def run(engine, step):
        for s in HEAD_STEPS:
            step(Tile(s // 2, s % 2))
        with engine.Fori(*LOOP_PAIRS) as pair:
            step(Tile(pair, 0))
            step(Tile(pair, 1))
        for s in TAIL_STEPS:
            step(Tile(s // 2, s % 2))

    def wide(ap, n=HEADS):
        return ap.unsqueeze(1).to_broadcast([P, n, ap.shape[-1]])

    with nc.Block() as block:

        @block.sync
        def _(sp):
            def small_load(dst, src):
                SMALL.append(1)
                sp.dma_start(dst, src, allow_slow_non_contiguous=True).then_inc(small, 16)

            Wqkv, Wo, W1, W2 = env["Wqkv"], env["Wo"], env["W1"], env["W2"]

            def load_layer(l, again):
                def src(w):
                    return w[l] if isinstance(l, int) else w[bass.ds(l, 1)].squeeze(0)

                if again:
                    sp.wait_ge(q_done, l * ROWS)
                sp.dma_start(wkq[:, 0:INNER], src(Wqkv)[:, INNER:2 * INNER]).then_inc(wkq_in, 16)
                sp.dma_start(wkq[:, INNER:2 * INNER], src(Wqkv)[:, 0:INNER]).then_inc(wkq_in, 16)
                if again:
                    sp.wait_ge(v_done, l * (4 * ROWS))
                sp.dma_start(wv[:, :], src(Wqkv)[:, 2 * INNER:3 * INNER]).then_inc(wv_in, 16)
                if again:
                    sp.wait_ge(wo_done, l * ROWS)
                sp.dma_start(wo[:, :, :], src(Wo).rearrange("(h p) d -> p h d", p=P)).then_inc(wo_in, 16)
                if again:
                    sp.wait_ge(up_done, l * ROWS)
                sp.dma_start(w1[:, :], src(W1)).then_inc(w1_in, 16)
                if again:
                    sp.wait_ge(y2_done, l * ROWS)
                whole = HIDDEN // P
                sp.dma_start(w2[:, 0:whole, :],
                             src(W2)[0:whole * P, :].rearrange("(c p) d -> p c d", p=P)).then_inc(w2_in, 16)
                sp.dma_start(w2[0:HIDDEN - whole * P, whole, :], src(W2)[whole * P:HIDDEN, :]).then_inc(w2_in, 16)

            load_layer(0, False)
            small_load(ropes[:, :, :], env["rope"])
            small_load(mask_in[:, :, :], env["mask"])
            small_load(first[:, :], env["first"])
            for n, name in ((0, "k_scale"), (2, "q_scale")):
                sc = env[name].rearrange("(o l) e -> o l e", o=1).to_broadcast([P, DEPTH, DH])
                small_load(scales[:, :, n, :], sc)
                small_load(scales[:, :, n + 1, 0:HALF], sc[:, :, HALF:DH])
                small_load(scales[:, :, n + 1, HALF:DH], sc[:, :, 0:HALF])
            small_load(g_all[:, :], env["ln_g"].rearrange("l d -> d l"))
            small_load(b_all[:, :], env["ln_b"].rearrange("l d -> d l"))
            for part in range(2):
                for c, (c0, m) in enumerate(CHUNKS):
                    o = part * HIDDEN + c0
                    small_load(b1_all[0:m, part, c, :], env["b1"][:, o:o + m].rearrange("l d -> d l"))
            small_load(b2_all[:, :, :], env["b2"].rearrange("(o l) d -> o l d", o=1).to_broadcast([P, DEPTH, DIM]))
            with nc.sync.Fori(1, DEPTH) as l:
                load_layer(l, True)

        SMALL_LOADED = 16 * len(SMALL)
        INIT = 10

        @block.gpsimd
        def _(pool):
            for buf in (xs[0], xs[1], xf[0], xf[1]):
                nc.gpsimd.memset(buf[:, :], 0.0).then_inc(init, 1)
            for buf in kT:
                nc.gpsimd.memset(buf[:, :, :], 0.0).then_inc(init, 1)
            nc.gpsimd.memset(qbd[:, :, :, :, :], 0.0).then_inc(init, 1)
            nc.gpsimd.memset(pd[:, :, :], 0.0).then_inc(init, 1)
            nc.gpsimd.tensor_copy(ident16[:, :], ident[:, :]).then_inc(init, 1)
            pool.wait_ge(small, SMALL_LOADED)
            nc.gpsimd.tensor_copy(masks[:, :, :], mask_in[:, :, :]).then_inc(init, 1)

            def step(now):
                nxt, a, f = now.lag(-1), now, now.lag(3)
                if nxt.live:
                    pool.wait_ge(x_ready, nxt.index + 1)
                    wait(pool, xp_done, nxt.index)
                    nc.gpsimd.tensor_copy(xcur[:, :], X[:, nxt.seq, bass.ds(nxt.pos, 1), :].squeeze(1)
                                          if not isinstance(nxt.pos, int) else X[:, nxt.seq, nxt.pos, :]
                                          ).then_inc(xcur_ready, 1)
                    wait(pool, q_prod, nxt.index - 1)
                    tab = turn_tab[nxt.seq][:, :, :].rearrange("p a e -> p (a e)")
                    if isinstance(nxt.pos, int):
                        rp, sc = ropes[:, nxt.pos, :], scales[:, nxt.layer, :, :].rearrange("p a e -> p (a e)")
                    else:
                        rp = ropes[:, bass.ds(nxt.pos, 1), :].squeeze(1)
                        sc = scales[:, bass.ds(nxt.layer, 1), :, :].rearrange("p l a e -> p (l a e)")
                    nc.gpsimd.tensor_tensor(tab, rp, sc, ALU.mult).then_inc(rope_ready, 1)
                if a.live:
                    pool.wait_ge(k_prod, a.index + 1)
                    nc.gpsimd.tensor_tensor(kq[:, 0], kq[:, 0], kq_sin[:, 0], ALU.add).then_inc(k_sum, 1)
                if f.live:
                    pool.wait_ge(ln_moments, f.index + 1)
                    nc.gpsimd.tensor_tensor(vareps[:, :], mv[:, 1:2], eps[:, 0:1], ALU.add).then_inc(eps_added, 1)
                    pool.wait_ge(eps_added, f.index + 1)
                    nc.gpsimd.tensor_tensor(rstd[:, :], vareps[:, :], minus_half[:, 0:1],
                                            ALU.pow).then_inc(rstd_ready, 1)
                if a.live:
                    pool.wait_ge(q_prod, a.index + 1)
                    nc.gpsimd.tensor_tensor(kq[:, 1], kq[:, 1], kq_sin[:, 1], ALU.add).then_inc(q_sum, 1)
                    pool.wait_ge(norm_ready, a.index + 1)
                    pool.wait_ge(k_sum, a.index + 1)
                    nc.gpsimd.tensor_tensor(kq[:, 0], kq[:, 0],
                                            inv[:, 0:HEADS].unsqueeze(2).to_broadcast([P, HEADS, DH]),
                                            ALU.mult).then_inc(k_hat, 1)
                    pool.wait_ge(q_sum, a.index + 1)
                    nc.gpsimd.tensor_tensor(kq[:, 1], kq[:, 1],
                                            inv[:, HEADS:2 * HEADS].unsqueeze(2).to_broadcast([P, HEADS, DH]),
                                            ALU.mult).then_inc(q_hat, 1)

            run(nc.gpsimd, step)

        @block.tensor
        def _(pe):
            pe.wait_ge(init, INIT)
            pe.wait_ge(small, SMALL_LOADED)

            def step(now):
                nxt, a, t, w, f = now.lag(-1), now, now.lag(1), now.lag(2), now.lag(3)
                if t.live:
                    pe.wait_ge(k_hat, t.index + 1)
                    for which, ready, done, banks in ((0, None, tk_done, (4, 5)), (1, q_hat, tq_done, (6, 4))):
                        if ready is not None:
                            pe.wait_ge(ready, t.index + 1)
                        for j in range(2):
                            if (which, j) == (1, 1):
                                pe.wait_ge(tk_out, t.index * 2 + 1)
                            for i in range(4):
                                h2 = 4 * j + i
                                last = nc.tensor.transpose(
                                    bank(banks[j])[:, i * P:(i + 1) * P],
                                    kq[:, which, 2 * h2:2 * h2 + 2, :].rearrange("p h e -> p (h e)"), ident[:, :])
                            last.then_inc(done, 1)
                if f.live:
                    pe.wait_ge(xmid_ready, f.index + 1)
                    wait(pe, x_ready, f.index + ROWS)
                    nc.tensor.transpose(bank(7)[:, 0:P], xmid[f.seq][:, :], ident[:, :]).then_inc(f1_done, 1)
                if a.live:
                    pe.wait_ge(wkq_in, (a.layer + 1) * 32)
                    pe.wait_ge(xs_ready, a.index + 1)
                    for done, j0 in ((k_done, 0), (q_done, 2)):
                        wait(pe, o_out, (a.index - 2) * 4 + 2 + j0)
                        for j in (j0, j0 + 1):
                            last = nc.tensor.matmul(bank(j), xs[a.seq][:, WIN:WIN + P],
                                                    wkq[:, j * BANK:(j + 1) * BANK], start=True, stop=True)
                        last.then_inc(done, 1)
                if f.live:
                    pe.wait_ge(xf_ready, f.index + 1)
                    nc.tensor.transpose(bank(7)[:, 0:P], xf[f.seq][:, 0:P], ident[:, :]).then_inc(f2_done, 1)
                if t.live:
                    pe.wait_ge(tk_out, t.index * 2 + 2)
                    pe.wait_ge(tq_out, t.index * 2 + 2)
                    for pw in range(2):
                        if pw == 1:
                            m = masks[:, POS, :]
                        elif isinstance(t.pos, int):
                            m = masks[:, t.pos, :]
                        else:
                            m = masks[:, bass.ds(t.pos, 1), :].squeeze(1)
                        nc.tensor.matmul(bank(5 + pw), ident16[:, :], wide(m, PAIRS), start=True, stop=False,
                                         skip_group_check=True)
                    for h2 in range(PAIRS):
                        for win in range(4):
                            last = nc.tensor.matmul(
                                bank(5 + win // 2)[64 * (win % 2):64 * (win % 2) + 64, h2 * KEYS:(h2 + 1) * KEYS],
                                qbd[:, h2, win].rearrange("p a i -> p (a i)"),
                                kT[t.seq][:, h2, WIN * win:WIN * win + KEYS],
                                start=False, stop=(h2 == PAIRS - 1), skip_group_check=True,
                                tile_position=(0, 64 * (win % 2)))
                    last.then_inc(s_done, 1)
                if f.live:
                    pe.wait_ge(xn_ready, f.index + 1)
                    nc.tensor.transpose(bank(7)[:, 0:P], xn[:, :], ident[:, :]).then_inc(f3_done, 1)
                if a.live:
                    pe.wait_ge(wv_in, (a.layer + 1) * 16)
                    for j in range(4):
                        pw, half = j // 2, j % 2
                        if half == 0:
                            pe.wait_ge((k_prod, q_prod)[pw], a.index + 1)
                        nc.tensor.matmul(bank(j)[0:FRAME, :], xs[a.seq][:, KEYS * pw:KEYS * pw + FRAME],
                                         wv[:, half * BANK:(half + 1) * BANK], start=True, stop=True
                                         ).then_inc(v_done, 1)
                if w.live:
                    pe.wait_ge(wo_in, (w.layer + 1) * 16)
                    pe.wait_ge(o_out, w.index * 4 + 4)
                    if now.lag(3).live:
                        pe.wait_ge(xnT_ready, f.index + 1)
                    for h2 in range(PAIRS):
                        last = nc.tensor.matmul(bank(7)[:, 0:DIM], oT[:, h2, :], wo[:, h2, :],
                                                start=(h2 == 0), stop=(h2 == PAIRS - 1))
                    last.then_inc(wo_done, 1)
                if nxt.live:
                    pe.wait_ge(xcur_ready, nxt.index + 1)
                    if w.live:
                        pe.wait_ge(xmid_ready, w.index + 1)
                    nc.tensor.transpose(bank(7)[:, 0:P], xcur[:, :], ident[:, :]).then_inc(xp_done, 1)
                if f.live:
                    pe.wait_ge(w1_in, (f.layer + 1) * 16)
                    pe.wait_ge(xnT_ready, f.index + 1)
                    if nxt.live:
                        pe.wait_ge(xs_ready, nxt.index + 1)
                    elif w.live:
                        pe.wait_ge(xmid_ready, w.index + 1)
                    if t.live:
                        pe.wait_ge(tq_out, t.index * 2 + 2)
                    for part, b, done in ((1, 4, gate_done), (0, 7, up_done)):
                        for c, (c0, m) in enumerate(CHUNKS):
                            last = nc.tensor.matmul(bank(b)[0:m, c * P:(c + 1) * P],
                                                    w1[:, part * HIDDEN + c0:part * HIDDEN + c0 + m], xnT[:, :],
                                                    start=True, stop=True)
                        last.then_inc(done, 1)
                if t.live:
                    pe.wait_ge(p_ready, t.index + 1)
                    if f.live:
                        pe.wait_ge(gelu_done, f.index + 1)
                    for j in range(4):
                        if j == 3:
                            pe.wait_ge(pt_out, t.index * 4 + 1)
                        for i in range(4):
                            last = nc.tensor.transpose(bank((4, 5, 6, 4)[j])[0:FRAME, i * P:(i + 1) * P],
                                                       pd[:, 4 * j + i, :], ident[:, :])
                        last.then_inc(pt_done, 1)
                if f.live:
                    pe.wait_ge(w2_in, (f.layer + 1) * 32)
                    pe.wait_ge(u_ready, f.index + 1)
                    for c, (c0, m) in enumerate(CHUNKS):
                        last = nc.tensor.matmul(bank(7)[:, 0:DIM], u[0:m, c, :], w2[0:m, c, :],
                                                start=(c == 0), stop=(c == NCH - 1))
                    last.then_inc(y2_done, 1)
                if t.live:
                    if a.live:
                        pe.wait_ge(v_out, a.index * 4 + 4)
                    else:
                        wait(pe, o_out, (t.index - 1) * 4 + 4)
                    for j in range(4):
                        pe.wait_ge(pt_out, t.index * 4 + j + 1)
                        for i in range(4):
                            g = 4 * j + i
                            pw, h2 = g // PAIRS, g % PAIRS
                            last = nc.tensor.matmul(bank(j)[:, i * P:(i + 1) * P], vf[t.seq][:, pw, h2 * P:(h2 + 1) * P],
                                                    pT[:, g, :], start=True, stop=True)
                        last.then_inc(pv_done, 1)

            run(nc.tensor, step)

        @block.scalar
        def _(act):
            act.wait_ge(init, INIT)
            act.wait_ge(small, SMALL_LOADED)

            def col(ap, index):
                return ap[:, index:index + 1] if isinstance(index, int) else ap[:, bass.ds(index, 1)]

            def step(now):
                a, t, f = now, now.lag(1), now.lag(3)
                if t.live:
                    pe_k = t.index * 2
                    act.wait_ge(k_halo, t.index + 1)
                    for j in range(2):
                        act.wait_ge(tk_done, pe_k + j + 1)
                        nc.scalar.activation(kT[t.seq][:, 4 * j:4 * j + 4, WIN:WIN + P],
                                             bank(4 + j).rearrange("p (h t) -> p h t", t=P),
                                             ACT.Copy).then_inc(tk_out, 1)
                    wait(act, s_done, t.index)
                    for j in range(2):
                        act.wait_ge(tq_done, pe_k + j + 1)
                        for half in range(2):
                            rows = slice(64 * half, 64 * half + 64)
                            last = nc.scalar.activation(
                                qbd[rows, 4 * j:4 * j + 4, :, half, :],
                                bank((6, 4)[j])[rows, :].rearrange("p (h w i) -> p h w i", w=4, i=WIN), ACT.Copy)
                        last.then_inc(tq_out, 1)
                if f.live:
                    act.wait_ge(f1_done, f.index + 1)
                    xb = xf[f.seq]
                    nc.scalar.activation(xb[:, 0:1], xb[:, P:P + 1], ACT.Copy,
                                         scale=col(first, f.pos)).then_inc(xf_halo, 1)
                    act.wait_ge(xf_halo, f.index + 1)
                    nc.scalar.activation(xb[0:64, 0:P], bank(7)[0:64, 0:P], ACT.Copy)
                    nc.scalar.activation(xb[64:P, 1:P + 1], bank(7)[64:P, 0:P], ACT.Copy).then_inc(xf_ready, 1)
                if a.live:
                    wait(act, norm_ready, a.index)
                    for n, (done, out) in enumerate(((k_done, k_sq), (q_done, q_sq))):
                        act.wait_ge(done, a.index + 1)
                        nc.scalar.activation(sqr[:, n * HEADS:(n + 1) * HEADS, :].rearrange("p h e -> p (h e)"),
                                             bank(2 * n, 2), ACT.Square).then_inc(out, 1)
                    wait(act, pv_done, (a.index - 1) * 4)
                    for j in range(4):
                        pw, half = j // 2, j % 2
                        act.wait_ge(v_done, a.index * 4 + j + 1)
                        nc.scalar.activation(vf[a.seq][:, pw, half * BANK:(half + 1) * BANK], bank(j)[0:FRAME, :],
                                             ACT.Copy).then_inc(v_out, 1)
                if t.live:
                    act.wait_ge(d_ready, t.index + 1)
                    nc.scalar.activation(ex[:, :, :], ex[:, :, :], ACT.Exp).then_inc(exp_done, 1)
                if f.live:
                    act.wait_ge(gate_done, f.index + 1)
                    wait(act, u_ready, f.index)
                    for c, (c0, m) in enumerate(CHUNKS):
                        last = nc.scalar.activation(ge[0:m, c, :], bank(4)[0:m, c * P:(c + 1) * P], ACT.Gelu,
                                                    bias=col(b1_all[0:m, 1, c, :], f.layer))
                    last.then_inc(gelu_done, 1)
                if t.live:
                    wait(act, pv_done, t.index * 4)
                    for j in range(4):
                        act.wait_ge(pt_done, t.index * 4 + j + 1)
                        nc.scalar.activation(pT[:, 4 * j:4 * j + 4, :].rearrange("p h t -> p (h t)"),
                                             bank((4, 5, 6, 4)[j])[0:FRAME, :], ACT.Copy).then_inc(pt_out, 1)

            run(nc.scalar, step)

        @block.vector
        def _(dve):
            dve.wait_ge(init, INIT)
            dve.wait_ge(small, SMALL_LOADED)

            def col(ap, index):
                return ap[:, index:index + 1] if isinstance(index, int) else ap[:, bass.ds(index, 1)]

            def tile_of(ap, index):
                return ap[:, index, :] if isinstance(index, int) else ap[:, bass.ds(index, 1), :].squeeze(1)

            NORM_LINKS = 12

            def step(now):
                nxt, a, t, w, f = now.lag(-1), now, now.lag(1), now.lag(2), now.lag(3)
                if w.live:
                    wait(dve, wo_done, w.index)
                    for pw in range(2):
                        dve.wait_ge(pv_done, w.index * 4 + 2 * pw + 2)
                        for head in range(2):
                            rows = slice(64 * head, 64 * head + 64)
                            src = bank(2 * pw, 2)[rows, :].rearrange("p (h w a i) -> p h w a i", w=2, a=2, i=WIN)
                            dst = oT[rows, :, 64 * pw:64 * pw + 64].rearrange("p h (w i) -> p h w i", i=WIN)
                            nc.vector.tensor_copy(dst, src[:, :, :, head, :]).then_inc(o_out, 1)
                if a.live:
                    wait(dve, s_done, a.index - 1)
                    wait(dve, tk_out, (a.index - 1) * 2)
                    nc.vector.tensor_scalar(kT[a.seq][:, :, 0:WIN], kT[a.seq][:, :, P:P + WIN],
                                            col(first, a.pos), None, ALU.mult).then_inc(k_halo, 1)
                    dve.wait_ge(rope_ready, a.index + 1)
                    wait(dve, tq_done, a.index * 2)
                    for n, (sq, done) in enumerate(((k_sq, k_prod), (q_sq, q_prod))):
                        dve.wait_ge(sq, a.index + 1)
                        src = bank(2 * n, 2).rearrange("p (h e) -> p h e", e=DH)
                        cos, sin = turn_tab[a.seq][:, 2 * n, :], turn_tab[a.seq][:, 2 * n + 1, :]
                        nc.vector.tensor_tensor(kq[:, n], src, wide(cos), ALU.mult)
                        nc.vector.tensor_tensor(kq_sin[:, n, :, 0:HALF], src[:, :, HALF:DH], wide(sin[:, 0:HALF]), ALU.mult)
                        nc.vector.tensor_tensor(kq_sin[:, n, :, HALF:DH], src[:, :, 0:HALF], wide(sin[:, HALF:DH]),
                                                ALU.mult).then_inc(done, 1)
                if f.live:
                    dve.wait_ge(f2_done, f.index + 1)
                    nc.vector.bn_stats(stats[:, :], bank(7)[:, 0:DIM]).then_inc(ln_chain, 1)
                if a.live:
                    count = [0]

                    def link(ins):
                        count[0] += 1
                        ins.then_inc(norm_chain, 1)
                        dve.wait_ge(norm_chain, a.index * NORM_LINKS + count[0])

                    wait(dve, q_hat, a.index)
                    if f.live:
                        dve.wait_ge(ln_chain, f.index + 1)
                    squares = nc.vector.tensor_reduce(ss[:, :], sqr[:, :, :], AX_X, ALU.add)
                if f.live:
                    if not a.live:
                        dve.wait_ge(ln_chain, f.index + 1)
                    nc.vector.bn_aggr(mv[:, :], stats[:, :]).then_inc(ln_moments, 1)
                if a.live:
                    link(squares)
                    link(nc.vector.tensor_scalar(ss[:, :], ss[:, :], 1e-24, None, ALU.max))
                    link(nc.vector.tensor_scalar(seed[:, :], ss[:, :].bitcast(I32), 1, None, ALU.logical_shift_right))
                    link(nc.vector.tensor_scalar(inv[:, :].bitcast(I32), seed[:, :], -1.0, float(RSQRT_SEED),
                                                 ALU.mult, ALU.add))
                    for n in range(3):
                        link(nc.vector.tensor_tensor(tmp[:, :], inv[:, :], inv[:, :], ALU.mult))
                        link(nc.vector.scalar_tensor_tensor(tmp[:, :], tmp[:, :], -0.5, ss[:, :], ALU.mult, ALU.mult))
                        ins = nc.vector.scalar_tensor_tensor(inv[:, :], tmp[:, :], 1.5, inv[:, :], ALU.add, ALU.mult)
                        if n < 2:
                            link(ins)
                    ins.then_inc(norm_ready, 1)
                    assert count[0] == NORM_LINKS
                if f.live:
                    dve.wait_ge(rstd_ready, f.index + 1)
                    wait(dve, f3_done, f.index)
                    nc.vector.tensor_scalar(xn[:, :], bank(7)[:, 0:DIM], mv[:, 0:1], rstd[:, 0:1],
                                            ALU.subtract, ALU.mult).then_inc(xn_ready, 1)
                if t.live:
                    dve.wait_ge(s_done, t.index + 1)
                    scores = bank(5, 2).rearrange("p (h k) -> p h k", k=KEYS)
                    nc.vector.tensor_reduce(mx[:, :], scores, AX_X, ALU.max).then_inc(max_ready, 1)
                    dve.wait_ge(max_ready, t.index + 1)
                    nc.vector.tensor_tensor(ex[:, :, :], scores, mx[:, :].unsqueeze(2).to_broadcast([P, HEADS, KEYS]),
                                            ALU.subtract).then_inc(d_ready, 1)
                if f.live:
                    dve.wait_ge(f3_done, f.index + 1)
                    wait(dve, up_done, f.index)
                    nc.vector.tensor_scalar(xnT[:, :], bank(7)[:, 0:P], col(g_all, f.layer), col(b_all, f.layer),
                                            ALU.mult, ALU.add).then_inc(xnT_ready, 1)
                if w.live:
                    dve.wait_ge(wo_done, w.index + 1)
                    wait(dve, f1_done, w.index - 1)
                    nc.vector.tensor_tensor(xmid[w.seq][:, :], bank(7)[:, 0:DIM], tile_of(X[:, w.seq], w.pos),
                                            ALU.add).then_inc(xmid_ready, 1)
                if nxt.live:
                    dve.wait_ge(xp_done, nxt.index + 1)
                    wait(dve, v_done, (nxt.index - 1) * 4)
                    xb = xs[nxt.seq]
                    nc.vector.tensor_scalar(xb[:, 0:WIN + 1], xb[:, P:P + WIN + 1], col(first, nxt.pos), None,
                                            ALU.mult).then_inc(xs_halo, 1)
                    dve.wait_ge(xs_halo, nxt.index + 1)
                    nc.vector.tensor_copy(xb[0:64, WIN:WIN + P], bank(7)[0:64, 0:P])
                    nc.vector.tensor_copy(xb[64:P, WIN + 1:WIN + P + 1], bank(7)[64:P, 0:P]).then_inc(xs_ready, 1)
                if t.live:
                    dve.wait_ge(exp_done, t.index + 1)
                    nc.vector.tensor_reduce(es[:, :], ex[:, :, :], AX_X, ALU.add).then_inc(sum_chain, 1)
                    dve.wait_ge(sum_chain, t.index * 2 + 1)
                    nc.vector.reciprocal(er[:, :], es[:, :]).then_inc(sum_chain, 1)
                    dve.wait_ge(sum_chain, t.index * 2 + 2)
                    wait(dve, pt_done, t.index * 4)
                    for half in range(2):
                        rows = slice(64 * half, 64 * half + 64)
                        last = nc.vector.tensor_tensor(pd[rows, :, WIN * half:WIN * half + KEYS], ex[rows, :, :],
                                                       er[rows, :].unsqueeze(2).to_broadcast([64, HEADS, KEYS]),
                                                       ALU.mult)
                    last.then_inc(p_ready, 1)
                if f.live:
                    dve.wait_ge(gelu_done, f.index + 1)
                    dve.wait_ge(up_done, f.index + 1)
                    wait(dve, y2_done, f.index)
                    for c, (c0, m) in enumerate(CHUNKS):
                        last = nc.vector.scalar_tensor_tensor(u[0:m, c, :], bank(7)[0:m, c * P:(c + 1) * P],
                                                              col(b1_all[0:m, 0, c, :], f.layer), ge[0:m, c, :],
                                                              ALU.add, ALU.mult)
                    last.then_inc(u_ready, 1)
                    nc.vector.tensor_tensor(xm2[:, :], xmid[f.seq][:, :], tile_of(b2_all, f.layer),
                                            ALU.add).then_inc(bias_added, 1)
                    dve.wait_ge(bias_added, f.index + 1)
                    dve.wait_ge(y2_done, f.index + 1)
                    nc.vector.tensor_tensor(tile_of(X[:, f.seq], f.pos), bank(7)[:, 0:DIM], xm2[:, :],
                                            ALU.add).then_inc(x_ready, 1)

            run(nc.vector, step)


def phase_three(nc, stack, new_sem, new_sb, env):
    X, X1, minus_half, eps = (env[k] for k in ("X", "X1", "minus_half", "eps"))

    def sem(name):
        return new_sem(name, stack)

    stats = new_sb("stats3", [P, ROWS, 6], F32, stack)
    mv = new_sb("mv3", [P, ROWS, 2], F32, stack)
    rstd = new_sb("rstd3", [P, ROWS], F32, stack)
    z = new_sb("z3", [P, ROWS, DIM], F32, stack)
    stats_in, moments, eps_added, rstd_ready = sem("p3_stats"), sem("p3_moments"), sem("p3_eps"), sem("p3_rstd")
    normed, summed, stored = sem("p3_normed"), sem("p3_summed"), sem("p3_stored")
    xf = X[:, :, :, :].rearrange("p b n d -> p (b n) d")
    x1f = X1[:, :, :, :].rearrange("p b n d -> p (b n) d")
    QUARTER = ROWS // 4

    with nc.Block() as block:

        @block.gpsimd
        def _(pool):
            pool.wait_ge(moments, 1)
            nc.gpsimd.tensor_tensor(rstd[:, :], mv[:, :, 1], eps[:, :], ALU.add).then_inc(eps_added, 1)
            pool.wait_ge(eps_added, 1)
            nc.gpsimd.tensor_tensor(rstd[:, :], rstd[:, :], minus_half[:, :], ALU.pow).then_inc(rstd_ready, 1)

        @block.vector
        def _(dve):
            for t in range(ROWS):
                last = nc.vector.bn_stats(stats[:, t, :], xf[:, t, :])
            last.then_inc(stats_in, 1)
            dve.wait_ge(stats_in, 1)
            for t in range(ROWS):
                last = nc.vector.bn_aggr(mv[:, t, :], stats[:, t, :])
            last.then_inc(moments, 1)
            dve.wait_ge(rstd_ready, 1)
            dve.wait_ge(moments, 1)
            for t in range(ROWS):
                nc.vector.tensor_scalar(z[:, t, :], xf[:, t, :], mv[:, t, 0:1], rstd[:, t:t + 1],
                                        ALU.subtract, ALU.mult).then_inc(normed, 1)
            for q in range(4):
                s = slice(q * QUARTER, (q + 1) * QUARTER)
                dve.wait_ge(normed, (q + 1) * QUARTER)
                nc.vector.tensor_tensor(z[:, s, :], z[:, s, :], x1f[:, s, :], ALU.add).then_inc(summed, 1)

        @block.sync
        def _(sp):
            dst = env["out"].rearrange("b (n t) d -> t (b n) d", t=P)
            for q in range(4):
                s = slice(q * QUARTER, (q + 1) * QUARTER)
                sp.wait_ge(summed, q + 1)
                sp.dma_start(dst[:, s, :], z[:, s, :]).then_inc(stored, 16)
            sp.wait_ge(stored, 64)


def shape_constants():
    import numpy as np
    f = np.float32
    half = np.arange(0, DH, 2, dtype=f)
    inv_freq = (f(1.0) / np.power(f(10000.0), half / f(DH))).astype(f)
    t = np.arange(LENGTH, dtype=f)
    ang = (t[:, None] * inv_freq[None, :]).astype(f)
    base = ((half + f(0.4 * DH)) / f(1.4 * DH)).astype(f)
    power = ((t - f(LENGTH // 2)) / f(WIN // 2)).astype(f)
    scale = np.power(base[None, :].astype(np.float64), power[:, None].astype(np.float64))
    cos, sin = np.cos(ang.astype(np.float64)), np.sin(ang.astype(np.float64))

    def both(lo, hi):
        return np.concatenate([lo, hi], -1)

    tabs = [both(cos / scale, cos / scale), both(-sin / scale, sin / scale),
            both(cos * scale, cos * scale) * QK_SCALE, both(-sin * scale, sin * scale) * QK_SCALE]
    rope = np.stack(tabs, 1).reshape(POS, P, 4 * DH).transpose(1, 0, 2).astype(f)
    i = np.arange(WIN)[:, None] + WIN
    j = np.arange(KEYS)[None, :]
    later = np.where((i < j) | (i > j + WIN), MASKED, 0.0)
    start = np.where(j < WIN, MASKED, later)
    rows = np.tile(later, (4, 1))
    rows0 = np.concatenate([start, start, later, later], 0)
    mask = np.stack([rows0] + [rows] * POS, 1)
    first = np.ones((P, POS), f)
    first[:, 0] = 0
    return rope, mask.astype(f), first


def kernel(**inputs):
    import numpy as np
    import concourse.bacc as bacc
    from concourse.bass_utils import run_bass_kernel_spmd

    def gla(name):
        return np.ascontiguousarray(inputs["L0_attn_" + name])

    def ffn(name):
        return np.ascontiguousarray(inputs["L0_ffn_" + name])

    def repeated(w):
        w = w.reshape(DIM, GLA_HEADS, GLA_DH).transpose(0, 2, 1)
        return np.ascontiguousarray(np.repeat(w, GLA_DH, axis=2))

    rope, mask, first = shape_constants()
    arrays = {"x": gla("x"), "Wq_rep": repeated(gla("Wq")), "Wk_rep": repeated(gla("Wk"))}
    for name in ("Wv", "Wg", "Wgk1", "Wgk2", "bgk2", "gamma", "beta", "Wout"):
        arrays[name] = gla(name)
    for name in ("Wqkv", "q_scale", "k_scale", "Wo", "ln_g", "ln_b", "W1", "b1", "W2", "b2"):
        arrays[name] = ffn(name)
    arrays.update(rope=rope, mask=mask, first=first)
    nc = bacc.Bacc("TRN2", target_bir_lowering=False, num_devices=1)
    aps = {name: nc.dram_tensor("in_" + name, a.shape, mybir.dt.from_np(a.dtype), kind="ExternalInput").ap()
           for name, a in arrays.items()}
    out = nc.dram_tensor("out", (BATCH, LENGTH, DIM), F32, kind="ExternalOutput").ap()
    build(nc, out=out, **aps)
    r = run_bass_kernel_spmd(nc, [{"in_" + name: a for name, a in arrays.items()}], core_ids=[0])
    return r.results[0]["out"]
```

```python
from contextlib import ExitStack

import concourse.bass as bass
from concourse import mybir

F32 = mybir.dt.float32
BF16 = mybir.dt.bfloat16
I32 = mybir.dt.int32
ALU = mybir.AluOpType
ACT = mybir.ActivationFunctionType
AX_X = mybir.AxisListType.X

P = 128
DIM = 128
BATCH = 2
LENGTH = 1024
POS = LENGTH // P
ROWS = BATCH * POS
GLA_HEADS = 16
GLA_DH = 8
RANK = 16
DEPTH = 6
HEADS = 16
DH = 64
PAIRS = HEADS // 2
INNER = HEADS * DH
HALF = DH // 2
WIN = 32
KEYS = 2 * WIN
HIDDEN = int(DIM * 4 * 2 / 3)
CHUNKS = [(c * P, min(P, HIDDEN - c * P)) for c in range((HIDDEN + P - 1) // P)]
NCH = len(CHUNKS)
QK_SCALE = 8.0
EPS = 1e-5
MASKED = -1e30
TILES = ROWS * DEPTH
BANK = 512
WINDOWS = P // WIN
RSQRT_SEED = 0x5F3759DF


def wait(eng, sem, value):
    if not (isinstance(value, int) and value <= 0):
        eng.wait_ge(sem, value)


class Tile:

    def __init__(self, pair, seq):
        self.pair, self.seq = pair, seq

    def lag(self, n):
        d = self.seq - n
        return Tile(self.pair + d // 2, d % 2)

    @property
    def index(self):
        return self.pair * 2 + self.seq

    @property
    def pos(self):
        return self.pair % POS

    @property
    def layer(self):
        return self.pair // POS

    @property
    def live(self):
        return not isinstance(self.pair, int) or 0 <= self.index < TILES


def at(ap, index, size=1):
    return bass.ds(index * size, size)


def build(nc, x, Wq_rep, Wk_rep, Wv, Wg, Wgk1, Wgk2, bgk2, gamma, beta, Wout,
          Wqkv, q_scale, k_scale, Wo, ln_g, ln_b, W1, b1, W2, b2, rope, mask, first, out):
    ctx = ExitStack()
    with ctx:
        def sem(name, stack=ctx):
            return stack.enter_context(nc.semaphore(name))

        def sb(name, shape, dt=F32, stack=ctx):
            return stack.enter_context(nc.sbuf_tensor(name, shape, dt))

        X = sb("X", [P, BATCH, POS, DIM])
        X1 = sb("X1", [P, BATCH, POS, DIM])
        ident = sb("ident", [P, P])
        minus_half = sb("minus_half", [P, ROWS])
        eps = sb("eps", [P, ROWS])
        PS = ctx.enter_context(nc.psum_tensor("PS", [P, 8 * BANK], F32))

        def bank(j, n=1):
            return PS[:, j * BANK:(j + n) * BANK]

        x_ready = sem("x_ready")
        const_ready = sem("const_ready")
        with ExitStack() as one:
            phase_one(nc, one, sem, sb, bank, locals())
        with ExitStack() as two:
            phase_two(nc, two, sem, sb, bank, locals())
        with ExitStack() as three:
            phase_three(nc, three, sem, sb, locals())


def phase_one(nc, stack, new_sem, new_sb, bank, env):
    X, X1, ident, minus_half, eps = (env[k] for k in ("X", "X1", "ident", "minus_half", "eps"))
    x_ready, const_ready = env["x_ready"], env["const_ready"]

    def sem(name):
        return new_sem(name, stack)

    def sb(name, shape, dt=F32):
        return new_sb(name, shape, dt, stack)

    T = BATCH * LENGTH
    NB = T // BANK
    wk = sb("wk", [P, GLA_DH, P])
    wq = sb("wq", [P, GLA_DH, P])
    wv = sb("wv", [P, P])
    wg = sb("wg", [P, P])
    wgk1 = sb("wgk1", [P, RANK])
    wgk2 = sb("wgk2", [RANK, P])
    wout = sb("wout", [P, P])
    bgk = sb("bgk", [P, 1])
    gam = sb("gam", [P, DIM])
    bet = sb("bet", [P, DIM])
    xn = sb("xn", [P, ROWS, DIM])
    xnT = sb("xnT", [P, T])
    vT = sb("vT", [P, T])
    low = sb("low", [RANK, T])
    gate = sb("gate", [P, T])
    za = sb("za", [P, T])
    zb = sb("zb", [P, T])
    kv = sb("kv", [P, 2, LENGTH])
    st = sb("st", [P, 2, LENGTH])
    sq = sb("sqg", [P, 2, LENGTH])
    oT = sb("oT", [P, T])
    stats = sb("stats1", [P, ROWS, 6])
    mv = sb("mv1", [P, ROWS, 2])
    rstd = sb("rstd1", [P, ROWS])

    loaded = sem("p1_loaded")
    pool_self = sem("p1_pool_self")
    moments = sem("p1_moments")
    rstd_ready = sem("p1_rstd")
    dve_self = sem("p1_dve_self")
    normed = sem("p1_normed")
    turned = sem("p1_turned")
    turned_out = sem("p1_turned_out")
    proj = sem("p1_proj")
    proj_out = sem("p1_proj_out")
    z_ready = sem("p1_z")
    act_self = sem("p1_act_self")
    soft = sem("p1_soft")
    arg_ready = sem("p1_arg")
    gate_ready = sem("p1_gate")
    krep_done = sem("p1_krep")
    krep_used = sem("p1_krep_used")
    qrep_done = sem("p1_qrep")
    read_done = sem("p1_read")
    summed = sem("p1_summed")
    gmul_done = sem("p1_gmul")
    silu_done = sem("p1_silu")
    o_used = sem("p1_o_used")
    mixed = sem("p1_mixed")
    y_done = sem("p1_y")
    y_used = sem("p1_y_used")
    x1_ready = sem("p1_x1")

    LOOPS = [(b, kk) for kk in range(GLA_DH) for b in range(BATCH)]
    x1f = X1[:, :, :, :].rearrange("p b n d -> p (b n) d")
    xf = X[:, :, :, :].rearrange("p b n d -> p (b n) d")
    with nc.Block() as block:

        @block.sync
        def _(sp):
            sp.dma_start(X1[:, :, :, :], env["x"].rearrange("b (n t) d -> t b n d", t=P)).then_inc(loaded, 16)
            for dst, src in ((wv[:, :], env["Wv"]), (wk[:, :, :], env["Wk_rep"]), (wq[:, :, :], env["Wq_rep"]),
                             (wgk1[:, :], env["Wgk1"]), (wgk2[:, :], env["Wgk2"]),
                             (bgk[:, :], env["bgk2"].rearrange("(p o) -> p o", o=1)),
                             (wg[:, :], env["Wg"]), (wout[:, :], env["Wout"]),
                             (gam[:, :], env["gamma"].rearrange("(o d) -> o d", o=1).to_broadcast([P, DIM])),
                             (bet[:, :], env["beta"].rearrange("(o d) -> o d", o=1).to_broadcast([P, DIM]))):
                sp.dma_start(dst, src).then_inc(loaded, 16)

        ALL_LOADED = 16 * 11

        @block.gpsimd
        def _(pool):
            nc.gpsimd.memset(ident[:, :], 0.0).then_inc(pool_self, 1)
            nc.gpsimd.memset(minus_half[:, :], -0.5).then_inc(const_ready, 1)
            nc.gpsimd.memset(eps[:, :], EPS).then_inc(const_ready, 1)
            pool.wait_ge(pool_self, 1)
            nc.gpsimd.affine_select(out=ident[:, :], in_=ident[:, :], compare_op=ALU.not_equal, fill=1.0,
                                    base=0, pattern=[[-1, P]], channel_multiplier=1).then_inc(const_ready, 1)
            pool.wait_ge(const_ready, 3)
            steps = [1]

            def inverse_deviation(k):
                pool.wait_ge(moments, k + 1)
                nc.gpsimd.tensor_tensor(rstd[:, :], mv[:, :, 1], eps[:, :], ALU.add).then_inc(pool_self, 1)
                steps[0] += 1
                pool.wait_ge(pool_self, steps[0])
                nc.gpsimd.tensor_tensor(rstd[:, :], rstd[:, :], minus_half[:, :], ALU.pow).then_inc(rstd_ready, 1)

            inverse_deviation(0)
            for i, (b, kk) in enumerate(LOOPS):
                pool.wait_ge(read_done, i + 1)
                dst = oT[:, b * LENGTH:(b + 1) * LENGTH]
                if kk == 0:
                    nc.gpsimd.tensor_copy(dst, sq[:, i % 2, :]).then_inc(summed, 1)
                else:
                    pool.wait_ge(summed, i - 1)
                    nc.gpsimd.tensor_tensor(dst, dst, sq[:, i % 2, :], ALU.add).then_inc(summed, 1)
            for k in (1, 2, 3):
                inverse_deviation(k)

        @block.tensor
        def _(pe):
            def turn(src, tiles_ready, use, base):
                for j in range(NB):
                    for i in range(4):
                        pe.wait_ge(tiles_ready, base + 4 * j + i + 1)
                        last = nc.tensor.transpose(bank(j)[:, i * P:(i + 1) * P], src(4 * j + i), ident[:, :])
                    last.then_inc(turned, 1)

            pe.wait_ge(const_ready, 3)
            turn(lambda i: xn[:, i, :], normed, None, 0)
            pe.wait_ge(loaded, ALL_LOADED)
            for j in range(NB):
                pe.wait_ge(turned_out, j + 1)
                nc.tensor.matmul(bank(4 + j), wv[:, :], xnT[:, j * BANK:(j + 1) * BANK],
                                 start=True, stop=True).then_inc(proj, 1)
            for j in range(NB):
                nc.tensor.matmul(bank(j)[0:RANK, :], wgk1[:, :], xnT[:, j * BANK:(j + 1) * BANK],
                                 start=True, stop=True).then_inc(proj, 1)
            for j in range(NB):
                pe.wait_ge(proj_out, 5 + j)
                nc.tensor.matmul(bank(4 + j), wgk2[:, :], low[:, j * BANK:(j + 1) * BANK],
                                 start=True, stop=True).then_inc(proj, 1)
            for i, (b, kk) in enumerate(LOOPS):
                base = 4 * (i % 2)
                if i == 1:
                    pe.wait_ge(z_ready, NB)
                if i >= 2:
                    pe.wait_ge(krep_used, i - 1)
                for j in range(2):
                    last = nc.tensor.matmul(bank(base + j), wk[:, kk, :],
                                            xnT[:, b * LENGTH + j * BANK:b * LENGTH + (j + 1) * BANK],
                                            start=True, stop=True)
                last.then_inc(krep_done, 1)
                if i >= 2:
                    pe.wait_ge(read_done, i - 1)
                for j in range(2):
                    last = nc.tensor.matmul(bank(base + 2 + j), wq[:, kk, :],
                                            xnT[:, b * LENGTH + j * BANK:b * LENGTH + (j + 1) * BANK],
                                            start=True, stop=True)
                last.then_inc(qrep_done, 1)
            pe.wait_ge(read_done, len(LOOPS))
            for j in range(NB):
                for i in range(4):
                    t = 4 * j + i
                    last = nc.tensor.matmul(bank(4 + j)[:, i * P:(i + 1) * P], xnT[:, t * P:(t + 1) * P],
                                            wg[:, :], start=True, stop=True)
                last.then_inc(gmul_done, 1)
            pe.wait_ge(summed, len(LOOPS))
            for j in range(NB):
                for i in range(4):
                    t = 4 * j + i
                    last = nc.tensor.transpose(bank(j)[:, i * P:(i + 1) * P], oT[:, t * P:(t + 1) * P], ident[:, :])
                last.then_inc(turned, 1)
            pe.wait_ge(o_used, ROWS)
            for j in range(NB):
                for i in range(4):
                    t = 4 * j + i
                    pe.wait_ge(mixed, t + 1)
                    last = nc.tensor.transpose(bank(j)[:, i * P:(i + 1) * P], xn[:, t, :], ident[:, :])
                last.then_inc(turned, 1)
            pe.wait_ge(silu_done, NB)
            for j in range(NB):
                pe.wait_ge(turned_out, NB + j + 1)
                for i in range(4):
                    t = 4 * j + i
                    last = nc.tensor.matmul(bank(4 + j)[:, i * P:(i + 1) * P], xnT[:, t * P:(t + 1) * P],
                                            wout[:, :], start=True, stop=True)
                last.then_inc(y_done, 1)

        @block.scalar
        def _(act):
            for j in range(NB):
                act.wait_ge(turned, j + 1)
                nc.scalar.activation(xnT[:, j * BANK:(j + 1) * BANK], bank(j), ACT.Copy).then_inc(turned_out, 1)
            for j in range(NB):
                act.wait_ge(proj, j + 1)
                nc.scalar.activation(vT[:, j * BANK:(j + 1) * BANK], bank(4 + j), ACT.Copy).then_inc(proj_out, 1)
            for j in range(NB):
                act.wait_ge(proj, NB + j + 1)
                nc.scalar.activation(low[:, j * BANK:(j + 1) * BANK], bank(j)[0:RANK, :],
                                     ACT.Copy).then_inc(proj_out, 1)
            for j in range(NB):
                s = slice(j * BANK, (j + 1) * BANK)
                act.wait_ge(z_ready, j + 1)
                nc.scalar.activation(zb[:, s], za[:, s], ACT.Abs).then_inc(act_self, 1)
            for j in range(NB):
                s = slice(j * BANK, (j + 1) * BANK)
                act.wait_ge(act_self, j + 1)
                nc.scalar.activation(zb[:, s], zb[:, s], ACT.Exp, scale=-1.0).then_inc(act_self, 1)
            for j in range(NB):
                s = slice(j * BANK, (j + 1) * BANK)
                act.wait_ge(act_self, NB + j + 1)
                nc.scalar.activation(zb[:, s], zb[:, s], ACT.Ln, bias=1.0).then_inc(soft, 1)
            for j in range(NB):
                s = slice(j * BANK, (j + 1) * BANK)
                act.wait_ge(arg_ready, j + 1)
                nc.scalar.activation(gate[:, s], zb[:, s], ACT.Exp, scale=1.0 / 16.0).then_inc(gate_ready, 1)
            for j in range(NB):
                act.wait_ge(gmul_done, j + 1)
                nc.scalar.activation(za[:, j * BANK:(j + 1) * BANK], bank(4 + j), ACT.Silu).then_inc(silu_done, 1)
            for j in range(NB):
                act.wait_ge(turned, 2 * NB + j + 1)
                nc.scalar.activation(xnT[:, j * BANK:(j + 1) * BANK], bank(j), ACT.Copy).then_inc(turned_out, 1)

        @block.vector
        def _(dve):
            links = [0]

            def link(ins):
                links[0] += 1
                ins.then_inc(dve_self, 1)
                dve.wait_ge(dve_self, links[0])

            def take_moments(k, src, ready=None):
                for t in range(ROWS):
                    if ready is not None and t % 4 == 0:
                        dve.wait_ge(*ready(t))
                    last = nc.vector.bn_stats(stats[:, t, :], src(t))
                link(last)
                for t in range(ROWS):
                    last = nc.vector.bn_aggr(mv[:, t, :], stats[:, t, :])
                last.then_inc(moments, 1)
                dve.wait_ge(rstd_ready, k + 1)

            def normalise(dst, src, t):
                return nc.vector.tensor_scalar(dst, src, mv[:, t, 0:1], rstd[:, t:t + 1], ALU.subtract, ALU.mult)

            dve.wait_ge(loaded, ALL_LOADED)
            take_moments(0, lambda t: x1f[:, t, :])
            for t in range(ROWS):
                normalise(xn[:, t, :], x1f[:, t, :], t).then_inc(normed, 1)
            for j in range(NB):
                s = slice(j * BANK, (j + 1) * BANK)
                dve.wait_ge(proj, 2 * NB + j + 1)
                nc.vector.tensor_scalar(za[:, s], bank(4 + j), bgk[:, 0:1], None, ALU.add).then_inc(z_ready, 1)
            dve.wait_ge(z_ready, NB)
            for j in range(NB):
                s = slice(j * BANK, (j + 1) * BANK)
                dve.wait_ge(soft, j + 1)
                nc.vector.scalar_tensor_tensor(zb[:, s], za[:, s], 0.0, zb[:, s], ALU.min,
                                               ALU.subtract).then_inc(arg_ready, 1)
            dve.wait_ge(gate_ready, NB)
            for i, (b, kk) in enumerate(LOOPS):
                s = slice(b * LENGTH, (b + 1) * LENGTH)
                base = 4 * (i % 2)
                dve.wait_ge(krep_done, i + 1)
                ins = nc.vector.tensor_tensor(kv[:, i % 2, :], bank(base, 2), vT[:, s], ALU.mult)
                ins.then_inc(krep_used, 1)
                dve.wait_ge(krep_used, i + 1)
                link(nc.vector.tensor_tensor_scan(st[:, i % 2, :], gate[:, s], kv[:, i % 2, :], 0.0,
                                                  ALU.mult, ALU.add))
                dve.wait_ge(qrep_done, i + 1)
                if i >= 2:
                    dve.wait_ge(summed, i - 1)
                nc.vector.tensor_tensor(sq[:, i % 2, :], bank(base + 2, 2), st[:, i % 2, :],
                                        ALU.mult).then_inc(read_done, 1)
            take_moments(1, lambda t: bank(t // 4)[:, (t % 4) * P:(t % 4 + 1) * P],
                         lambda t: (turned, NB + t // 4 + 1))
            for t in range(ROWS):
                normalise(xn[:, t, :], bank(t // 4)[:, (t % 4) * P:(t % 4 + 1) * P], t).then_inc(o_used, 1)
            dve.wait_ge(o_used, ROWS)
            wide = [P, ROWS, DIM]
            link(nc.vector.tensor_tensor(xn[:, :, :], xn[:, :, :], gam[:, :].unsqueeze(1).to_broadcast(wide), ALU.mult))
            link(nc.vector.tensor_tensor(xn[:, :, :], xn[:, :, :], bet[:, :].unsqueeze(1).to_broadcast(wide), ALU.add))
            zv = za[:, :].rearrange("p (t d) -> p t d", d=DIM)
            for t in range(ROWS):
                if t % 4 == 0:
                    dve.wait_ge(silu_done, t // 4 + 1)
                nc.vector.tensor_tensor(xn[:, t, :], xn[:, t, :], zv[:, t, :], ALU.mult).then_inc(mixed, 1)

            def y(t):
                return bank(4 + t // 4)[:, (t % 4) * P:(t % 4 + 1) * P]

            take_moments(2, y, lambda t: (y_done, t // 4 + 1))
            for t in range(ROWS):
                last = normalise(vT[:, t * DIM:(t + 1) * DIM], y(t), t)
            link(last)
            link(nc.vector.tensor_tensor(x1f, x1f, vT[:, :].rearrange("p (t d) -> p t d", d=DIM), ALU.add))
            take_moments(3, lambda t: x1f[:, t, :])
            for t in range(ROWS):
                normalise(xf[:, t, :], x1f[:, t, :], t).then_inc(x_ready, 1)


def phase_two(nc, stack, new_sem, new_sb, bank, env):
    X, ident, minus_half, eps = (env[k] for k in ("X", "ident", "minus_half", "eps"))
    x_ready = env["x_ready"]

    def sem(name):
        return new_sem(name, stack)

    def sb(name, shape, dt=F32):
        return new_sb(name, shape, dt, stack)

    BLOCKS = 4 * WINDOWS
    wkq = sb("wkq", [P, 2 * INNER])
    wv = sb("w_v", [P, INNER])
    wo = sb("w_o", [P, PAIRS, DIM])
    w1 = sb("w_1", [P, 2 * HIDDEN])
    w2 = sb("w_2", [P, NCH, DIM])
    scales = sb("scales", [P, DEPTH, 4, DH])
    g_all = sb("g_all", [P, DEPTH])
    b_all = sb("b_all", [P, DEPTH])
    b1_all = sb("b1_all", [P, 2, NCH, DEPTH])
    b2_all = sb("b2_all", [P, DEPTH, DIM])
    ropes = sb("ropes", [P, POS, 4 * DH])
    mask_in = sb("mask_in", [P, POS, WINDOWS * KEYS])
    masks = sb("masks", [P, POS, WINDOWS * KEYS], BF16)
    first = sb("first", [P, POS])
    ident16 = sb("ident16", [P, P], BF16)
    xcur = sb("xcur", [P, DIM])
    xs = [sb(f"xs{b}", [P, P + 1]) for b in range(2)]
    turn_tab = [sb(f"turn_tab{b}", [P, 4, DH]) for b in range(2)]
    sqr = sb("sqr", [P, 2 * HEADS, DH])
    kq = [sb(f"kq{b}", [P, 2, HEADS, DH]) for b in range(2)]
    kq_sin = sb("kq_sin", [P, 2, HEADS, DH])
    ss = sb("ss", [P, 2 * HEADS])
    seed = sb("seed", [P, 2 * HEADS], I32)
    inv = sb("inv", [P, 2 * HEADS])
    tmp = sb("tmp", [P, 2 * HEADS])
    kT = [sb(f"kT{b}", [P, PAIRS, WIN + P]) for b in range(2)]
    qbd = sb("qbd", [P, PAIRS, 4, 2, WIN])
    vn = [sb(f"vn{b}", [P, INNER]) for b in range(2)]
    vs = [sb(f"vs{b}", [P, INNER]) for b in range(2)]
    mx = sb("mx", [P, BLOCKS])
    ex = sb("ex", [P, BLOCKS, KEYS])
    es = sb("es", [P, BLOCKS])
    er = sb("er", [P, BLOCKS])
    pn = sb("pn", [P, BLOCKS, KEYS])
    pT = sb("pT", [P, 8, 4, 2, WIN])
    warm = sb("warm", [P, 1])
    oT = sb("o_T", [P, PAIRS, P])
    xmid = [sb(f"xmid{b}", [P, DIM]) for b in range(2)]
    xf = [sb(f"xf{b}", [P, P + 1]) for b in range(2)]
    stats = sb("stats2", [P, 6])
    mv = sb("mv2", [P, 2])
    rstd = sb("rstd2", [P, 1])
    vareps = sb("vareps", [P, 1])
    xn = sb("xn2", [P, DIM])
    xnT = sb("xnT2", [P, P])
    ge = sb("ge", [P, NCH, P])
    u = sb("u", [P, NCH, P])
    xm2 = sb("xm2", [P, DIM])

    small = sem("small_loaded")
    init = sem("init")
    wkq_in, wv_in, wo_in, w1_in, w2_in = (sem(n) for n in ("wkq_in", "wv_in", "wo_in", "w1_in", "w2_in"))
    xcur_ready = sem("xcur_ready")
    rope_ready = sem("rope_ready")
    xp_done = sem("xp_done")
    xs_halo = sem("xs_halo")
    xs_ready = sem("xs_ready")
    k_done, q_done, v_done = sem("k_done"), sem("q_done"), sem("v_done")
    k_sq, q_sq, v_out = sem("k_sq"), sem("q_sq"), sem("v_out")
    k_prod, q_prod = sem("k_prod"), sem("q_prod")
    norm_chain = sem("norm_chain")
    norm_ready = sem("norm_ready")
    k_sum, q_sum = sem("k_sum"), sem("q_sum")
    k_hat, q_hat = sem("k_hat"), sem("q_hat")
    k_halo = sem("k_halo")
    tk_done, tq_done, tk_out, tq_out = sem("tk_done"), sem("tq_done"), sem("tk_out"), sem("tq_out")
    s_done = sem("s_done")
    max_ready = sem("max_ready")
    d_ready = sem("d_ready")
    exp_done = sem("exp_done")
    sum_chain = sem("sum_chain")
    p_ready = sem("p_ready")
    pt_done, pt_out = sem("pt_done"), sem("pt_out")
    v_halo = [sem(f"v_halo{b}") for b in range(2)]
    v_shifted = [sem(f"v_shifted{b}") for b in range(2)]
    pv_done, o_out = sem("pv_done"), sem("o_out")
    warmed = sem("warmed")
    wo_done = sem("wo_done")
    xmid_ready = sem("xmid_ready")
    f1_done, xf_halo, xf_ready, f2_done = sem("f1_done"), sem("xf_halo"), sem("xf_ready"), sem("f2_done")
    ln_chain = sem("ln_chain")
    ln_moments = sem("ln_moments")
    eps_added = sem("eps_added")
    rstd_ready = sem("rstd_ready")
    xn_ready = sem("xn_ready")
    f3_done = sem("f3_done")
    xnT_ready = sem("xnT_ready")
    gate_done, up_done = sem("gate_done"), sem("up_done")
    gelu_done = sem("gelu_done")
    u_ready = sem("u_ready")
    y2_done = sem("y2_done")
    bias_added = sem("bias_added")

    SMALL = []

    TAIL = 4
    HEAD_STEPS = range(-1, 6)
    LOOP_PAIRS = (3, (TILES - 2) // 2)
    TAIL_STEPS = range(2 * LOOP_PAIRS[1], TILES + TAIL)

    def run(engine, step):
        for s in HEAD_STEPS:
            step(Tile(s // 2, s % 2))
        with engine.Fori(*LOOP_PAIRS) as pair:
            step(Tile(pair, 0))
            step(Tile(pair, 1))
        for s in TAIL_STEPS:
            step(Tile(s // 2, s % 2))

    def wide(ap, n=HEADS):
        return ap.unsqueeze(1).to_broadcast([P, n, ap.shape[-1]])

    def col(ap, index):
        return ap[:, index:index + 1] if isinstance(index, int) else ap[:, bass.ds(index, 1)]

    def tile_of(ap, index):
        return ap[:, index, :] if isinstance(index, int) else ap[:, bass.ds(index, 1), :].squeeze(1)

    T_BANKS = {"k": (4, 6), "q": (5, 7)}
    Y2_BANK = 4
    S_BANK = 5
    LN_BANK = 7
    WO_BANK = 4
    GATE_BANK = 4

    with nc.Block() as block:

        @block.sync
        def _(sp):
            def small_load(dst, src):
                SMALL.append(1)
                sp.dma_start(dst, src, allow_slow_non_contiguous=True).then_inc(small, 16)

            Wqkv, Wo, W1, W2 = env["Wqkv"], env["Wo"], env["W1"], env["W2"]

            def src(w, l):
                return w[l] if isinstance(l, int) else w[bass.ds(l, 1)].squeeze(0)

            def load_wkq(l):
                sp.dma_start(wkq[:, 0:INNER], src(Wqkv, l)[:, INNER:2 * INNER]).then_inc(wkq_in, 16)
                sp.dma_start(wkq[:, INNER:2 * INNER], src(Wqkv, l)[:, 0:INNER]).then_inc(wkq_in, 16)

            def load_wv(l):
                sp.dma_start(wv[:, :], src(Wqkv, l)[:, 2 * INNER:3 * INNER]).then_inc(wv_in, 16)

            def load_wo(l):
                sp.dma_start(wo[:, :, :], src(Wo, l).rearrange("(h p) d -> p h d", p=P)).then_inc(wo_in, 16)

            def load_w1(l):
                sp.dma_start(w1[:, :], src(W1, l)).then_inc(w1_in, 16)

            def load_w2(l):
                whole = HIDDEN // P
                sp.dma_start(w2[:, 0:whole, :],
                             src(W2, l)[0:whole * P, :].rearrange("(c p) d -> p c d", p=P)).then_inc(w2_in, 16)
                sp.dma_start(w2[0:HIDDEN - whole * P, whole, :],
                             src(W2, l)[whole * P:HIDDEN, :]).then_inc(w2_in, 16)

            def halo(a):
                sp.wait_ge(pv_done, (a.index - 1) * 2)
                sp.dma_start(vs[a.seq][0:WIN, :], vn[a.seq][P - WIN:P, :]).then_inc(v_halo[a.seq], 16)

            def shift(a):
                sp.wait_ge(v_out, (a.index + 1) * 2)
                sp.dma_start(vs[a.seq][WIN:P, :], vn[a.seq][0:P - WIN, :]).then_inc(v_shifted[a.seq], 16)

            def pair_of_tiles(pair):
                for seq in range(2):
                    halo(Tile(pair, seq))
                    shift(Tile(pair, seq))

            for load in (load_wkq, load_wv, load_wo, load_w1, load_w2):
                load(0)
            small_load(ropes[:, :, :], env["rope"])
            small_load(mask_in[:, :, :], env["mask"])
            small_load(first[:, :], env["first"])
            for n, name in ((0, "k_scale"), (2, "q_scale")):
                sc = env[name].rearrange("(o l) e -> o l e", o=1).to_broadcast([P, DEPTH, DH])
                small_load(scales[:, :, n, :], sc)
                small_load(scales[:, :, n + 1, 0:HALF], sc[:, :, HALF:DH])
                small_load(scales[:, :, n + 1, HALF:DH], sc[:, :, 0:HALF])
            small_load(g_all[:, :], env["ln_g"].rearrange("l d -> d l"))
            small_load(b_all[:, :], env["ln_b"].rearrange("l d -> d l"))
            for part in range(2):
                for c, (c0, m) in enumerate(CHUNKS):
                    o = part * HIDDEN + c0
                    small_load(b1_all[0:m, part, c, :], env["b1"][:, o:o + m].rearrange("l d -> d l"))
            small_load(b2_all[:, :, :], env["b2"].rearrange("(o l) d -> o l d", o=1).to_broadcast([P, DEPTH, DIM]))
            for seq in range(2):
                shift(Tile(0, seq))
            with nc.sync.Fori(1, POS - 1) as pair:
                pair_of_tiles(pair)
            with nc.sync.Fori(1, DEPTH) as l:
                pair_before, first_pair, second_pair = l * POS - 1, l * POS, l * POS + 1
                halo(Tile(pair_before, 0))
                shift(Tile(pair_before, 0))
                halo(Tile(pair_before, 1))
                sp.wait_ge(q_done, l * ROWS)
                load_wkq(l)
                shift(Tile(pair_before, 1))
                sp.wait_ge(v_done, l * (2 * ROWS))
                load_wv(l)
                pair_of_tiles(first_pair)
                sp.wait_ge(wo_done, l * ROWS)
                load_wo(l)
                halo(Tile(second_pair, 0))
                shift(Tile(second_pair, 0))
                sp.wait_ge(gate_done, l * ROWS)
                load_w1(l)
                halo(Tile(second_pair, 1))
                sp.wait_ge(y2_done, l * ROWS)
                load_w2(l)
                shift(Tile(second_pair, 1))
                with nc.sync.Fori(2, POS - 1) as n:
                    pair_of_tiles(first_pair + n)
            pair_of_tiles(TILES // 2 - 1)

        SMALL_LOADED = 16 * len(SMALL)
        INIT = 15

        @block.gpsimd
        def _(pool):
            for buf in (xs[0], xs[1], xf[0], xf[1]):
                nc.gpsimd.memset(buf[:, :], 0.0).then_inc(init, 1)
            for buf in kT:
                nc.gpsimd.memset(buf[:, :, :], 0.0).then_inc(init, 1)
            nc.gpsimd.memset(qbd[:, :, :, :, :], 0.0).then_inc(init, 1)
            nc.gpsimd.memset(pT[:, :, :, :, :], 0.0).then_inc(init, 1)
            nc.gpsimd.memset(warm[:, :], 0.0).then_inc(init, 1)
            for buf in vn + vs:
                nc.gpsimd.memset(buf[:, :], 0.0).then_inc(init, 1)
            nc.gpsimd.tensor_copy(ident16[:, :], ident[:, :]).then_inc(init, 1)
            pool.wait_ge(small, SMALL_LOADED)
            nc.gpsimd.tensor_copy(masks[:, :, :], mask_in[:, :, :]).then_inc(init, 1)

            def step(now):
                nxt, a, f = now.lag(-1), now, now.lag(3)
                if nxt.live:
                    pool.wait_ge(x_ready, nxt.index + 1)
                    wait(pool, xp_done, nxt.index)
                    nc.gpsimd.tensor_copy(xcur[:, :], tile_of(X[:, nxt.seq], nxt.pos)).then_inc(xcur_ready, 1)
                    wait(pool, q_prod, nxt.index - 1)
                    sc = scales[:, :, :, :].rearrange("p l a e -> p l (a e)")
                    nc.gpsimd.tensor_tensor(turn_tab[nxt.seq][:, :, :].rearrange("p a e -> p (a e)"),
                                            tile_of(ropes, nxt.pos), tile_of(sc, nxt.layer),
                                            ALU.mult).then_inc(rope_ready, 1)
                if a.live:
                    k, q = kq[a.seq][:, 0], kq[a.seq][:, 1]
                    pool.wait_ge(k_prod, a.index + 1)
                    nc.gpsimd.tensor_tensor(k, k, kq_sin[:, 0], ALU.add).then_inc(k_sum, 1)
                    pool.wait_ge(q_prod, a.index + 1)
                    nc.gpsimd.tensor_tensor(q, q, kq_sin[:, 1], ALU.add).then_inc(q_sum, 1)
                if f.live:
                    pool.wait_ge(ln_moments, f.index + 1)
                    nc.gpsimd.tensor_tensor(vareps[:, :], mv[:, 1:2], eps[:, 0:1], ALU.add).then_inc(eps_added, 1)
                    pool.wait_ge(eps_added, f.index + 1)
                    nc.gpsimd.tensor_tensor(rstd[:, :], vareps[:, :], minus_half[:, 0:1],
                                            ALU.pow).then_inc(rstd_ready, 1)
                if a.live:
                    pool.wait_ge(norm_ready, a.index + 1)
                    pool.wait_ge(k_sum, a.index + 1)
                    nc.gpsimd.tensor_tensor(k, k, inv[:, 0:HEADS].unsqueeze(2).to_broadcast([P, HEADS, DH]),
                                            ALU.mult).then_inc(k_hat, 1)
                    pool.wait_ge(q_sum, a.index + 1)
                    nc.gpsimd.tensor_tensor(q, q, inv[:, HEADS:2 * HEADS].unsqueeze(2).to_broadcast([P, HEADS, DH]),
                                            ALU.mult).then_inc(q_hat, 1)

            run(nc.gpsimd, step)

        @block.tensor
        def _(pe):
            pe.wait_ge(init, INIT)
            pe.wait_ge(small, SMALL_LOADED)

            def turn(dst, src):
                return nc.tensor.transpose(dst, src, ident[:, :])

            def step(now):
                nxt, a, t, w, f, g = (now.lag(n) for n in (-1, 0, 1, 2, 3, 4))
                if a.live:
                    pe.wait_ge(wkq_in, (a.layer + 1) * 32)
                    pe.wait_ge(xs_ready, a.index + 1)
                    wait(pe, v_out, a.index * 2)
                    for n, done in enumerate((k_done, q_done)):
                        if n == 1:
                            wait(pe, o_out, (a.index - 1) * 2)
                            if not w.live:
                                wait(pe, q_prod, a.index)
                        for j in (2 * n, 2 * n + 1):
                            last = nc.tensor.matmul(bank(j), xs[a.seq][:, 0:P],
                                                    wkq[:, j * BANK:(j + 1) * BANK], start=True, stop=True)
                        last.then_inc(done, 1)
                if g.live:
                    pe.wait_ge(gelu_done, g.index + 1)
                    pe.wait_ge(u_ready, g.index + 1)
                if t.live:
                    for j in range(2):
                        for n, (name, ready, done) in enumerate((("k", k_hat, tk_done), ("q", q_hat, tq_done))):
                            if j == 0:
                                pe.wait_ge(ready, t.index + 1)
                            for i in range(4):
                                h = 2 * (4 * j + i)
                                last = turn(bank(T_BANKS[name][j])[:, i * P:(i + 1) * P],
                                            kq[t.seq][:, n, h:h + 2, :].rearrange("p h e -> p (h e)"))
                            last.then_inc(done, 1)
                if g.live:
                    pe.wait_ge(w2_in, (g.layer + 1) * 32)
                    if t.live:
                        pe.wait_ge(tk_out, t.index * 2 + 1)
                    for c, (c0, m) in enumerate(CHUNKS):
                        last = nc.tensor.matmul(bank(Y2_BANK)[:, 0:DIM], u[0:m, c, :], w2[0:m, c, :],
                                                start=(c == 0), stop=(c == NCH - 1))
                    last.then_inc(y2_done, 1)
                if f.live or nxt.live:
                    if a.live:
                        pe.wait_ge(k_prod, a.index + 1)
                    elif not nxt.live:
                        pe.wait_ge(v_out, TILES * 2)
                if f.live:
                    pe.wait_ge(xmid_ready, f.index + 1)
                    turn(bank(0)[:, 0:P], xmid[f.seq][:, :]).then_inc(f1_done, 1)
                if nxt.live:
                    pe.wait_ge(xcur_ready, nxt.index + 1)
                    turn(bank(0)[:, P:2 * P], xcur[:, :]).then_inc(xp_done, 1)
                if t.live:
                    for half in range(2):
                        pe.wait_ge(tk_out, t.index * 2 + half + 1)
                        pe.wait_ge(tq_out, t.index * 2 + half + 1)
                        nc.tensor.matmul(bank(S_BANK + half), ident16[:, :], wide(tile_of(masks, t.pos), 2),
                                         start=True, stop=False, skip_group_check=True)
                        for h2 in range(4 * half, 4 * half + 4):
                            rows = 64 * (h2 % 2)
                            for win in range(WINDOWS):
                                block_at = ((h2 // 2) % 2) * WINDOWS + (win % 2) * 2 + win // 2
                                last = nc.tensor.matmul(
                                    bank(S_BANK + half)[rows:rows + 64, block_at * KEYS:(block_at + 1) * KEYS],
                                    qbd[:, h2, win].rearrange("p a i -> p (a i)"),
                                    kT[t.seq][:, h2, WIN * win:WIN * win + KEYS],
                                    start=False, stop=(win == WINDOWS - 1), skip_group_check=True,
                                    tile_position=(0, rows))
                        last.then_inc(s_done, 1)
                if f.live:
                    pe.wait_ge(xf_ready, f.index + 1)
                    turn(bank(LN_BANK)[:, 0:P], xf[f.seq][:, 0:P]).then_inc(f2_done, 1)
                if a.live:
                    pe.wait_ge(wv_in, (a.layer + 1) * 16)
                    if nxt.live:
                        pe.wait_ge(xs_ready, nxt.index + 1)
                    for half in range(2):
                        nc.tensor.matmul(bank(half), xs[a.seq][:, 0:P], wv[:, half * BANK:(half + 1) * BANK],
                                         start=True, stop=True).then_inc(v_done, 1)
                if w.live:
                    pe.wait_ge(wo_in, (w.layer + 1) * 16)
                    pe.wait_ge(o_out, w.index * 2 + 2)
                    if g.live:
                        pe.wait_ge(x_ready, g.index + ROWS + 1)
                    for h2 in range(PAIRS):
                        last = nc.tensor.matmul(bank(WO_BANK)[:, 0:DIM], oT[:, h2, :], wo[:, h2, :],
                                                start=(h2 == 0), stop=(h2 == PAIRS - 1))
                    last.then_inc(wo_done, 1)

                def probabilities(half):
                    pe.wait_ge(p_ready, t.index * 2 + half + 1)
                    for i in range(4):
                        b = 8 * half + 2 * i
                        last = turn(bank(S_BANK + half)[:, i * P:(i + 1) * P],
                                    pn[:, b:b + 2, :].rearrange("p w k -> p (w k)"))
                    last.then_inc(pt_done, 1)

                if t.live:
                    probabilities(0)
                if f.live:
                    pe.wait_ge(xn_ready, f.index + 1)
                    turn(bank(LN_BANK)[:, 0:P], xn[:, :]).then_inc(f3_done, 1)
                if t.live:
                    probabilities(1)
                if f.live:
                    pe.wait_ge(w1_in, (f.layer + 1) * 16)
                    pe.wait_ge(xnT_ready, f.index + 1)
                    for part, b, done in ((0, LN_BANK, up_done), (1, GATE_BANK, gate_done)):
                        if part == 1:
                            if w.live:
                                pe.wait_ge(xmid_ready, w.index + 1)
                            elif g.live:
                                pe.wait_ge(x_ready, g.index + ROWS + 1)
                        for c, (c0, m) in enumerate(CHUNKS):
                            last = nc.tensor.matmul(bank(b)[0:m, c * P:(c + 1) * P],
                                                    w1[:, part * HIDDEN + c0:part * HIDDEN + c0 + m], xnT[:, :],
                                                    start=True, stop=True)
                        last.then_inc(done, 1)
                if t.live:
                    if a.live:
                        pe.wait_ge(q_prod, a.index + 1)
                    else:
                        wait(pe, o_out, t.index * 2)
                    pe.wait_ge(v_out, (t.index + 1) * 2)
                    pe.wait_ge(v_shifted[t.seq], (t.pair + 1) * 16)
                    for half in range(2):
                        pe.wait_ge(pt_out, t.index * 2 + half + 1)
                        for h in range(8 * half, 8 * half + 8):
                            h2, odd = h // 2, h % 2
                            out = bank(2 + half)[64 * odd:64 * odd + 64, (h2 % 4) * P:(h2 % 4 + 1) * P]
                            out = out.rearrange("p (v w i) -> p v w i", w=2, i=WIN)
                            for parity, values in enumerate((vs[t.seq], vn[t.seq])):
                                last = nc.tensor.matmul(out[:, :, parity, :], values[:, h * DH:(h + 1) * DH],
                                                        pT[:, 2 * (h // 4) + parity, h % 4, :, :],
                                                        start=True, stop=True, skip_group_check=True,
                                                        tile_position=(0, 64 * odd))
                        last.then_inc(pv_done, 1)

            run(nc.tensor, step)

        @block.scalar
        def _(act):
            act.wait_ge(init, INIT)
            act.wait_ge(small, SMALL_LOADED)

            def shifted(xb, src, halo, ready):
                nc.scalar.activation(xb[0:64, 0:P], src[0:64, :], ACT.Copy)
                nc.scalar.activation(xb[64:P, 1:P + 1], src[64:P, :], ACT.Copy).then_inc(ready, 1)

            def step(now):
                nxt, a, t, f = (now.lag(n) for n in (-1, 0, 1, 3))
                if f.live:
                    xb = xf[f.seq]
                    wait(act, f2_done, f.index - 1)
                    nc.scalar.activation(xb[:, 0:1], xb[:, P:P + 1], ACT.Copy,
                                         scale=col(first, f.pos)).then_inc(xf_halo, 1)
                if nxt.live:
                    xb = xs[nxt.seq]
                    wait(act, v_done, (nxt.index - 1) * 2)
                    nc.scalar.activation(xb[:, 0:1], xb[:, P:P + 1], ACT.Copy,
                                         scale=col(first, nxt.pos)).then_inc(xs_halo, 1)
                if a.live:
                    wait(act, norm_ready, a.index)
                    for n, (done, out) in enumerate(((k_done, k_sq), (q_done, q_sq))):
                        act.wait_ge(done, a.index + 1)
                        nc.scalar.activation(sqr[:, n * HEADS:(n + 1) * HEADS, :].rearrange("p h e -> p (h e)"),
                                             bank(2 * n, 2), ACT.Square).then_inc(out, 1)
                if t.live:
                    act.wait_ge(k_halo, t.index + 1)
                    wait(act, s_done, t.index * 2)
                    for j in range(2):
                        act.wait_ge(tk_done, t.index * 2 + j + 1)
                        nc.scalar.activation(kT[t.seq][:, 4 * j:4 * j + 4, WIN:WIN + P],
                                             bank(T_BANKS["k"][j]).rearrange("p (h t) -> p h t", t=P),
                                             ACT.Copy).then_inc(tk_out, 1)
                        act.wait_ge(tq_done, t.index * 2 + j + 1)
                        for half in range(2):
                            rows = slice(64 * half, 64 * half + 64)
                            last = nc.scalar.activation(
                                qbd[rows, 4 * j:4 * j + 4, :, half, :],
                                bank(T_BANKS["q"][j])[rows, :].rearrange("p (h w i) -> p h w i", w=WINDOWS, i=WIN),
                                ACT.Copy)
                        last.then_inc(tq_out, 1)
                if f.live:
                    act.wait_ge(f1_done, f.index + 1)
                    if nxt.live:
                        act.wait_ge(xp_done, nxt.index + 1)
                    act.wait_ge(xf_halo, f.index + 1)
                    shifted(xf[f.seq], bank(0)[:, 0:P], xf_halo, xf_ready)
                if nxt.live:
                    act.wait_ge(xp_done, nxt.index + 1)
                    act.wait_ge(xs_halo, nxt.index + 1)
                    shifted(xs[nxt.seq], bank(0)[:, P:2 * P], xs_halo, xs_ready)
                if t.live:
                    wait(act, warmed, t.index)
                    nc.scalar.activation(warm[:, :], warm[:, :], ACT.Exp, scale=0.0).then_inc(warmed, 1)
                    for half in range(2):
                        act.wait_ge(d_ready, t.index * 2 + half + 1)
                        e = ex[:, 8 * half:8 * half + 8, :]
                        nc.scalar.activation(e, e, ACT.Exp).then_inc(exp_done, 1)
                if a.live:
                    wait(act, v_halo[a.seq], a.pair * 16)
                    for half in range(2):
                        act.wait_ge(v_done, a.index * 2 + half + 1)
                        nc.scalar.activation(vn[a.seq][:, half * BANK:(half + 1) * BANK], bank(half),
                                             ACT.Copy).then_inc(v_out, 1)

                def probabilities(half):
                    act.wait_ge(pt_done, t.index * 2 + half + 1)
                    for wi in range(2):
                        rows = slice(64 * wi, 64 * wi + 64)
                        last = nc.scalar.activation(
                            pT[rows, 4 * half:4 * half + 4, :, wi, :],
                            bank(S_BANK + half)[rows, :].rearrange("p (g h i) -> p g h i", h=4, i=WIN), ACT.Copy)
                    last.then_inc(pt_out, 1)

                if t.live:
                    wait(act, pv_done, t.index * 2)
                    probabilities(0)
                if f.live:
                    act.wait_ge(f3_done, f.index + 1)
                    wait(act, gate_done, f.index)
                    nc.scalar.activation(xnT[:, :], bank(LN_BANK)[:, 0:P], ACT.Identity,
                                         scale=col(g_all, f.layer), bias=col(b_all, f.layer)).then_inc(xnT_ready, 1)
                if t.live:
                    probabilities(1)
                if f.live:
                    act.wait_ge(gate_done, f.index + 1)
                    wait(act, u_ready, f.index)
                    for c, (c0, m) in enumerate(CHUNKS):
                        last = nc.scalar.activation(ge[0:m, c, :], bank(GATE_BANK)[0:m, c * P:(c + 1) * P], ACT.Gelu,
                                                    bias=col(b1_all[0:m, 1, c, :], f.layer))
                    last.then_inc(gelu_done, 1)
                if t.live:
                    wait(act, wo_done, t.index)
                    for half in range(2):
                        act.wait_ge(pv_done, t.index * 2 + half + 1)
                        nc.scalar.activation(oT[:, 4 * half:4 * half + 4, :].rearrange("p h t -> p (h t)"),
                                             bank(2 + half), ACT.Copy).then_inc(o_out, 1)

            run(nc.scalar, step)

        @block.vector
        def _(dve):
            dve.wait_ge(init, INIT)
            dve.wait_ge(small, SMALL_LOADED)

            NORM_LINKS = 12

            def step(now):
                a, t, w, f, g = (now.lag(n) for n in (0, 1, 2, 3, 4))
                if g.live:
                    dve.wait_ge(gelu_done, g.index + 1)
                    dve.wait_ge(up_done, g.index + 1)
                    wait(dve, y2_done, g.index)
                    for c, (c0, m) in enumerate(CHUNKS):
                        last = nc.vector.scalar_tensor_tensor(u[0:m, c, :], bank(LN_BANK)[0:m, c * P:(c + 1) * P],
                                                              col(b1_all[0:m, 0, c, :], g.layer), ge[0:m, c, :],
                                                              ALU.add, ALU.mult)
                    last.then_inc(u_ready, 1)
                    nc.vector.tensor_tensor(xm2[:, :], xmid[g.seq][:, :], tile_of(b2_all, g.layer),
                                            ALU.add).then_inc(bias_added, 1)
                if a.live:
                    wait(dve, s_done, (a.index - 1) * 2)
                    wait(dve, tk_out, (a.index - 1) * 2)
                    nc.vector.tensor_scalar(kT[a.seq][:, :, 0:WIN], kT[a.seq][:, :, P:P + WIN],
                                            col(first, a.pos), None, ALU.mult).then_inc(k_halo, 1)
                    dve.wait_ge(rope_ready, a.index + 1)
                    wait(dve, tq_done, (a.index - 1) * 2)

                def products(n, square, done):
                    dve.wait_ge(square, a.index + 1)
                    wait(dve, (k_sum, q_sum)[n], a.index)
                    src = bank(2 * n, 2).rearrange("p (h e) -> p h e", e=DH)
                    cos, sin = turn_tab[a.seq][:, 2 * n, :], turn_tab[a.seq][:, 2 * n + 1, :]
                    nc.vector.tensor_tensor(kq[a.seq][:, n], src, wide(cos), ALU.mult)
                    nc.vector.tensor_tensor(kq_sin[:, n, :, 0:HALF], src[:, :, HALF:DH], wide(sin[:, 0:HALF]), ALU.mult)
                    nc.vector.tensor_tensor(kq_sin[:, n, :, HALF:DH], src[:, :, 0:HALF], wide(sin[:, HALF:DH]),
                                            ALU.mult).then_inc(done, 1)

                if a.live:
                    products(0, k_sq, k_prod)
                if a.live:
                    products(1, q_sq, q_prod)
                if g.live:
                    dve.wait_ge(bias_added, g.index + 1)
                    dve.wait_ge(y2_done, g.index + 1)
                    nc.vector.tensor_tensor(tile_of(X[:, g.seq], g.pos), bank(Y2_BANK)[:, 0:DIM], xm2[:, :],
                                            ALU.add).then_inc(x_ready, 1)
                def blocks(half, buf):
                    return buf[:, 8 * half:8 * half + 8]

                def over_keys(half, buf):
                    return blocks(half, buf).unsqueeze(2).to_broadcast([P, 8, KEYS])

                if t.live:
                    for half in range(2):
                        dve.wait_ge(s_done, t.index * 2 + half + 1)
                        scores = bank(S_BANK + half).rearrange("p (b k) -> p b k", k=KEYS)
                        nc.vector.tensor_reduce(blocks(half, mx), scores, AX_X, ALU.max).then_inc(max_ready, 1)
                        dve.wait_ge(max_ready, t.index * 2 + half + 1)
                        nc.vector.tensor_tensor(ex[:, 8 * half:8 * half + 8, :], scores, over_keys(half, mx),
                                                ALU.subtract).then_inc(d_ready, 1)
                if f.live:
                    dve.wait_ge(f2_done, f.index + 1)
                    nc.vector.bn_stats(stats[:, :], bank(LN_BANK)[:, 0:DIM]).then_inc(ln_chain, 1)

                def probabilities(half):
                    dve.wait_ge(sum_chain, t.index * 4 + 2 * half + 1)
                    nc.vector.reciprocal(blocks(half, er), blocks(half, es)).then_inc(sum_chain, 1)
                    dve.wait_ge(sum_chain, t.index * 4 + 2 * half + 2)
                    wait(dve, pt_done, t.index * 2)
                    nc.vector.tensor_tensor(pn[:, 8 * half:8 * half + 8, :], ex[:, 8 * half:8 * half + 8, :],
                                            over_keys(half, er), ALU.mult).then_inc(p_ready, 1)

                def sums(half):
                    dve.wait_ge(exp_done, t.index * 2 + half + 1)
                    nc.vector.tensor_reduce(blocks(half, es), ex[:, 8 * half:8 * half + 8, :], AX_X,
                                            ALU.add).then_inc(sum_chain, 1)

                if t.live:
                    if f.live:
                        dve.wait_ge(ln_chain, f.index + 1)
                    sums(0)
                if f.live:
                    if not t.live:
                        dve.wait_ge(ln_chain, f.index + 1)
                    nc.vector.bn_aggr(mv[:, :], stats[:, :]).then_inc(ln_moments, 1)
                if t.live:
                    probabilities(0)
                if f.live:
                    dve.wait_ge(rstd_ready, f.index + 1)
                    wait(dve, f3_done, f.index)
                    nc.vector.tensor_scalar(xn[:, :], bank(LN_BANK)[:, 0:DIM], mv[:, 0:1], rstd[:, 0:1],
                                            ALU.subtract, ALU.mult).then_inc(xn_ready, 1)
                if t.live:
                    sums(1)
                    probabilities(1)
                if w.live:
                    dve.wait_ge(wo_done, w.index + 1)
                    wait(dve, f1_done, w.index - 1)
                    nc.vector.tensor_tensor(xmid[w.seq][:, :], bank(WO_BANK)[:, 0:DIM], tile_of(X[:, w.seq], w.pos),
                                            ALU.add).then_inc(xmid_ready, 1)

                if a.live:
                    count = [0]

                    def link(ins):
                        count[0] += 1
                        ins.then_inc(norm_chain, 1)
                        dve.wait_ge(norm_chain, a.index * NORM_LINKS + count[0])

                    wait(dve, q_hat, a.index)
                    link(nc.vector.tensor_reduce(ss[:, :], sqr[:, :, :], AX_X, ALU.add))
                    link(nc.vector.tensor_scalar(ss[:, :], ss[:, :], 1e-24, None, ALU.max))
                    link(nc.vector.tensor_scalar(seed[:, :], ss[:, :].bitcast(I32), 1, None, ALU.logical_shift_right))
                    link(nc.vector.tensor_scalar(inv[:, :].bitcast(I32), seed[:, :], -1.0, float(RSQRT_SEED),
                                                 ALU.mult, ALU.add))
                    for n in range(3):
                        link(nc.vector.tensor_tensor(tmp[:, :], inv[:, :], inv[:, :], ALU.mult))
                        link(nc.vector.scalar_tensor_tensor(tmp[:, :], tmp[:, :], -0.5, ss[:, :], ALU.mult, ALU.mult))
                        ins = nc.vector.scalar_tensor_tensor(inv[:, :], tmp[:, :], 1.5, inv[:, :], ALU.add, ALU.mult)
                        if n < 2:
                            link(ins)
                    ins.then_inc(norm_ready, 1)
                    assert count[0] == NORM_LINKS

            run(nc.vector, step)


def phase_three(nc, stack, new_sem, new_sb, env):
    X, X1, minus_half, eps = (env[k] for k in ("X", "X1", "minus_half", "eps"))

    def sem(name):
        return new_sem(name, stack)

    stats = new_sb("stats3", [P, ROWS, 6], F32, stack)
    mv = new_sb("mv3", [P, ROWS, 2], F32, stack)
    rstd = new_sb("rstd3", [P, ROWS], F32, stack)
    z = new_sb("z3", [P, ROWS, DIM], F32, stack)
    stats_in, moments, eps_added, rstd_ready = sem("p3_stats"), sem("p3_moments"), sem("p3_eps"), sem("p3_rstd")
    normed, summed, stored = sem("p3_normed"), sem("p3_summed"), sem("p3_stored")
    xf = X[:, :, :, :].rearrange("p b n d -> p (b n) d")
    x1f = X1[:, :, :, :].rearrange("p b n d -> p (b n) d")
    QUARTER = ROWS // 4

    with nc.Block() as block:

        @block.gpsimd
        def _(pool):
            pool.wait_ge(moments, 1)
            nc.gpsimd.tensor_tensor(rstd[:, :], mv[:, :, 1], eps[:, :], ALU.add).then_inc(eps_added, 1)
            pool.wait_ge(eps_added, 1)
            nc.gpsimd.tensor_tensor(rstd[:, :], rstd[:, :], minus_half[:, :], ALU.pow).then_inc(rstd_ready, 1)

        @block.vector
        def _(dve):
            for t in range(ROWS):
                last = nc.vector.bn_stats(stats[:, t, :], xf[:, t, :])
            last.then_inc(stats_in, 1)
            dve.wait_ge(stats_in, 1)
            for t in range(ROWS):
                last = nc.vector.bn_aggr(mv[:, t, :], stats[:, t, :])
            last.then_inc(moments, 1)
            dve.wait_ge(rstd_ready, 1)
            dve.wait_ge(moments, 1)
            for t in range(ROWS):
                nc.vector.tensor_scalar(z[:, t, :], xf[:, t, :], mv[:, t, 0:1], rstd[:, t:t + 1],
                                        ALU.subtract, ALU.mult).then_inc(normed, 1)
            for q in range(4):
                s = slice(q * QUARTER, (q + 1) * QUARTER)
                dve.wait_ge(normed, (q + 1) * QUARTER)
                nc.vector.tensor_tensor(z[:, s, :], z[:, s, :], x1f[:, s, :], ALU.add).then_inc(summed, 1)

        @block.sync
        def _(sp):
            dst = env["out"].rearrange("b (n t) d -> t (b n) d", t=P)
            for q in range(4):
                s = slice(q * QUARTER, (q + 1) * QUARTER)
                sp.wait_ge(summed, q + 1)
                sp.dma_start(dst[:, s, :], z[:, s, :]).then_inc(stored, 16)
            sp.wait_ge(stored, 64)


def shape_constants():
    import numpy as np
    f = np.float32
    half = np.arange(0, DH, 2, dtype=f)
    inv_freq = (f(1.0) / np.power(f(10000.0), half / f(DH))).astype(f)
    t = np.arange(LENGTH, dtype=f)
    ang = (t[:, None] * inv_freq[None, :]).astype(f)
    base = ((half + f(0.4 * DH)) / f(1.4 * DH)).astype(f)
    power = ((t - f(LENGTH // 2)) / f(WIN // 2)).astype(f)
    scale = np.power(base[None, :].astype(np.float64), power[:, None].astype(np.float64))
    cos, sin = np.cos(ang.astype(np.float64)), np.sin(ang.astype(np.float64))

    def both(lo, hi):
        return np.concatenate([lo, hi], -1)

    tabs = [both(cos / scale, cos / scale), both(-sin / scale, sin / scale),
            both(cos * scale, cos * scale) * QK_SCALE, both(-sin * scale, sin * scale) * QK_SCALE]
    rope = np.stack(tabs, 1).reshape(POS, P, 4 * DH).transpose(1, 0, 2).astype(f)
    i = np.arange(WIN)[:, None] + WIN
    j = np.arange(KEYS)[None, :]
    later = np.where((i < j) | (i > j + WIN), MASKED, 0.0)
    start = np.where(j < WIN, MASKED, later)
    rows0 = np.tile(np.concatenate([start, later, later, later], 1), (4, 1))
    rows = np.tile(np.concatenate([later] * WINDOWS, 1), (4, 1))
    mask = np.stack([rows0] + [rows] * (POS - 1), 1)
    first = np.ones((P, POS), f)
    first[:, 0] = 0
    return rope, mask.astype(f), first


def kernel(**inputs):
    import numpy as np
    import concourse.bacc as bacc
    from concourse.bass_utils import run_bass_kernel_spmd

    def gla(name):
        return np.ascontiguousarray(inputs["L0_attn_" + name])

    def ffn(name):
        return np.ascontiguousarray(inputs["L0_ffn_" + name])

    def repeated(w):
        w = w.reshape(DIM, GLA_HEADS, GLA_DH).transpose(0, 2, 1)
        return np.ascontiguousarray(np.repeat(w, GLA_DH, axis=2))

    rope, mask, first = shape_constants()
    arrays = {"x": gla("x"), "Wq_rep": repeated(gla("Wq")), "Wk_rep": repeated(gla("Wk"))}
    for name in ("Wv", "Wg", "Wgk1", "Wgk2", "bgk2", "gamma", "beta", "Wout"):
        arrays[name] = gla(name)
    for name in ("Wqkv", "q_scale", "k_scale", "Wo", "ln_g", "ln_b", "W1", "b1", "W2", "b2"):
        arrays[name] = ffn(name)
    arrays.update(rope=rope, mask=mask, first=first)
    nc = bacc.Bacc("TRN2", target_bir_lowering=False, num_devices=1)
    aps = {name: nc.dram_tensor("in_" + name, a.shape, mybir.dt.from_np(a.dtype), kind="ExternalInput").ap()
           for name, a in arrays.items()}
    out = nc.dram_tensor("out", (BATCH, LENGTH, DIM), F32, kind="ExternalOutput").ap()
    build(nc, out=out, **aps)
    r = run_bass_kernel_spmd(nc, [{"in_" + name: a for name, a in arrays.items()}], core_ids=[0])
    return r.results[0]["out"]
```

```python
from contextlib import ExitStack

import concourse.bass as bass
from concourse import mybir

F32 = mybir.dt.float32
BF16 = mybir.dt.bfloat16
F32R = mybir.dt.float32r
I32 = mybir.dt.int32
ALU = mybir.AluOpType
ACT = mybir.ActivationFunctionType
AX_X = mybir.AxisListType.X

P = 128
DIM = 128
BATCH = 2
LENGTH = 1024
POS = LENGTH // P
ROWS = BATCH * POS
GLA_HEADS = 16
GLA_DH = 8
RANK = 16
DEPTH = 6
HEADS = 16
DH = 64
PAIRS = HEADS // 2
INNER = HEADS * DH
HALF = DH // 2
WIN = 32
KEYS = 2 * WIN
HIDDEN = int(DIM * 4 * 2 / 3)
CHUNKS = [(c * P, min(P, HIDDEN - c * P)) for c in range((HIDDEN + P - 1) // P)]
NCH = len(CHUNKS)
QK_SCALE = 8.0
EPS = 1e-5
MASKED = -1e30
TILES = ROWS * DEPTH
BANK = 512
WINDOWS = P // WIN
BLOCKS = 4 * WINDOWS
RSQRT_SEED = 0x5F3759DF
SMALL_LOADED = 16 * (3 + 6 + 2 + 2 * NCH + 1)


def wait(eng, sem, value):
    if not (isinstance(value, int) and value <= 0):
        eng.wait_ge(sem, value)


class Tile:

    def __init__(self, pair, seq):
        self.pair, self.seq = pair, seq

    def lag(self, n):
        d = self.seq - n
        return Tile(self.pair + d // 2, d % 2)

    @property
    def index(self):
        return self.pair * 2 + self.seq

    @property
    def pos(self):
        return self.pair % POS

    @property
    def layer(self):
        return self.pair // POS

    @property
    def live(self):
        return not isinstance(self.pair, int) or 0 <= self.index < TILES


def at(ap, index, size=1):
    return bass.ds(index * size, size)


def build(nc, x, Wq_rep, Wk_rep, Wv, Wg, Wgk1, Wgk2, bgk2, gamma, beta, Wout,
          Wqkv, q_scale, k_scale, Wo, ln_g, ln_b, W1, b1, W2, b2, rope, mask, first, out):
    ctx = ExitStack()
    with ctx:
        def sem(name, stack=ctx):
            return stack.enter_context(nc.semaphore(name))

        def sb(name, shape, dt=F32, stack=ctx):
            return stack.enter_context(nc.sbuf_tensor(name, shape, dt))

        X = sb("X", [P, BATCH, POS, DIM])
        X1 = sb("X1", [P, BATCH, POS, DIM])
        ident = sb("ident", [P, P])
        minus_half = sb("minus_half", [P, ROWS])
        eps = sb("eps", [P, ROWS])
        PS = ctx.enter_context(nc.psum_tensor("PS", [P, 8 * BANK], F32))

        def bank(j, n=1):
            return PS[:, j * BANK:(j + n) * BANK]

        x_ready = sem("x_ready")
        const_ready = sem("const_ready")
        resident = phase_two_residents(locals(), sem, sb)
        with ExitStack() as one:
            phase_one(nc, one, sem, sb, bank, locals())
        with ExitStack() as two:
            phase_two(nc, two, sem, sb, bank, locals())
        with ExitStack() as three:
            phase_three(nc, three, sem, sb, locals())


def phase_one(nc, stack, new_sem, new_sb, bank, env):
    X, X1, ident, minus_half, eps = (env[k] for k in ("X", "X1", "ident", "minus_half", "eps"))
    x_ready, const_ready = env["x_ready"], env["const_ready"]

    def sem(name):
        return new_sem(name, stack)

    def sb(name, shape, dt=F32):
        return new_sb(name, shape, dt, stack)

    T = BATCH * LENGTH
    NB = T // BANK
    wk = sb("wk", [P, GLA_DH, P])
    wq = sb("wq", [P, GLA_DH, P])
    wv = sb("wv", [P, P])
    wg = sb("wg", [P, P])
    wgk1 = sb("wgk1", [P, RANK])
    wgk2 = sb("wgk2", [RANK, P])
    wout = sb("wout", [P, P])
    bgk = sb("bgk", [P, 1])
    gam = sb("gam", [P, 1])
    bet = sb("bet", [P, 1])
    xn = sb("xn", [P, ROWS, DIM])
    xnT = sb("xnT", [P, T])
    vT = sb("vT", [P, T])
    low = sb("low", [RANK, T])
    gate = sb("gate", [P, T])
    za = sb("za", [P, T])
    zb = sb("zb", [P, T])
    kv = sb("kv", [P, 2, LENGTH])
    st = sb("st", [P, 2, LENGTH])
    sq = sb("sqg", [P, 2, LENGTH])
    oT = sb("oT", [P, T])
    stats = sb("stats1", [P, ROWS, 6])
    mv = sb("mv1", [P, ROWS, 2])
    rstd = sb("rstd1", [P, ROWS])

    mask_in = sb("mask_in", [P, POS, WINDOWS * KEYS])
    resident = env["resident"]

    loaded = sem("p1_loaded")
    x_loaded = [sem(f"p1_x_loaded{b}") for b in range(BATCH)]
    pool_self = sem("p1_pool_self")
    moments = sem("p1_moments")
    rstd_ready = sem("p1_rstd")
    dve_self = sem("p1_dve_self")
    normed = sem("p1_normed")
    turned = sem("p1_turned")
    turned_out = sem("p1_turned_out")
    proj = sem("p1_proj")
    proj_out = sem("p1_proj_out")
    z_ready = sem("p1_z")
    act_self = sem("p1_act_self")
    soft = sem("p1_soft")
    arg_ready = sem("p1_arg")
    gate_ready = sem("p1_gate")
    krep_done = sem("p1_krep")
    krep_used = sem("p1_krep_used")
    scanned = sem("p1_scanned")
    qrep_done = sem("p1_qrep")
    read_done = sem("p1_read")
    summed = sem("p1_summed")
    gmul_done = sem("p1_gmul")
    silu_done = sem("p1_silu")
    o_used = sem("p1_o_used")
    mixed = sem("p1_mixed")
    y_done = sem("p1_y")
    y_used = sem("p1_y_used")
    x1_ready = sem("p1_x1")

    LOOPS = [(b, kk) for kk in range(GLA_DH) for b in range(BATCH)]
    x1f = X1[:, :, :, :].rearrange("p b n d -> p (b n) d")
    xf = X[:, :, :, :].rearrange("p b n d -> p (b n) d")
    with nc.Block() as block:

        @block.sync
        def _(sp):
            for b in range(BATCH):
                sp.dma_start(X1[:, b], env["x"][b].rearrange("(n t) d -> t n d", t=P)).then_inc(x_loaded[b], 16)
            for dst, src in ((wv[:, :], env["Wv"]), (wk[:, :, :], env["Wk_rep"]), (wq[:, :, :], env["Wq_rep"]),
                             (wgk1[:, :], env["Wgk1"]), (wgk2[:, :], env["Wgk2"]),
                             (bgk[:, :], env["bgk2"].rearrange("(p o) -> p o", o=1)),
                             (wg[:, :], env["Wg"]), (wout[:, :], env["Wout"]),
                             (gam[:, :], env["gamma"].rearrange("(p o) -> p o", o=1)),
                             (bet[:, :], env["beta"].rearrange("(p o) -> p o", o=1))):
                sp.dma_start(dst, src).then_inc(loaded, 16)
            resident["load_first"](sp, mask_in)

        ALL_LOADED = 16 * 10

        @block.gpsimd
        def _(pool):
            nc.gpsimd.memset(ident[:, :], 0.0).then_inc(pool_self, 1)
            nc.gpsimd.memset(minus_half[:, :], -0.5).then_inc(const_ready, 1)
            nc.gpsimd.memset(eps[:, :], EPS).then_inc(const_ready, 1)
            pool.wait_ge(pool_self, 1)
            nc.gpsimd.affine_select(out=ident[:, :], in_=ident[:, :], compare_op=ALU.not_equal, fill=1.0,
                                    base=0, pattern=[[-1, P]], channel_multiplier=1).then_inc(const_ready, 1)
            pool.wait_ge(const_ready, 3)
            steps = [1]

            def inverse_deviation(k):
                for b in range(BATCH):
                    s = slice(b * POS, (b + 1) * POS)
                    pool.wait_ge(moments, BATCH * k + b + 1)
                    nc.gpsimd.tensor_tensor(rstd[:, s], mv[:, s, 1], eps[:, s], ALU.add).then_inc(pool_self, 1)
                    steps[0] += 1
                    pool.wait_ge(pool_self, steps[0])
                    nc.gpsimd.tensor_tensor(rstd[:, s], rstd[:, s], minus_half[:, s], ALU.pow).then_inc(rstd_ready, 1)

            inverse_deviation(0)
            nc.gpsimd.tensor_copy(resident["ident16"][:, :], ident[:, :]).then_inc(const_ready, 1)
            nc.gpsimd.memset(resident["qbd"][:, :, :, :, :], 0.0).then_inc(const_ready, 1)
            nc.gpsimd.memset(resident["pT"][:, :, :, :, :], 0.0).then_inc(const_ready, 1)
            pool.wait_ge(resident["small_loaded"], SMALL_LOADED)
            nc.gpsimd.tensor_copy(resident["masks"][:, :, :], mask_in[:, :, :]).then_inc(const_ready, 1)
            for i, (b, kk) in enumerate(LOOPS):
                pool.wait_ge(read_done, i + 1)
                dst = oT[:, b * LENGTH:(b + 1) * LENGTH]
                if kk == 0:
                    nc.gpsimd.tensor_copy(dst, sq[:, i % 2, :]).then_inc(summed, 1)
                else:
                    pool.wait_ge(summed, i - 1)
                    nc.gpsimd.tensor_tensor(dst, dst, sq[:, i % 2, :], ALU.add).then_inc(summed, 1)
            for k in (1, 2, 3):
                inverse_deviation(k)

        @block.tensor
        def _(pe):
            def turn(src, tiles_ready, use, base):
                for j in range(NB):
                    for i in range(4):
                        pe.wait_ge(tiles_ready, base + 4 * j + i + 1)
                        last = nc.tensor.transpose(bank(j)[:, i * P:(i + 1) * P], src(4 * j + i), ident[:, :])
                    last.then_inc(turned, 1)

            pe.wait_ge(const_ready, 3)
            turn(lambda i: xn[:, i, :], normed, None, 0)
            pe.wait_ge(loaded, ALL_LOADED)
            for j in range(NB):
                pe.wait_ge(turned_out, j + 1)
                nc.tensor.matmul(bank(4 + j), wv[:, :], xnT[:, j * BANK:(j + 1) * BANK],
                                 start=True, stop=True).then_inc(proj, 1)
            for j in range(NB):
                nc.tensor.matmul(bank(j)[0:RANK, :], wgk1[:, :], xnT[:, j * BANK:(j + 1) * BANK],
                                 start=True, stop=True).then_inc(proj, 1)
            for j in range(NB):
                pe.wait_ge(proj_out, 5 + j)
                nc.tensor.matmul(bank(4 + j), wgk2[:, :], low[:, j * BANK:(j + 1) * BANK],
                                 start=True, stop=True).then_inc(proj, 1)
            for i, (b, kk) in enumerate(LOOPS):
                base = 4 * (i % 2)
                if i == 1:
                    pe.wait_ge(z_ready, NB)
                if i >= 2:
                    pe.wait_ge(krep_used, i - 1)
                for j in range(2):
                    last = nc.tensor.matmul(bank(base + j), wk[:, kk, :],
                                            xnT[:, b * LENGTH + j * BANK:b * LENGTH + (j + 1) * BANK],
                                            start=True, stop=True)
                last.then_inc(krep_done, 1)
                if i >= 2:
                    pe.wait_ge(read_done, i - 1)
                for j in range(2):
                    last = nc.tensor.matmul(bank(base + 2 + j), wq[:, kk, :],
                                            xnT[:, b * LENGTH + j * BANK:b * LENGTH + (j + 1) * BANK],
                                            start=True, stop=True)
                last.then_inc(qrep_done, 1)
            pe.wait_ge(read_done, len(LOOPS))
            for j in range(NB):
                nc.tensor.matmul(bank(4 + j), wg[:, :], xnT[:, j * BANK:(j + 1) * BANK],
                                 start=True, stop=True).then_inc(gmul_done, 1)
            for j in range(NB):
                if j % 2 == 0:
                    pe.wait_ge(summed, len(LOOPS) - 1 + j // 2)
                for i in range(4):
                    t = 4 * j + i
                    last = nc.tensor.transpose(bank(j)[:, i * P:(i + 1) * P], oT[:, t * P:(t + 1) * P], ident[:, :])
                last.then_inc(turned, 1)
            for j in range(NB):
                if j % 2 == 0:
                    pe.wait_ge(o_used, (j // 2 + 1) * POS)
                for i in range(4):
                    last = nc.tensor.transpose(bank(j)[:, i * P:(i + 1) * P], xn[:, 4 * j + i, :], ident[:, :])
                last.then_inc(turned, 1)
            pe.wait_ge(silu_done, NB)
            for j in range(NB):
                pe.wait_ge(mixed, j + 1)
                for i in range(4):
                    t = 4 * j + i
                    last = nc.tensor.matmul(bank(4 + j)[:, i * P:(i + 1) * P], xnT[:, t * P:(t + 1) * P],
                                            wout[:, :], start=True, stop=True)
                last.then_inc(y_done, 1)

        @block.scalar
        def _(act):
            for j in range(NB):
                act.wait_ge(turned, j + 1)
                nc.scalar.activation(xnT[:, j * BANK:(j + 1) * BANK], bank(j), ACT.Copy).then_inc(turned_out, 1)
            for j in range(NB):
                act.wait_ge(proj, j + 1)
                nc.scalar.activation(vT[:, j * BANK:(j + 1) * BANK], bank(4 + j), ACT.Copy).then_inc(proj_out, 1)
            for j in range(NB):
                act.wait_ge(proj, NB + j + 1)
                nc.scalar.activation(low[:, j * BANK:(j + 1) * BANK], bank(j)[0:RANK, :],
                                     ACT.Copy).then_inc(proj_out, 1)
            for j in range(NB):
                s = slice(j * BANK, (j + 1) * BANK)
                act.wait_ge(z_ready, j + 1)
                nc.scalar.activation(zb[:, s], za[:, s], ACT.Abs).then_inc(act_self, 1)
            for j in range(NB):
                s = slice(j * BANK, (j + 1) * BANK)
                act.wait_ge(act_self, j + 1)
                nc.scalar.activation(zb[:, s], zb[:, s], ACT.Exp, scale=-1.0).then_inc(act_self, 1)
            for j in range(NB):
                s = slice(j * BANK, (j + 1) * BANK)
                act.wait_ge(act_self, NB + j + 1)
                nc.scalar.activation(zb[:, s], zb[:, s], ACT.Ln, bias=1.0).then_inc(soft, 1)
            for j in range(NB):
                s = slice(j * BANK, (j + 1) * BANK)
                act.wait_ge(arg_ready, j + 1)
                nc.scalar.activation(gate[:, s], zb[:, s], ACT.Exp, scale=1.0 / 16.0).then_inc(gate_ready, 1)
            for j in range(NB):
                act.wait_ge(gmul_done, j + 1)
                nc.scalar.activation(za[:, j * BANK:(j + 1) * BANK], bank(4 + j), ACT.Silu).then_inc(silu_done, 1)
            for j in range(NB):
                act.wait_ge(turned, 2 * NB + j + 1)
                nc.scalar.activation(xnT[:, j * BANK:(j + 1) * BANK], bank(j), ACT.Identity,
                                     scale=gam[:, 0:1], bias=bet[:, 0:1]).then_inc(turned_out, 1)

        @block.vector
        def _(dve):
            links = [0]

            def link(ins):
                links[0] += 1
                ins.then_inc(dve_self, 1)
                dve.wait_ge(dve_self, links[0])

            def take_moments(b, src):
                for t in tiles(b):
                    last = nc.vector.bn_stats(stats[:, t, :], src(t))
                link(last)
                for t in tiles(b):
                    last = nc.vector.bn_aggr(mv[:, t, :], stats[:, t, :])
                last.then_inc(moments, 1)

            def tiles(b):
                return range(b * POS, (b + 1) * POS)

            def deviation_ready(k, b):
                dve.wait_ge(rstd_ready, BATCH * k + b + 1)

            def normalise(dst, src, t):
                return nc.vector.tensor_scalar(dst, src, mv[:, t, 0:1], rstd[:, t:t + 1], ALU.subtract, ALU.mult)

            for b in range(BATCH):
                dve.wait_ge(x_loaded[b], 16)
                take_moments(b, lambda t: x1f[:, t, :])
            for b in range(BATCH):
                deviation_ready(0, b)
                for t in tiles(b):
                    normalise(xn[:, t, :], x1f[:, t, :], t).then_inc(normed, 1)
            dve.wait_ge(loaded, ALL_LOADED)
            for j in range(NB):
                s = slice(j * BANK, (j + 1) * BANK)
                dve.wait_ge(proj, 2 * NB + j + 1)
                nc.vector.tensor_scalar(za[:, s], bank(4 + j), bgk[:, 0:1], None, ALU.add).then_inc(z_ready, 1)
            dve.wait_ge(z_ready, NB)
            for j in range(NB):
                s = slice(j * BANK, (j + 1) * BANK)
                dve.wait_ge(soft, j + 1)
                nc.vector.scalar_tensor_tensor(zb[:, s], za[:, s], 0.0, zb[:, s], ALU.min,
                                               ALU.subtract).then_inc(arg_ready, 1)
            def key_times_value(i):
                b = LOOPS[i][0]
                dve.wait_ge(krep_done, i + 1)
                nc.vector.tensor_tensor(kv[:, i % 2, :], bank(4 * (i % 2), 2), vT[:, b * LENGTH:(b + 1) * LENGTH],
                                        ALU.mult).then_inc(krep_used, 1)

            key_times_value(0)
            dve.wait_ge(gate_ready, NB)
            for i, (b, kk) in enumerate(LOOPS):
                dve.wait_ge(krep_used, i + 1)
                nc.vector.tensor_tensor_scan(st[:, i % 2, :], gate[:, b * LENGTH:(b + 1) * LENGTH], kv[:, i % 2, :],
                                             0.0, ALU.mult, ALU.add).then_inc(scanned, 1)
                if i + 1 < len(LOOPS):
                    key_times_value(i + 1)
                dve.wait_ge(scanned, i + 1)
                dve.wait_ge(qrep_done, i + 1)
                if i >= 2:
                    dve.wait_ge(summed, i - 1)
                nc.vector.tensor_tensor(sq[:, i % 2, :], bank(4 * (i % 2) + 2, 2), st[:, i % 2, :],
                                        ALU.mult).then_inc(read_done, 1)
            def o(t):
                return bank(t // 4)[:, (t % 4) * P:(t % 4 + 1) * P]

            for b in range(BATCH):
                dve.wait_ge(turned, NB + 2 * b + 2)
                take_moments(b, o)
            for b in range(BATCH):
                deviation_ready(1, b)
                for t in tiles(b):
                    normalise(xn[:, t, :], o(t), t).then_inc(o_used, 1)
            dve.wait_ge(silu_done, NB)
            for j in range(NB):
                s = slice(j * BANK, (j + 1) * BANK)
                dve.wait_ge(turned_out, NB + j + 1)
                nc.vector.tensor_tensor(xnT[:, s], xnT[:, s], za[:, s], ALU.mult).then_inc(mixed, 1)

            def y(t):
                return bank(4 + t // 4)[:, (t % 4) * P:(t % 4 + 1) * P]

            for b in range(BATCH):
                dve.wait_ge(y_done, 2 * b + 2)
                take_moments(b, y)
            for b in range(BATCH):
                deviation_ready(2, b)
                for t in tiles(b):
                    last = normalise(vT[:, t * DIM:(t + 1) * DIM], y(t), t)
                link(last)
                normalised = vT[:, b * LENGTH:(b + 1) * LENGTH].rearrange("p (t d) -> p t d", d=DIM)
                link(nc.vector.tensor_tensor(X1[:, b], X1[:, b], normalised, ALU.add))
                take_moments(b, lambda t: x1f[:, t, :])
            for b in range(BATCH):
                deviation_ready(3, b)
                for t in tiles(b):
                    normalise(xf[:, t, :], x1f[:, t, :], t).then_inc(x_ready, 1)


def phase_two_residents(env, sem, sb):
    wkq = sb("wkq", [P, 2 * INNER])
    wv = sb("w_v", [P, INNER])
    wo = sb("w_o", [P, PAIRS, DIM])
    w1 = sb("w_1", [P, 2 * HIDDEN])
    w2 = sb("w_2", [P, NCH, DIM])
    scales = sb("scales", [P, DEPTH, 4, DH])
    g_all = sb("g_all", [P, DEPTH])
    b_all = sb("b_all", [P, DEPTH])
    b1_all = sb("b1_all", [P, 2, NCH, DEPTH])
    b2_all = sb("b2_all", [P, DEPTH, DIM])
    ropes = sb("ropes", [P, POS, 4 * DH])
    masks = sb("masks", [P, POS, WINDOWS * KEYS], BF16)
    first = sb("first", [P, POS])
    ident16 = sb("ident16", [P, P], BF16)
    qbd = sb("qbd", [P, PAIRS, 4, 2, WIN])
    pT = sb("pT", [P, 8, 4, 2, WIN])
    wkq_in, wv_in, wo_in, w1_in, w2_in = (sem(n) for n in ("wkq_in", "wv_in", "wo_in", "w1_in", "w2_in"))
    small_loaded = sem("small_loaded")

    def loads(sp):
        Wqkv, Wo, W1, W2 = env["Wqkv"], env["Wo"], env["W1"], env["W2"]

        def src(w, l):
            return w[l] if isinstance(l, int) else w[bass.ds(l, 1)].squeeze(0)

        def load_wkq(l):
            sp.dma_start(wkq[:, 0:INNER], src(Wqkv, l)[:, INNER:2 * INNER]).then_inc(wkq_in, 16)
            sp.dma_start(wkq[:, INNER:2 * INNER], src(Wqkv, l)[:, 0:INNER]).then_inc(wkq_in, 16)

        def load_wv(l):
            sp.dma_start(wv[:, :], src(Wqkv, l)[:, 2 * INNER:3 * INNER]).then_inc(wv_in, 16)

        def load_wo(l):
            sp.dma_start(wo[:, :, :], src(Wo, l).rearrange("(h p) d -> p h d", p=P)).then_inc(wo_in, 16)

        def load_w1(l):
            sp.dma_start(w1[:, :], src(W1, l)).then_inc(w1_in, 16)

        def load_w2(l):
            whole = HIDDEN // P
            sp.dma_start(w2[:, 0:whole, :],
                         src(W2, l)[0:whole * P, :].rearrange("(c p) d -> p c d", p=P)).then_inc(w2_in, 16)
            sp.dma_start(w2[0:HIDDEN - whole * P, whole, :],
                         src(W2, l)[whole * P:HIDDEN, :]).then_inc(w2_in, 16)

        return load_wkq, load_wv, load_wo, load_w1, load_w2

    def load_first(sp, mask_in):
        for load in loads(sp):
            load(0)
        small = []

        def small_load(dst, src):
            small.append(1)
            sp.dma_start(dst, src, allow_slow_non_contiguous=True).then_inc(small_loaded, 16)

        small_load(ropes[:, :, :], env["rope"])
        small_load(mask_in[:, :, :], env["mask"])
        small_load(first[:, :], env["first"])
        for n, name in ((0, "k_scale"), (2, "q_scale")):
            sc = env[name].rearrange("(o l) e -> o l e", o=1).to_broadcast([P, DEPTH, DH])
            small_load(scales[:, :, n, :], sc)
            small_load(scales[:, :, n + 1, 0:HALF], sc[:, :, HALF:DH])
            small_load(scales[:, :, n + 1, HALF:DH], sc[:, :, 0:HALF])
        small_load(g_all[:, :], env["ln_g"].rearrange("l d -> d l"))
        small_load(b_all[:, :], env["ln_b"].rearrange("l d -> d l"))
        for part in range(2):
            for c, (c0, m) in enumerate(CHUNKS):
                o = part * HIDDEN + c0
                small_load(b1_all[0:m, part, c, :], env["b1"][:, o:o + m].rearrange("l d -> d l"))
        small_load(b2_all[:, :, :], env["b2"].rearrange("(o l) d -> o l d", o=1).to_broadcast([P, DEPTH, DIM]))
        assert 16 * len(small) == SMALL_LOADED

    return locals()


def phase_two(nc, stack, new_sem, new_sb, bank, env):
    X, ident, minus_half, eps = (env[k] for k in ("X", "ident", "minus_half", "eps"))
    x_ready = env["x_ready"]

    def sem(name):
        return new_sem(name, stack)

    def sb(name, shape, dt=F32):
        return new_sb(name, shape, dt, stack)

    wkq, wv, wo, w1, w2 = (env["resident"][k] for k in ("wkq", "wv", "wo", "w1", "w2"))
    scales, g_all, b_all, b1_all, b2_all = (env["resident"][k] for k in ("scales", "g_all", "b_all", "b1_all", "b2_all"))
    ropes, masks, first, ident16 = (env["resident"][k] for k in ("ropes", "masks", "first", "ident16"))
    qbd, pT = env["resident"]["qbd"], env["resident"]["pT"]
    loads, small_loaded = env["resident"]["loads"], env["resident"]["small_loaded"]
    w_hi = sb("w_hi", [P, 3 * INNER], F32R)
    w_lo = sb("w_lo", [P, 3 * INNER], F32R)
    x_hi = [sb(f"x_hi{b}", [P, P], F32R) for b in range(2)]
    x_lo = [sb(f"x_lo{b}", [P, P], F32R) for b in range(2)]
    one = sb("one", [P, 1])
    W_CHUNKS = 3 * INNER // BANK
    xcur = sb("xcur", [P, DIM])
    xs = [sb(f"xs{b}", [P, P + 1]) for b in range(2)]
    turn_tab = [sb(f"turn_tab{b}", [P, 4, DH]) for b in range(2)]
    sqr = sb("sqr", [P, 2 * HEADS, DH])
    kq = [sb(f"kq{b}", [P, 2, HEADS, DH]) for b in range(2)]
    kq_sin = sb("kq_sin", [P, 2, HEADS, DH])
    ss = sb("ss", [P, 2 * HEADS])
    seed = sb("seed", [P, 2 * HEADS], I32)
    inv = sb("inv", [P, 2 * HEADS])
    tmp = sb("tmp", [P, 2 * HEADS])
    kT = [sb(f"kT{b}", [P, PAIRS, WIN + P]) for b in range(2)]
    vn = [sb(f"vn{b}", [P, INNER]) for b in range(2)]
    vs = [sb(f"vs{b}", [P, INNER]) for b in range(2)]
    mx = sb("mx", [P, BLOCKS])
    ex = sb("ex", [P, BLOCKS, KEYS])
    es = sb("es", [P, BLOCKS])
    er = sb("er", [P, BLOCKS])
    pn = sb("pn", [P, BLOCKS, KEYS])
    warm = sb("warm", [P, 1])
    oT = sb("o_T", [P, PAIRS, P])
    xmid = [sb(f"xmid{b}", [P, DIM]) for b in range(2)]
    xf = [sb(f"xf{b}", [P, P + 1]) for b in range(2)]
    stats = sb("stats2", [P, 6])
    mv = sb("mv2", [P, 2])
    rstd = sb("rstd2", [P, 1])
    vareps = sb("vareps", [P, 1])
    xn = sb("xn2", [P, DIM])
    xnT = sb("xnT2", [P, P])
    ge = sb("ge", [P, NCH, P])
    u = sb("u", [P, NCH, P])
    xm2 = sb("xm2", [P, DIM])

    init = sem("init")
    wkq_in, wv_in, wo_in, w1_in, w2_in = (env["resident"][k + "_in"] for k in ("wkq", "wv", "wo", "w1", "w2"))
    w_rounded, w_split = sem("w_rounded"), sem("w_split")
    x_rounded, x_split = sem("x_rounded"), sem("x_split")
    xcur_ready = sem("xcur_ready")
    rope_ready = sem("rope_ready")
    xp_done = sem("xp_done")
    xs_halo = sem("xs_halo")
    xs_ready = sem("xs_ready")
    k_done, q_done, v_done = sem("k_done"), sem("q_done"), sem("v_done")
    v_out = sem("v_out")
    squared, products = sem("squared"), sem("products")
    norm_chain = sem("norm_chain")
    sq_halved = sem("sq_halved")
    norm_ready = sem("norm_ready")
    k_sum, q_sum = sem("k_sum"), sem("q_sum")
    k_hat, q_hat, q_hat_rest = sem("k_hat"), sem("q_hat"), sem("q_hat_rest")
    k_halo = sem("k_halo")
    tk_done, tq_done, tk_out, tq_out = sem("tk_done"), sem("tq_done"), sem("tk_out"), sem("tq_out")
    s_done = sem("s_done")
    max_ready = sem("max_ready")
    d_ready = sem("d_ready")
    exp_done = sem("exp_done")
    sum_chain = sem("sum_chain")
    p_ready = [sem(f"p_ready{half}") for half in range(2)]
    pt_done, pt_out = sem("pt_done"), sem("pt_out")
    v_halo = [sem(f"v_halo{b}") for b in range(2)]
    v_shifted = [sem(f"v_shifted{b}") for b in range(2)]
    pv_done, o_out = sem("pv_done"), sem("o_out")
    warmed = sem("warmed")
    wo_done = sem("wo_done")
    xmid_ready = sem("xmid_ready")
    f1_done, xf_halo, xf_ready, f2_done = sem("f1_done"), sem("xf_halo"), sem("xf_ready"), sem("f2_done")
    ln_chain = sem("ln_chain")
    ln_moments = sem("ln_moments")
    eps_added = sem("eps_added")
    rstd_ready = sem("rstd_ready")
    xn_ready = sem("xn_ready")
    f3_done = sem("f3_done")
    xnT_ready = sem("xnT_ready")
    gate_done, up_done = sem("gate_done"), sem("up_done")
    gelu_done = sem("gelu_done")
    u_ready = sem("u_ready")
    y2_done = sem("y2_done")
    bias_added = sem("bias_added")

    TAIL = 4
    HEAD_STEPS = range(-1, 6)
    LOOP_PAIRS = (3, (TILES - 2) // 2)
    TAIL_STEPS = range(2 * LOOP_PAIRS[1], TILES + TAIL)

    def run(engine, step, new_layer=None):
        def both(pair):
            step(Tile(pair, 0))
            step(Tile(pair, 1))

        if new_layer is not None:
            new_layer(0)
        for s in HEAD_STEPS:
            step(Tile(s // 2, s % 2))
        if new_layer is None:
            with engine.Fori(*LOOP_PAIRS) as pair:
                both(pair)
        else:
            with engine.Fori(LOOP_PAIRS[0], POS) as pair:
                both(pair)
            with engine.Fori(1, DEPTH - 1) as l:
                new_layer(l)
                with engine.Fori(0, POS) as n:
                    both(l * POS + n)
            new_layer(DEPTH - 1)
            with engine.Fori((DEPTH - 1) * POS, LOOP_PAIRS[1]) as pair:
                both(pair)
        for s in TAIL_STEPS:
            step(Tile(s // 2, s % 2))

    def weights(chunk):
        w, c = (wkq, chunk) if chunk < 2 * INNER // BANK else (wv, chunk - 2 * INNER // BANK)
        return w[:, c * BANK:(c + 1) * BANK]

    def wide(ap, n=HEADS):
        return ap.unsqueeze(1).to_broadcast([P, n, ap.shape[-1]])

    def col(ap, index):
        return ap[:, index:index + 1] if isinstance(index, int) else ap[:, bass.ds(index, 1)]

    def tile_of(ap, index):
        return ap[:, index, :] if isinstance(index, int) else ap[:, bass.ds(index, 1), :].squeeze(1)

    T_BANKS = {"k": (4, 6), "q": (5, 7)}
    Y2_BANK = 4
    S_BANK = 5
    LN_BANK = 7
    WO_BANK = 4
    GATE_BANK = 4

    with nc.Block() as block:

        @block.sync
        def _(sp):
            load_wkq, load_wv, load_wo, load_w1, load_w2 = loads(sp)

            def halo(a):
                sp.wait_ge(pv_done, (a.index - 1) * 2)
                sp.dma_start(vs[a.seq][0:WIN, :], vn[a.seq][P - WIN:P, :]).then_inc(v_halo[a.seq], 16)

            def shift(a):
                sp.wait_ge(v_out, (a.index + 1) * 2)
                sp.dma_start(vs[a.seq][WIN:P, :], vn[a.seq][0:P - WIN, :]).then_inc(v_shifted[a.seq], 16)

            def pair_of_tiles(pair):
                for seq in range(2):
                    halo(Tile(pair, seq))
                    shift(Tile(pair, seq))

            for seq in range(2):
                shift(Tile(0, seq))
            with nc.sync.Fori(1, POS - 1) as pair:
                pair_of_tiles(pair)
            with nc.sync.Fori(1, DEPTH) as l:
                pair_before, first_pair, second_pair = l * POS - 1, l * POS, l * POS + 1
                sp.wait_ge(w_split, l * W_CHUNKS)
                load_wkq(l)
                load_wv(l)
                pair_of_tiles(pair_before)
                pair_of_tiles(first_pair)
                sp.wait_ge(wo_done, l * ROWS)
                load_wo(l)
                halo(Tile(second_pair, 0))
                shift(Tile(second_pair, 0))
                sp.wait_ge(gate_done, l * ROWS)
                load_w1(l)
                halo(Tile(second_pair, 1))
                sp.wait_ge(y2_done, l * ROWS)
                load_w2(l)
                shift(Tile(second_pair, 1))
                with nc.sync.Fori(2, POS - 1) as n:
                    pair_of_tiles(first_pair + n)
            pair_of_tiles(TILES // 2 - 1)

        INIT = 10

        @block.gpsimd
        def _(pool):
            for buf in (xs[0], xs[1], xf[0], xf[1]):
                nc.gpsimd.memset(buf[:, P:P + 1], 0.0).then_inc(init, 1)
            for buf in kT:
                nc.gpsimd.memset(buf[:, :, P:P + WIN], 0.0).then_inc(init, 1)
            nc.gpsimd.memset(warm[:, :], 0.0).then_inc(init, 1)
            nc.gpsimd.memset(one[:, :], 1.0).then_inc(init, 1)
            for buf in vs:
                nc.gpsimd.memset(buf[0:WIN, :], 0.0).then_inc(init, 1)
            pool.wait_ge(small_loaded, SMALL_LOADED)

            def inverse_deviation(f):
                pool.wait_ge(ln_moments, f.index + 1)
                nc.gpsimd.tensor_tensor(vareps[:, :], mv[:, 1:2], eps[:, 0:1], ALU.add).then_inc(eps_added, 1)
                pool.wait_ge(eps_added, f.index + 1)
                nc.gpsimd.tensor_tensor(rstd[:, :], vareps[:, :], minus_half[:, 0:1], ALU.pow).then_inc(rstd_ready, 1)

            def step(now):
                nxt, a, t, f = (now.lag(n) for n in (-1, 0, 1, 3))
                if nxt.live:
                    pool.wait_ge(x_ready, nxt.index + 1)
                    wait(pool, xp_done, nxt.index)
                    nc.gpsimd.tensor_copy(xcur[:, :], tile_of(X[:, nxt.seq], nxt.pos)).then_inc(xcur_ready, 1)
                    wait(pool, products, (nxt.index - 1) * 4)
                    sc = scales[:, :, :, :].rearrange("p l a e -> p l (a e)")
                    nc.gpsimd.tensor_tensor(turn_tab[nxt.seq][:, :, :].rearrange("p a e -> p (a e)"),
                                            tile_of(ropes, nxt.pos), tile_of(sc, nxt.layer),
                                            ALU.mult).then_inc(rope_ready, 1)
                if a.live:
                    k, q = kq[a.seq][:, 0], kq[a.seq][:, 1]
                    pool.wait_ge(products, a.index * 4 + 2)
                    nc.gpsimd.tensor_tensor(k, k, kq_sin[:, 0], ALU.add).then_inc(k_sum, 1)
                    for n in range(2):
                        pool.wait_ge(squared, a.index * 4 + 2 * n + 2)
                        part = sqr[:, n * HEADS:(n + 1) * HEADS, :]
                        nc.gpsimd.tensor_tensor(part[:, :, 0:HALF], part[:, :, 0:HALF], part[:, :, HALF:DH],
                                                ALU.add).then_inc(sq_halved, 1)
                    if f.live:
                        inverse_deviation(f)
                if f.live and not a.live:
                    inverse_deviation(f)
                if nxt.live:
                    pool.wait_ge(xs_ready, nxt.index + 1)
                    wait(pool, v_done, (nxt.index - 1) * 2)
                    whole = xs[nxt.seq][:, 0:P]
                    nc.gpsimd.tensor_tensor(x_hi[nxt.seq][:, :], whole, one[:, :].to_broadcast([P, P]),
                                            ALU.mult).then_inc(x_rounded, 1)
                    pool.wait_ge(x_rounded, nxt.index + 1)
                    nc.gpsimd.tensor_tensor(x_lo[nxt.seq][:, :], whole, x_hi[nxt.seq][:, :].bitcast(F32),
                                            ALU.subtract).then_inc(x_split, 1)
                if t.live:
                    pool.wait_ge(sum_chain, t.index * 4 + 2)
                    wait(pool, pt_done, t.index * 2)
                    nc.gpsimd.tensor_tensor(pn[:, 0:8, :], ex[:, 0:8, :],
                                            er[:, 0:8].unsqueeze(2).to_broadcast([P, 8, KEYS]),
                                            ALU.mult).then_inc(p_ready[0], 1)
                if a.live:
                    pool.wait_ge(products, a.index * 4 + 4)
                    nc.gpsimd.tensor_tensor(q, q, kq_sin[:, 1], ALU.add).then_inc(q_sum, 1)
                if a.live:
                    pool.wait_ge(norm_ready, a.index + 1)
                    pool.wait_ge(k_sum, a.index + 1)
                    pool.wait_ge(q_sum, a.index + 1)
                    for j in range(2):
                        for n, hat in enumerate((k_hat, q_hat)):
                            if (n, j) == (1, 1):
                                continue
                            part = kq[a.seq][:, n, 8 * j:8 * j + 8]
                            by = inv[:, n * HEADS + 8 * j:n * HEADS + 8 * j + 8]
                            nc.gpsimd.tensor_tensor(part, part, by.unsqueeze(2).to_broadcast([P, 8, DH]),
                                                    ALU.mult).then_inc(hat, 1)

            run(nc.gpsimd, step)

        @block.tensor
        def _(pe):
            pe.wait_ge(init, INIT)
            pe.wait_ge(small_loaded, SMALL_LOADED)

            def project(a, b, chunk):
                columns = slice(chunk * BANK, (chunk + 1) * BANK)
                hi, lo = x_hi[a.seq][:, :], x_lo[a.seq][:, :]
                nc.tensor.matmul(bank(b), hi, w_hi[:, columns], start=True, stop=False)
                nc.tensor.matmul(bank(b), hi, w_lo[:, columns], start=False, stop=False)
                return nc.tensor.matmul(bank(b), lo, w_hi[:, columns], start=False, stop=True)

            def turn(dst, src):
                return nc.tensor.transpose(dst, src, ident[:, :])

            def step(now):
                nxt, a, t, w, f, g = (now.lag(n) for n in (-1, 0, 1, 2, 3, 4))
                if a.live:
                    pe.wait_ge(x_split, a.index + 1)
                    wait(pe, v_out, a.index * 2)
                    for j in range(4):
                        if j % 2 == 0:
                            pe.wait_ge(w_split, a.layer * W_CHUNKS + j + 2)
                        if j >= 2:
                            wait(pe, o_out, (a.index - 2) * 2 + j - 1)
                        if j == 2 and not w.live:
                            wait(pe, products, a.index * 4)
                        project(a, j, j).then_inc((k_done, q_done)[j // 2], 1)
                if g.live:
                    pe.wait_ge(gelu_done, g.index + 1)
                if t.live:
                    for j in range(2):
                        for n, (name, done) in enumerate((("k", tk_done), ("q", tq_done))):
                            if name == "k":
                                pe.wait_ge(k_hat, t.index * 2 + j + 1)
                            else:
                                pe.wait_ge((q_hat, q_hat_rest)[j], t.index + 1)
                            if (n, j) == (1, 1) and g.live:
                                pe.wait_ge(u_ready, g.index + 1)
                            for i in range(4):
                                h = 2 * (4 * j + i)
                                last = turn(bank(T_BANKS[name][j])[:, i * P:(i + 1) * P],
                                            kq[t.seq][:, n, h:h + 2, :].rearrange("p h e -> p (h e)"))
                            last.then_inc(done, 1)
                if g.live:
                    pe.wait_ge(w2_in, (g.layer + 1) * 32)
                    pe.wait_ge(u_ready, g.index + 1)
                    if t.live:
                        pe.wait_ge(tk_out, t.index * 2 + 1)
                    for c, (c0, m) in enumerate(CHUNKS):
                        last = nc.tensor.matmul(bank(Y2_BANK)[:, 0:DIM], u[0:m, c, :], w2[0:m, c, :],
                                                start=(c == 0), stop=(c == NCH - 1))
                    last.then_inc(y2_done, 1)
                if f.live or nxt.live:
                    if a.live:
                        pe.wait_ge(squared, a.index * 4 + 2)
                    elif not nxt.live:
                        pe.wait_ge(v_out, TILES * 2)
                if f.live:
                    pe.wait_ge(xmid_ready, f.index + 1)
                    turn(bank(0)[:, 0:P], xmid[f.seq][:, :]).then_inc(f1_done, 1)
                if nxt.live:
                    pe.wait_ge(xcur_ready, nxt.index + 1)
                    turn(bank(0)[:, P:2 * P], xcur[:, :]).then_inc(xp_done, 1)

                def shifted_back():
                    pe.wait_ge(xf_ready, f.index + 1)
                    if t.live:
                        pe.wait_ge(tq_out, t.index * 2 + 2)
                    turn(bank(LN_BANK)[:, 0:P], xf[f.seq][:, 0:P]).then_inc(f2_done, 1)

                if t.live:
                    for half in range(2):
                        pe.wait_ge(tq_out, t.index * 2 + half + 1)
                        nc.tensor.matmul(bank(S_BANK + half), ident16[:, :], wide(tile_of(masks, t.pos), 2),
                                         start=True, stop=False, skip_group_check=True)
                        for h2 in range(4 * half, 4 * half + 4):
                            rows = 64 * (h2 % 2)
                            for win in range(WINDOWS):
                                block_at = ((h2 // 2) % 2) * WINDOWS + (win % 2) * 2 + win // 2
                                last = nc.tensor.matmul(
                                    bank(S_BANK + half)[rows:rows + 64, block_at * KEYS:(block_at + 1) * KEYS],
                                    qbd[:, h2, win].rearrange("p a i -> p (a i)"),
                                    kT[t.seq][:, h2, WIN * win:WIN * win + KEYS],
                                    start=False, stop=(win == WINDOWS - 1), skip_group_check=True,
                                    tile_position=(0, rows))
                        last.then_inc(s_done, 1)
                        if half == 0 and f.live:
                            shifted_back()
                if f.live and not t.live:
                    shifted_back()
                if a.live:
                    pe.wait_ge(w_split, (a.layer + 1) * W_CHUNKS)
                    if nxt.live:
                        pe.wait_ge(xs_ready, nxt.index + 1)
                    pe.wait_ge(products, a.index * 4 + 2)
                    for half in range(2):
                        project(a, half, 4 + half).then_inc(v_done, 1)

                def normalised_back():
                    pe.wait_ge(xn_ready, f.index + 1)
                    turn(bank(LN_BANK)[:, 0:P], xn[:, :]).then_inc(f3_done, 1)

                if w.live:
                    pe.wait_ge(wo_in, (w.layer + 1) * 16)
                    if not a.live:
                        pe.wait_ge(o_out, w.index * 2 + 2)
                    if g.live:
                        pe.wait_ge(x_ready, g.index + ROWS + 1)
                    for h2 in range(PAIRS):
                        if h2 == PAIRS - 2 and f.live:
                            normalised_back()
                        last = nc.tensor.matmul(bank(WO_BANK)[:, 0:DIM], oT[:, h2, :], wo[:, h2, :],
                                                start=(h2 == 0), stop=(h2 == PAIRS - 1))
                    last.then_inc(wo_done, 1)

                def probabilities(half):
                    pe.wait_ge(p_ready[half], t.index + 1)
                    for i in range(4):
                        b = 8 * half + 2 * i
                        last = turn(bank(S_BANK + half)[:, i * P:(i + 1) * P],
                                    pn[:, b:b + 2, :].rearrange("p w k -> p (w k)"))
                    last.then_inc(pt_done, 1)

                def feed_forward(part, b, done):
                    for c, (c0, m) in enumerate(CHUNKS):
                        last = nc.tensor.matmul(bank(b)[0:m, c * P:(c + 1) * P],
                                                w1[:, part * HIDDEN + c0:part * HIDDEN + c0 + m], xnT[:, :],
                                                start=True, stop=True)
                    last.then_inc(done, 1)

                if f.live and not w.live:
                    normalised_back()
                if t.live:
                    probabilities(0)
                if f.live:
                    pe.wait_ge(w1_in, (f.layer + 1) * 16)
                    pe.wait_ge(xnT_ready, f.index + 1)
                    feed_forward(0, LN_BANK, up_done)
                    if w.live:
                        pe.wait_ge(xmid_ready, w.index + 1)
                    elif g.live:
                        pe.wait_ge(x_ready, g.index + ROWS + 1)
                    feed_forward(1, GATE_BANK, gate_done)
                if t.live:
                    probabilities(1)
                if t.live:
                    if not a.live:
                        wait(pe, o_out, t.index * 2)
                    pe.wait_ge(v_shifted[t.seq], (t.pair + 1) * 16)
                    for half in range(2):
                        pe.wait_ge(pt_out, t.index * 2 + half + 1)
                        for h in range(8 * half, 8 * half + 8):
                            h2, odd = h // 2, h % 2
                            out = bank(2 + half)[64 * odd:64 * odd + 64, (h2 % 4) * P:(h2 % 4 + 1) * P]
                            out = out.rearrange("p (v w i) -> p v w i", w=2, i=WIN)
                            for parity, values in enumerate((vs[t.seq], vn[t.seq])):
                                last = nc.tensor.matmul(out[:, :, parity, :], values[:, h * DH:(h + 1) * DH],
                                                        pT[:, 2 * (h // 4) + parity, h % 4, :, :],
                                                        start=True, stop=True, skip_group_check=True,
                                                        tile_position=(0, 64 * odd))
                        last.then_inc(pv_done, 1)

            run(nc.tensor, step)

        @block.scalar
        def _(act):
            act.wait_ge(init, INIT)
            act.wait_ge(small_loaded, SMALL_LOADED)

            def shifted(xb, src, ready):
                nc.scalar.activation(xb[0:64, 0:P], src[0:64, :], ACT.Copy)
                nc.scalar.activation(xb[64:P, 1:P + 1], src[64:P, :], ACT.Copy).then_inc(ready, 1)

            def step(now):
                nxt, a, t, f = (now.lag(n) for n in (-1, 0, 1, 3))
                if a.live:
                    wait(act, norm_ready, a.index)
                    for b, (before, count) in ((1, (k_done, a.index * 2 + 2)), (0, (products, a.index * 4 + 1)),
                                               (2, (q_done, a.index * 2 + 1)), (3, (q_done, a.index * 2 + 2))):
                        act.wait_ge(before, count)
                        nc.scalar.activation(sqr[:, 8 * b:8 * b + 8, :].rearrange("p h e -> p (h e)"), bank(b),
                                             ACT.Square).then_inc(squared, 1)
                if t.live:
                    act.wait_ge(k_halo, t.index + 1)
                    wait(act, s_done, t.index * 2)
                    for j in range(2):
                        act.wait_ge(tk_done, t.index * 2 + j + 1)
                        nc.scalar.activation(kT[t.seq][:, 4 * j:4 * j + 4, WIN:WIN + P],
                                             bank(T_BANKS["k"][j]).rearrange("p (h t) -> p h t", t=P),
                                             ACT.Copy).then_inc(tk_out, 1)
                        act.wait_ge(tq_done, t.index * 2 + j + 1)
                        for half in range(2):
                            rows = slice(64 * half, 64 * half + 64)
                            last = nc.scalar.activation(
                                qbd[rows, 4 * j:4 * j + 4, :, half, :],
                                bank(T_BANKS["q"][j])[rows, :].rearrange("p (h w i) -> p h w i", w=WINDOWS, i=WIN),
                                ACT.Copy)
                        last.then_inc(tq_out, 1)
                if f.live:
                    act.wait_ge(f1_done, f.index + 1)
                    if nxt.live:
                        act.wait_ge(xp_done, nxt.index + 1)
                    act.wait_ge(xf_halo, f.index + 1)
                    shifted(xf[f.seq], bank(0)[:, 0:P], xf_ready)
                if nxt.live:
                    act.wait_ge(xp_done, nxt.index + 1)
                    act.wait_ge(xs_halo, nxt.index + 1)
                    shifted(xs[nxt.seq], bank(0)[:, P:2 * P], xs_ready)
                if t.live:
                    wait(act, warmed, t.index)
                    nc.scalar.activation(warm[:, :], warm[:, :], ACT.Exp, scale=0.0).then_inc(warmed, 1)
                    for half in range(2):
                        act.wait_ge(d_ready, t.index * 2 + half + 1)
                        e = ex[:, 8 * half:8 * half + 8, :]
                        nc.scalar.activation(e, e, ACT.Exp).then_inc(exp_done, 1)
                if a.live:
                    wait(act, v_halo[a.seq], a.pair * 16)
                    for half in range(2):
                        act.wait_ge(v_done, a.index * 2 + half + 1)
                        nc.scalar.activation(vn[a.seq][:, half * BANK:(half + 1) * BANK], bank(half),
                                             ACT.Copy).then_inc(v_out, 1)

                nn, nf = now.lag(-2), now.lag(2)
                if nf.live:
                    xb = xf[nf.seq]
                    nc.scalar.activation(xb[:, 0:1], xb[:, P:P + 1], ACT.Copy,
                                         scale=col(first, nf.pos)).then_inc(xf_halo, 1)
                if nn.live:
                    xb = xs[nn.seq]
                    nc.scalar.activation(xb[:, 0:1], xb[:, P:P + 1], ACT.Copy,
                                         scale=col(first, nn.pos)).then_inc(xs_halo, 1)

                def probabilities(half):
                    act.wait_ge(pt_done, t.index * 2 + half + 1)
                    for wi in range(2):
                        rows = slice(64 * wi, 64 * wi + 64)
                        last = nc.scalar.activation(
                            pT[rows, 4 * half:4 * half + 4, :, wi, :],
                            bank(S_BANK + half)[rows, :].rearrange("p (g h i) -> p g h i", h=4, i=WIN), ACT.Copy)
                    last.then_inc(pt_out, 1)

                if f.live:
                    act.wait_ge(f3_done, f.index + 1)
                    wait(act, gate_done, f.index)
                    nc.scalar.activation(xnT[:, :], bank(LN_BANK)[:, 0:P], ACT.Identity,
                                         scale=col(g_all, f.layer), bias=col(b_all, f.layer)).then_inc(xnT_ready, 1)
                if t.live:
                    wait(act, pv_done, t.index * 2)
                    probabilities(0)
                if t.live:
                    probabilities(1)

                def outputs(half):
                    act.wait_ge(pv_done, t.index * 2 + half + 1)
                    nc.scalar.activation(oT[:, 4 * half:4 * half + 4, :].rearrange("p h t -> p (h t)"),
                                         bank(2 + half), ACT.Copy).then_inc(o_out, 1)

                if t.live:
                    wait(act, wo_done, t.index)
                    outputs(0)
                if f.live:
                    act.wait_ge(gate_done, f.index + 1)
                    wait(act, u_ready, f.index)
                    for c, (c0, m) in enumerate(CHUNKS):
                        last = nc.scalar.activation(ge[0:m, c, :], bank(GATE_BANK)[0:m, c * P:(c + 1) * P], ACT.Gelu,
                                                    bias=col(b1_all[0:m, 1, c, :], f.layer))
                    last.then_inc(gelu_done, 1)
                if t.live:
                    outputs(1)

            def round_weights(l):
                if isinstance(l, int) and l == 0:
                    nc.scalar.activation(xs[0][:, 0:1], xs[0][:, P:P + 1], ACT.Copy,
                                         scale=first[:, 0:1]).then_inc(xs_halo, 1)
                for chunk in range(W_CHUNKS):
                    if chunk == 0:
                        act.wait_ge(wkq_in, (l + 1) * 32)
                        wait(act, q_done, l * (2 * ROWS))
                    if chunk == 4:
                        act.wait_ge(wv_in, (l + 1) * 16)
                        wait(act, v_done, l * (2 * ROWS))
                    nc.scalar.activation(w_hi[:, chunk * BANK:(chunk + 1) * BANK], weights(chunk),
                                         ACT.Copy).then_inc(w_rounded, 1)

            run(nc.scalar, step, round_weights)

        @block.vector
        def _(dve):
            dve.wait_ge(init, INIT)
            dve.wait_ge(small_loaded, SMALL_LOADED)

            NORM_LINKS = 12

            def step(now):
                nxt, a, t, w, f, g = (now.lag(n) for n in (-1, 0, 1, 2, 3, 4))
                if a.live:
                    dve.wait_ge(rope_ready, a.index + 1)
                    wait(dve, tq_done, (a.index - 1) * 2)

                def turn_bank(b):
                    n, h = b // 2, 8 * (b % 2)
                    if b == 0:
                        dve.wait_ge(k_done, a.index * 2 + 1)
                    else:
                        dve.wait_ge(squared, a.index * 4 + (1, 3, 4)[b - 1])
                    if b % 2 == 0:
                        wait(dve, (k_sum, q_sum)[n], a.index)
                    src = bank(b).rearrange("p (h e) -> p h e", e=DH)
                    cos, sin = turn_tab[a.seq][:, 2 * n, :], turn_tab[a.seq][:, 2 * n + 1, :]
                    nc.vector.tensor_tensor(kq[a.seq][:, n, h:h + 8], src, wide(cos, 8), ALU.mult)
                    nc.vector.tensor_tensor(kq_sin[:, n, h:h + 8, 0:HALF], src[:, :, HALF:DH],
                                            wide(sin[:, 0:HALF], 8), ALU.mult)
                    nc.vector.tensor_tensor(kq_sin[:, n, h:h + 8, HALF:DH], src[:, :, 0:HALF],
                                            wide(sin[:, HALF:DH], 8), ALU.mult).then_inc(products, 1)

                if a.live:
                    turn_bank(0)
                if g.live:
                    dve.wait_ge(gelu_done, g.index + 1)
                    dve.wait_ge(up_done, g.index + 1)
                    wait(dve, y2_done, g.index)
                    for c, (c0, m) in enumerate(CHUNKS):
                        last = nc.vector.scalar_tensor_tensor(u[0:m, c, :], bank(LN_BANK)[0:m, c * P:(c + 1) * P],
                                                              col(b1_all[0:m, 0, c, :], g.layer), ge[0:m, c, :],
                                                              ALU.add, ALU.mult)
                    last.then_inc(u_ready, 1)
                if a.live:
                    turn_bank(1)
                    turn_bank(2)
                    turn_bank(3)
                if g.live:
                    dve.wait_ge(bias_added, g.index + 1)
                    dve.wait_ge(y2_done, g.index + 1)
                    nc.vector.tensor_tensor(tile_of(X[:, g.seq], g.pos), bank(Y2_BANK)[:, 0:DIM], xm2[:, :],
                                            ALU.add).then_inc(x_ready, 1)

                def blocks(half, buf):
                    return buf[:, 8 * half:8 * half + 8]

                def over_keys(half, buf):
                    return blocks(half, buf).unsqueeze(2).to_broadcast([P, 8, KEYS])

                def statistics():
                    dve.wait_ge(f2_done, f.index + 1)
                    nc.vector.bn_stats(stats[:, :], bank(LN_BANK)[:, 0:DIM]).then_inc(ln_chain, 1)

                if t.live:
                    for half in range(2):
                        if half == 1 and f.live:
                            dve.wait_ge(ln_chain, f.index + 1)
                        dve.wait_ge(s_done, t.index * 2 + half + 1)
                        scores = bank(S_BANK + half).rearrange("p (b k) -> p b k", k=KEYS)
                        nc.vector.tensor_reduce(blocks(half, mx), scores, AX_X, ALU.max).then_inc(max_ready, 1)
                        if half == 1 and f.live:
                            nc.vector.bn_aggr(mv[:, :], stats[:, :]).then_inc(ln_moments, 1)
                        dve.wait_ge(max_ready, t.index * 2 + half + 1)
                        if half == 0:
                            wait(dve, p_ready[0], t.index)
                        nc.vector.tensor_tensor(ex[:, 8 * half:8 * half + 8, :], scores, over_keys(half, mx),
                                                ALU.subtract).then_inc(d_ready, 1)
                        if half == 0 and f.live:
                            statistics()
                if f.live and not t.live:
                    statistics()
                    dve.wait_ge(ln_chain, f.index + 1)
                    nc.vector.bn_aggr(mv[:, :], stats[:, :]).then_inc(ln_moments, 1)

                def add_attention():
                    dve.wait_ge(wo_done, w.index + 1)
                    wait(dve, f1_done, w.index - 1)
                    nc.vector.tensor_tensor(xmid[w.seq][:, :], bank(WO_BANK)[:, 0:DIM], tile_of(X[:, w.seq], w.pos),
                                            ALU.add).then_inc(xmid_ready, 1)

                def probabilities(half):
                    dve.wait_ge(sum_chain, t.index * 4 + 2 * half + 1)
                    nc.vector.reciprocal(blocks(half, er), blocks(half, es)).then_inc(sum_chain, 1)
                    if half == 0:
                        return
                    if w.live:
                        add_attention()
                    dve.wait_ge(sum_chain, t.index * 4 + 2 * half + 2)
                    wait(dve, pt_done, t.index * 2)
                    nc.vector.tensor_tensor(pn[:, 8 * half:8 * half + 8, :], ex[:, 8 * half:8 * half + 8, :],
                                            over_keys(half, er), ALU.mult).then_inc(p_ready[1], 1)

                def sums(half):
                    dve.wait_ge(exp_done, t.index * 2 + half + 1)
                    nc.vector.tensor_reduce(blocks(half, es), ex[:, 8 * half:8 * half + 8, :], AX_X,
                                            ALU.add).then_inc(sum_chain, 1)

                if t.live:
                    sums(0)
                if f.live:
                    dve.wait_ge(rstd_ready, f.index + 1)
                    wait(dve, f3_done, f.index)
                    nc.vector.tensor_scalar(xn[:, :], bank(LN_BANK)[:, 0:DIM], mv[:, 0:1], rstd[:, 0:1],
                                            ALU.subtract, ALU.mult).then_inc(xn_ready, 1)
                if t.live:
                    probabilities(0)
                    sums(1)
                if w.live and not t.live:
                    add_attention()
                if t.live:
                    probabilities(1)

                def add_bias():
                    nc.vector.tensor_tensor(xm2[:, :], xmid[f.seq][:, :], tile_of(b2_all, f.layer),
                                            ALU.add).then_inc(bias_added, 1)

                def keep_window():
                    wait(dve, s_done, (nxt.index - 1) * 2)
                    wait(dve, tk_out, (nxt.index - 1) * 2)
                    nc.vector.tensor_scalar(kT[nxt.seq][:, :, 0:WIN], kT[nxt.seq][:, :, P:P + WIN],
                                            col(first, nxt.pos), None, ALU.mult).then_inc(k_halo, 1)

                between = ([keep_window] if nxt.live else []) + ([add_bias] if f.live else [])
                if not a.live:
                    for other in between:
                        other()
                if a.live:
                    count = [0]

                    def link(ins):
                        count[0] += 1
                        ins.then_inc(norm_chain, 1)
                        if between:
                            between.pop(0)()
                        dve.wait_ge(norm_chain, a.index * NORM_LINKS + count[0])

                    wait(dve, k_hat, a.index * 2)
                    dve.wait_ge(sq_halved, (a.index + 1) * 2)
                    link(nc.vector.tensor_reduce(ss[:, :], sqr[:, :, 0:HALF], AX_X, ALU.add))
                    link(nc.vector.tensor_scalar(ss[:, :], ss[:, :], 1e-24, None, ALU.max))
                    link(nc.vector.tensor_scalar(seed[:, :], ss[:, :].bitcast(I32), 1, None, ALU.logical_shift_right))
                    link(nc.vector.tensor_scalar(inv[:, :].bitcast(I32), seed[:, :], -1.0, float(RSQRT_SEED),
                                                 ALU.mult, ALU.add))
                    for n in range(3):
                        link(nc.vector.tensor_tensor(tmp[:, :], inv[:, :], inv[:, :], ALU.mult))
                        link(nc.vector.scalar_tensor_tensor(tmp[:, :], tmp[:, :], -0.5, ss[:, :], ALU.mult, ALU.mult))
                        ins = nc.vector.scalar_tensor_tensor(inv[:, :], tmp[:, :], 1.5, inv[:, :], ALU.add, ALU.mult)
                        if n < 2:
                            link(ins)
                    ins.then_inc(norm_ready, 1)
                    assert count[0] == NORM_LINKS
                    dve.wait_ge(q_sum, a.index + 1)
                    dve.wait_ge(norm_ready, a.index + 1)
                    part, by = kq[a.seq][:, 1, 8:HEADS], inv[:, HEADS + 8:2 * HEADS]
                    nc.vector.tensor_tensor(part, part, by.unsqueeze(2).to_broadcast([P, 8, DH]),
                                            ALU.mult).then_inc(q_hat_rest, 1)

            def rest_of_weights(l):
                wait(dve, v_done, l * (2 * ROWS))
                for chunk in range(W_CHUNKS):
                    s = slice(chunk * BANK, (chunk + 1) * BANK)
                    dve.wait_ge(w_rounded, l * W_CHUNKS + chunk + 1)
                    nc.vector.tensor_tensor(w_lo[:, s], weights(chunk), w_hi[:, s].bitcast(F32),
                                            ALU.subtract).then_inc(w_split, 1)

            run(nc.vector, step, rest_of_weights)


def phase_three(nc, stack, new_sem, new_sb, env):
    X, X1, minus_half, eps = (env[k] for k in ("X", "X1", "minus_half", "eps"))

    def sem(name):
        return new_sem(name, stack)

    stats = new_sb("stats3", [P, ROWS, 6], F32, stack)
    mv = new_sb("mv3", [P, ROWS, 2], F32, stack)
    rstd = new_sb("rstd3", [P, ROWS], F32, stack)
    z = new_sb("z3", [P, ROWS, DIM], F32, stack)
    stats_in, moments, eps_added, rstd_ready = sem("p3_stats"), sem("p3_moments"), sem("p3_eps"), sem("p3_rstd")
    normed, summed, stored = sem("p3_normed"), sem("p3_summed"), sem("p3_stored")
    xf = X[:, :, :, :].rearrange("p b n d -> p (b n) d")
    x1f = X1[:, :, :, :].rearrange("p b n d -> p (b n) d")
    QUARTER = ROWS // 4

    with nc.Block() as block:

        @block.gpsimd
        def _(pool):
            pool.wait_ge(moments, 1)
            nc.gpsimd.tensor_tensor(rstd[:, :], mv[:, :, 1], eps[:, :], ALU.add).then_inc(eps_added, 1)
            pool.wait_ge(eps_added, 1)
            nc.gpsimd.tensor_tensor(rstd[:, :], rstd[:, :], minus_half[:, :], ALU.pow).then_inc(rstd_ready, 1)

        @block.vector
        def _(dve):
            for t in range(ROWS):
                last = nc.vector.bn_stats(stats[:, t, :], xf[:, t, :])
            last.then_inc(stats_in, 1)
            dve.wait_ge(stats_in, 1)
            for t in range(ROWS):
                last = nc.vector.bn_aggr(mv[:, t, :], stats[:, t, :])
            last.then_inc(moments, 1)
            dve.wait_ge(rstd_ready, 1)
            dve.wait_ge(moments, 1)
            for t in range(ROWS):
                nc.vector.tensor_scalar(z[:, t, :], xf[:, t, :], mv[:, t, 0:1], rstd[:, t:t + 1],
                                        ALU.subtract, ALU.mult).then_inc(normed, 1)
            for q in range(4):
                s = slice(q * QUARTER, (q + 1) * QUARTER)
                dve.wait_ge(normed, (q + 1) * QUARTER)
                nc.vector.tensor_tensor(z[:, s, :], z[:, s, :], x1f[:, s, :], ALU.add).then_inc(summed, 1)

        @block.sync
        def _(sp):
            dst = env["out"].rearrange("b (n t) d -> t (b n) d", t=P)
            for q in range(4):
                s = slice(q * QUARTER, (q + 1) * QUARTER)
                sp.wait_ge(summed, q + 1)
                sp.dma_start(dst[:, s, :], z[:, s, :]).then_inc(stored, 16)
            sp.wait_ge(stored, 64)


def shape_constants():
    import numpy as np
    f = np.float32
    half = np.arange(0, DH, 2, dtype=f)
    inv_freq = (f(1.0) / np.power(f(10000.0), half / f(DH))).astype(f)
    t = np.arange(LENGTH, dtype=f)
    ang = (t[:, None] * inv_freq[None, :]).astype(f)
    base = ((half + f(0.4 * DH)) / f(1.4 * DH)).astype(f)
    power = ((t - f(LENGTH // 2)) / f(WIN // 2)).astype(f)
    scale = np.power(base[None, :].astype(np.float64), power[:, None].astype(np.float64))
    cos, sin = np.cos(ang.astype(np.float64)), np.sin(ang.astype(np.float64))

    def both(lo, hi):
        return np.concatenate([lo, hi], -1)

    tabs = [both(cos / scale, cos / scale), both(-sin / scale, sin / scale),
            both(cos * scale, cos * scale) * QK_SCALE, both(-sin * scale, sin * scale) * QK_SCALE]
    rope = np.stack(tabs, 1).reshape(POS, P, 4 * DH).transpose(1, 0, 2).astype(f)
    i = np.arange(WIN)[:, None] + WIN
    j = np.arange(KEYS)[None, :]
    later = np.where((i < j) | (i > j + WIN), MASKED, 0.0)
    start = np.where(j < WIN, MASKED, later)
    rows0 = np.tile(np.concatenate([start, later, later, later], 1), (4, 1))
    rows = np.tile(np.concatenate([later] * WINDOWS, 1), (4, 1))
    mask = np.stack([rows0] + [rows] * (POS - 1), 1)
    first = np.ones((P, POS), f)
    first[:, 0] = 0
    return rope, mask.astype(f), first


def kernel(**inputs):
    import numpy as np
    import concourse.bacc as bacc
    from concourse.bass_utils import run_bass_kernel_spmd

    def gla(name):
        return np.ascontiguousarray(inputs["L0_attn_" + name])

    def ffn(name):
        return np.ascontiguousarray(inputs["L0_ffn_" + name])

    def repeated(w):
        w = w.reshape(DIM, GLA_HEADS, GLA_DH).transpose(0, 2, 1)
        return np.ascontiguousarray(np.repeat(w, GLA_DH, axis=2))

    rope, mask, first = shape_constants()
    arrays = {"x": gla("x"), "Wq_rep": repeated(gla("Wq")), "Wk_rep": repeated(gla("Wk"))}
    for name in ("Wv", "Wg", "Wgk1", "Wgk2", "bgk2", "gamma", "beta", "Wout"):
        arrays[name] = gla(name)
    for name in ("Wqkv", "q_scale", "k_scale", "Wo", "ln_g", "ln_b", "W1", "b1", "W2", "b2"):
        arrays[name] = ffn(name)
    arrays.update(rope=rope, mask=mask, first=first)
    nc = bacc.Bacc("TRN2", target_bir_lowering=False, num_devices=1)
    aps = {name: nc.dram_tensor("in_" + name, a.shape, mybir.dt.from_np(a.dtype), kind="ExternalInput").ap()
           for name, a in arrays.items()}
    out = nc.dram_tensor("out", (BATCH, LENGTH, DIM), F32, kind="ExternalOutput").ap()
    build(nc, out=out, **aps)
    r = run_bass_kernel_spmd(nc, [{"in_" + name: a for name, a in arrays.items()}], core_ids=[0])
    return r.results[0]["out"]
```
